# Optimizing a Trainium2 kernel written in Bass

```python
import numpy as np
import jax
import jax.numpy as jnp

def _softmax(x, axis=-1):
    return jax.nn.softmax(x, axis=axis)

def _gelu(x):
    return jax.nn.gelu(x, approximate=True)

def _silu(x):
    return jax.nn.silu(x)

def _sigmoid(x):
    return jax.nn.sigmoid(x)

def _layernorm(x, axis=-1, eps=1e-05):
    m = jnp.mean(x, axis=axis, keepdims=True)
    v = jnp.var(x, axis=axis, keepdims=True)
    return (x - m) / jnp.sqrt(v + eps)

def _scatter_add(tgt, idx, src, axis=0):
    return tgt.at[idx].add(src)

def _segment_sum(src, seg, n):
    return jax.ops.segment_sum(src, seg, n)
kernel_name = 'mk_gnn_resnorm_d4_gnn_r32_ca4442'

def setup_inputs(seed: int=0):
    np.random.seed(seed)
    _w = jnp.asarray

    def _rec_inputs():
        import jax
        import jax.numpy as jnp
        _gk = jax.random.key(seed)
        x = 8.953e-05 + 1 * jax.random.normal(jax.random.fold_in(_gk, 1), (3125, 32), jnp.float32)
        _s = jax.random.randint(jax.random.fold_in(_gk, 2), (50000,), 0, 3125, jnp.int32)
        _d = jax.random.randint(jax.random.fold_in(_gk, 3), (50000,), 0, 3125, jnp.int32)
        _loop = jnp.arange(3125, dtype=jnp.int32)
        src = jnp.concatenate([_s, _d, _loop])
        dst = jnp.concatenate([_d, _s, _loop])
        _o = jnp.argsort(dst, stable=True)
        src = src[_o]
        dst = dst[_o]
        edge_attr_4 = 0.00109026 + 0.999989 * jax.random.normal(jax.random.fold_in(_gk, 12), (103125, 4), jnp.float32)
        edge_attr_8 = jax.random.uniform(jax.random.fold_in(_gk, 13), (103125, 8), jnp.float32, 0.0, 1)
        return (x, src, dst, edge_attr_4, edge_attr_8)
    x, src, dst, edge_attr_4, edge_attr_8 = _rec_inputs()

    def _L0_gnn_setup():
        import jax, jax.numpy as jnp
        import numpy as np
        N = 625
        E = 10000
        D = 32
        H1 = 8
        H2 = 1
        NEG_SLOPE = 0.2

        def gat_conv(x, src, dst, W, a_src, a_dst, b, heads, out_c, concat):
            n = x.shape[0]
            xh = (x @ W).reshape(n, heads, out_c)
            alpha_src = jnp.sum(xh * a_src, axis=-1)
            alpha_dst = jnp.sum(xh * a_dst, axis=-1)
            e = jax.nn.leaky_relu(alpha_src[src] + alpha_dst[dst], NEG_SLOPE)
            m = jax.lax.stop_gradient(jax.ops.segment_max(e, dst, num_segments=n))
            ex = jnp.exp(e - m[dst])
            denom = jax.ops.segment_sum(ex, dst, num_segments=n)
            alpha = ex / (denom[dst] + 1e-16)
            out = jax.ops.segment_sum(xh[src] * alpha[:, :, None], dst, num_segments=n)
            out = out.reshape(n, heads * out_c) if concat else out.mean(axis=1)
            return out + b
        key = jax.random.key(seed)
        ks = jax.random.split(key, 12)
        features = jax.random.normal(ks[0], (N, D), jnp.float32)
        src = jax.random.randint(ks[1], (E,), 0, N, dtype=jnp.int32)
        dst = jax.random.randint(ks[2], (E,), 0, N, dtype=jnp.int32)
        dst = jnp.where(src == dst, (dst + 1) % N, dst)
        edge_index = jnp.stack([src, dst])
        s = 0.1
        W1 = jax.random.normal(ks[3], (D, H1 * D), jnp.float32) * s
        att_src1 = jax.random.normal(ks[4], (1, H1, D), jnp.float32) * s
        att_dst1 = jax.random.normal(ks[5], (1, H1, D), jnp.float32) * s
        b1 = jnp.zeros((H1 * D,), jnp.float32)
        W2 = jax.random.normal(ks[6], (H1 * D, H2 * D), jnp.float32) * s
        att_src2 = jax.random.normal(ks[7], (1, H2, D), jnp.float32) * s
        att_dst2 = jax.random.normal(ks[8], (1, H2, D), jnp.float32) * s
        b2 = jnp.zeros((D,), jnp.float32)
        return {'features': features, 'edge_index': edge_index, 'W1': W1, 'att_src1': att_src1, 'att_dst1': att_dst1, 'b1': b1, 'W2': W2, 'att_src2': att_src2, 'att_dst2': att_dst2, 'b2': b2}
    _L0_gnn_all = _L0_gnn_setup()
    _L0_gnn_in = {k: v for k, v in _L0_gnn_all.items() if k in ('W1', 'att_src1', 'att_dst1', 'b1', 'W2', 'att_src2', 'att_dst2', 'b2')}
    del _L0_gnn_all

    def _L1_gnn_setup():
        import jax, jax.numpy as jnp
        import numpy as np
        N_NODES = 3125
        N_EDGES = 50000
        D_FEAT = 32
        K = 10
        ALPHA = 0.1
        key = jax.random.key(seed)
        k1, k2, k3 = jax.random.split(key, 3)
        feat = jax.random.normal(k1, (N_NODES, D_FEAT), dtype=jnp.float32)
        src = jax.random.randint(k2, (N_EDGES,), 0, N_NODES, dtype=jnp.int64)
        dst = jax.random.randint(k3, (N_EDGES,), 0, N_NODES, dtype=jnp.int64)
        return {'feat': feat, 'src': src, 'dst': dst}
    _L1_gnn_all = _L1_gnn_setup()
    _L1_gnn_in = {k: v for k, v in _L1_gnn_all.items() if k in ()}
    del _L1_gnn_all

    def _L2_gnn_setup():
        import jax, jax.numpy as jnp
        import numpy as np
        N_NODES = 50000
        N_EDGES = 25000
        FEAT = 32
        HEADS = 4
        key = jax.random.key(seed)
        ks = jax.random.split(key, 6)
        s = 1.0 / np.sqrt(FEAT)
        x = jax.random.normal(ks[0], (N_NODES, FEAT), dtype=jnp.float32)
        edge_index = jax.random.randint(ks[1], (2, N_EDGES), 0, N_NODES, dtype=jnp.int32)
        Wq = jax.random.normal(ks[2], (HEADS, FEAT, FEAT), dtype=jnp.float32) * s
        Wk = jax.random.normal(ks[3], (HEADS, FEAT, FEAT), dtype=jnp.float32) * s
        Wv = jax.random.normal(ks[4], (HEADS, FEAT, FEAT), dtype=jnp.float32) * s
        Wout = jax.random.normal(ks[5], (FEAT, FEAT), dtype=jnp.float32) * s
        return {'x': x, 'edge_index': edge_index, 'Wq': Wq, 'Wk': Wk, 'Wv': Wv, 'Wout': Wout}
    _L2_gnn_all = _L2_gnn_setup()
    _L2_gnn_in = {k: v for k, v in _L2_gnn_all.items() if k in ('Wq', 'Wk', 'Wv', 'Wout')}
    del _L2_gnn_all

    def _L3_gnn_setup():
        import jax, jax.numpy as jnp
        import numpy as np
        MUL = 8
        INV_SQRT3 = float(1.0 / np.sqrt(3.0))
        A_SCALAR = float(np.sqrt(1.0 / 128.0))
        A_VECTOR = float(np.sqrt(3.0 / 128.0))
        SQRT2 = float(np.sqrt(2.0))
        N_NODES, N_EDGES, NUM_BASIS, HIDDEN = (50000, 25000, 8, 256)
        WEIGHT_NUMEL = 4 * MUL * MUL
        k = jax.random.split(jax.random.key(seed), 7)
        node_features = jax.random.normal(k[0], (N_NODES, 4 * MUL), jnp.float32)
        edge_src = jax.random.randint(k[1], (N_EDGES,), 0, N_NODES)
        edge_dst = jax.random.randint(k[2], (N_EDGES,), 0, N_NODES)
        edge_sh = jax.random.normal(k[3], (N_EDGES, 4), jnp.float32)
        edge_scalars = jax.random.uniform(k[4], (N_EDGES, NUM_BASIS), jnp.float32)
        fc_w1 = jax.random.normal(k[5], (NUM_BASIS, HIDDEN), jnp.float32)
        fc_w2 = jax.random.normal(k[6], (HIDDEN, WEIGHT_NUMEL), jnp.float32)
        return dict(node_features=node_features, edge_src=edge_src, edge_dst=edge_dst, edge_sh=edge_sh, edge_scalars=edge_scalars, fc_w1=fc_w1, fc_w2=fc_w2)
    _L3_gnn_all = _L3_gnn_setup()
    _L3_gnn_in = {k: v for k, v in _L3_gnn_all.items() if k in ('fc_w1', 'fc_w2')}
    del _L3_gnn_all
    return {'x': x, 'src': src, 'dst': dst, 'edge_attr_4': edge_attr_4, 'edge_attr_8': edge_attr_8, 'L0_gnn_W1': _L0_gnn_in['W1'], 'L0_gnn_att_src1': _L0_gnn_in['att_src1'], 'L0_gnn_att_dst1': _L0_gnn_in['att_dst1'], 'L0_gnn_b1': _L0_gnn_in['b1'], 'L0_gnn_W2': _L0_gnn_in['W2'], 'L0_gnn_att_src2': _L0_gnn_in['att_src2'], 'L0_gnn_att_dst2': _L0_gnn_in['att_dst2'], 'L0_gnn_b2': _L0_gnn_in['b2'], 'L2_gnn_Wq': _L2_gnn_in['Wq'], 'L2_gnn_Wk': _L2_gnn_in['Wk'], 'L2_gnn_Wv': _L2_gnn_in['Wv'], 'L2_gnn_Wout': _L2_gnn_in['Wout'], 'L3_gnn_fc_w1': _L3_gnn_in['fc_w1'], 'L3_gnn_fc_w2': _L3_gnn_in['fc_w2']}

def reference(x, src, dst, edge_attr_4, edge_attr_8, L0_gnn_W1, L0_gnn_att_src1, L0_gnn_att_dst1, L0_gnn_b1, L0_gnn_W2, L0_gnn_att_src2, L0_gnn_att_dst2, L0_gnn_b2, L2_gnn_Wq, L2_gnn_Wk, L2_gnn_Wv, L2_gnn_Wout, L3_gnn_fc_w1, L3_gnn_fc_w2):
    import jax
    import jax.numpy as jnp

    def _L0_gnn_ref(features, edge_index, W1, att_src1, att_dst1, b1, W2, att_src2, att_dst2, b2):
        import jax, jax.numpy as jnp
        import numpy as np
        N = 625
        E = 10000
        D = 32
        H1 = 8
        H2 = 1
        NEG_SLOPE = 0.2

        def gat_conv(x, src, dst, W, a_src, a_dst, b, heads, out_c, concat):
            n = x.shape[0]
            xh = (x @ W).reshape(n, heads, out_c)
            alpha_src = jnp.sum(xh * a_src, axis=-1)
            alpha_dst = jnp.sum(xh * a_dst, axis=-1)
            e = jax.nn.leaky_relu(alpha_src[src] + alpha_dst[dst], NEG_SLOPE)
            m = jax.lax.stop_gradient(jax.ops.segment_max(e, dst, num_segments=n))
            ex = jnp.exp(e - m[dst])
            denom = jax.ops.segment_sum(ex, dst, num_segments=n)
            alpha = ex / (denom[dst] + 1e-16)
            out = jax.ops.segment_sum(xh[src] * alpha[:, :, None], dst, num_segments=n)
            out = out.reshape(n, heads * out_c) if concat else out.mean(axis=1)
            return out + b
        n = features.shape[0]
        loops = jnp.arange(n, dtype=edge_index.dtype)
        src = jnp.concatenate([edge_index[0], loops])
        dst = jnp.concatenate([edge_index[1], loops])
        x = jax.nn.relu(gat_conv(features, src, dst, W1, att_src1, att_dst1, b1, H1, D, True))
        out = gat_conv(x, src, dst, W2, att_src2, att_dst2, b2, H2, D, False)
        return out

    def _L1_gnn_ref(feat, src, dst):
        import jax, jax.numpy as jnp
        import numpy as np
        N_NODES = 3125
        N_EDGES = 50000
        D_FEAT = 32
        K = 10
        ALPHA = 0.1
        n = feat.shape[0]
        ones = jnp.ones(src.shape[0], dtype=feat.dtype)
        out_deg = jax.ops.segment_sum(ones, src, num_segments=n)
        in_deg = jax.ops.segment_sum(ones, dst, num_segments=n)
        src_norm = jnp.clip(out_deg, 1.0, None) ** (-0.5)
        dst_norm = jnp.clip(in_deg, 1.0, None) ** (-0.5)
        feat0 = feat

        def step(f, _):
            f = f * src_norm[:, None]
            agg = jax.ops.segment_sum(f[src], dst, num_segments=n)
            f = agg * dst_norm[:, None]
            f = (1.0 - ALPHA) * f + ALPHA * feat0
            return (f, None)
        feat, _ = jax.lax.scan(step, feat, None, length=K)
        return feat

    def _L2_gnn_ref(x, edge_index, Wq, Wk, Wv, Wout):
        import jax, jax.numpy as jnp
        import numpy as np
        N_NODES = 50000
        N_EDGES = 25000
        FEAT = 32
        HEADS = 4
        sender, receiver = (edge_index[0], edge_index[1])
        n, f = x.shape
        scale = f ** (-0.5)
        Q = jnp.einsum('nf,hfo->hno', x, Wq)
        K = jnp.einsum('nf,hfo->hno', x, Wk)
        V = jnp.einsum('nf,hfo->hno', x, Wv)
        s = jnp.einsum('hef,hef->eh', Q[:, receiver], K[:, sender]) * scale
        m = jax.ops.segment_max(s, receiver, num_segments=n)
        m = jnp.where(jnp.isfinite(m), m, 0.0)
        e = jnp.exp(s - m[receiver])
        denom = jax.ops.segment_sum(e, receiver, num_segments=n)
        Vs = jnp.transpose(V[:, sender], (1, 0, 2))
        num = jax.ops.segment_sum(e[..., None] * Vs, receiver, num_segments=n)
        denom_safe = jnp.where(denom > 0, denom, 1.0)
        attn = jnp.where(denom[..., None] > 0, num / denom_safe[..., None], 0.0)
        out = attn.mean(axis=1)
        return x + out @ Wout

    def _L3_gnn_ref(node_features, edge_src, edge_dst, edge_sh, edge_scalars, fc_w1, fc_w2):
        import jax, jax.numpy as jnp
        import numpy as np
        MUL = 8
        INV_SQRT3 = float(1.0 / np.sqrt(3.0))
        A_SCALAR = float(np.sqrt(1.0 / 128.0))
        A_VECTOR = float(np.sqrt(3.0 / 128.0))
        SQRT2 = float(np.sqrt(2.0))
        N_NODES, N_EDGES, NUM_BASIS, HIDDEN = (50000, 25000, 8, 256)
        WEIGHT_NUMEL = 4 * MUL * MUL
        N = node_features.shape[0]
        E = edge_src.shape[0]
        h = jax.nn.relu(edge_scalars @ (fc_w1 * (1.0 / np.sqrt(NUM_BASIS)))) * SQRT2
        w = (h @ (fc_w2 * (1.0 / np.sqrt(HIDDEN)))).reshape(E, 4, MUL, MUL)
        x = node_features[edge_src]
        s1 = x[:, :MUL]
        v1 = x[:, MUL:].reshape(E, MUL, 3)
        s2 = edge_sh[:, 0]
        v2 = edge_sh[:, 1:4]
        out_s = A_SCALAR * (jnp.einsum('eu,euw->ew', s1 * s2[:, None], w[:, 0]) + INV_SQRT3 * jnp.einsum('eui,ei,euw->ew', v1, v2, w[:, 1]))
        out_v = A_VECTOR * INV_SQRT3 * (jnp.einsum('eu,euw,ei->ewi', s1, w[:, 2], v2) + jnp.einsum('eui,euw->ewi', v1 * s2[:, None, None], w[:, 3]))
        edge_features = jnp.concatenate([out_s, out_v.reshape(E, 3 * MUL)], axis=1)
        node_out = jax.ops.segment_sum(edge_features, edge_dst, num_segments=N)
        return node_out * (1.0 / np.sqrt(E / N))
    edge_index = jnp.stack([src, dst])
    x = _layernorm(x + _L0_gnn_ref(x, edge_index, L0_gnn_W1, L0_gnn_att_src1, L0_gnn_att_dst1, L0_gnn_b1, L0_gnn_W2, L0_gnn_att_src2, L0_gnn_att_dst2, L0_gnn_b2), axis=-1)
    x = _layernorm(x + _L1_gnn_ref(x, src, dst), axis=-1)
    x = _layernorm(x + _L2_gnn_ref(x, edge_index, L2_gnn_Wq, L2_gnn_Wk, L2_gnn_Wv, L2_gnn_Wout), axis=-1)
    x = _layernorm(x + _L3_gnn_ref(x, src, dst, edge_attr_4, edge_attr_8, L3_gnn_fc_w1, L3_gnn_fc_w2), axis=-1)
    return x

_drawn_inputs = setup_inputs


def setup_inputs(seed=0):
    import zlib

    import numpy as np

    out = dict(_drawn_inputs(seed))
    spreads = {'L0_gnn_b1': (0.0, 0.1), 'L0_gnn_b2': (0.0, 0.1)}
    factors = {'L0_gnn_att_dst1': 64.0, 'L0_gnn_att_src2': 49.379, 'L0_gnn_att_dst2': 64.0}
    for name, (base, spread) in spreads.items():
        noise = np.random.default_rng([zlib.crc32(name.encode()), seed]).standard_normal(out[name].shape)
        drawn = base * np.exp(spread * noise) if base else spread * noise
        out[name] = jnp.asarray(drawn.astype(out[name].dtype))
    for name, factor in factors.items():
        out[name] = (out[name] * factor).astype(out[name].dtype)
    return out
```

```python
import numpy as np
from contextlib import ExitStack

import concourse.bass as bass
import concourse.mybir as mybir

F32, I32, BF16 = mybir.dt.float32, mybir.dt.int32, mybir.dt.bfloat16
ALU = mybir.AluOpType
ACT = mybir.ActivationFunctionType
AX = mybir.AxisListType.X

N, E, D = 3125, 103125, 32
P = 125
W = N // P
J = E // P
U = 5
G = E // (P * U)
X = W - 1
NG = G + X
SLOTS = 3
TRIPS = NG // SLOTS
NGP = NG + SLOTS
H1, H2, HQ = 8, 1, 4
K1 = D + 1
BIG = 1e30
EPS_LN = 1e-5
STEPS_APPNP = 10
ALPHA = 0.1
MUL, BASIS, HID = 8, 8, 256


class Steps:

    def __init__(self, eng, sem, base=0, n=0):
        self.eng, self.sem, self.base, self.n = eng, sem, base, n

    def did(self, ins):
        ins.then_inc(self.sem, 1)
        self.n += 1

    def link(self, ins):
        self.did(ins)
        self.eng.wait_ge(self.sem, self.base + self.n)


def gate(eng, gate_sem):
    eng.sem_inc(gate_sem, 1)


def bcast(ap, axis, n):
    shape = list(ap.shape)
    return ap.unsqueeze(axis).broadcast_to(shape[:axis] + [n] + shape[axis:])


class Kept:
    pass


class Stage:

    def __init__(self, nc, name):
        self.nc, self.name, self.ctx, self.sems = nc, name, ExitStack(), []

    def __enter__(self):
        self.ctx.__enter__()
        return self

    def __exit__(self, *a):
        left = self.ctx.__exit__(*a)
        if self.sems:
            self.nc.clear_and_free_semaphores(self.sems)
            self.nc.all_engine_barrier()
        return left

    def sb(self, name, shape, dt=F32):
        return self.ctx.enter_context(self.nc.sbuf_tensor(f"{self.name}_{name}", shape, dt))

    def ps(self, name, shape, dt=F32):
        return self.ctx.enter_context(self.nc.psum_tensor(f"{self.name}_{name}", shape, dt))

    def sem(self, name):
        self.sems.append(self.nc.alloc_semaphore(f"{self.name}_{name}"))
        return self.sems[-1]

    def block(self):
        return self.ctx.enter_context(self.nc.Block())


def edge_rows(dram, c):
    return dram.rearrange("(g p u) c -> g p (u c)", p=P, u=U)


def nodes_view(dram):
    return dram.rearrange("(w d) c -> d w c", d=P)


def stage_index(nc, k, src, dst, ea4, ea8):
    GB = G - 128
    with Stage(nc, "ix") as st:
        zeros = st.sb("zeros", [P, 3300])
        d_a, d_b, d_x = st.sb("d_a", [128, P * U], I32), st.sb("d_b", [GB, P * U], I32), st.sb("d_x", [X, P * U], I32)
        s_a, s_b, s_x = st.sb("s_a", [128, P * U], I32), st.sb("s_b", [GB, P * U], I32), st.sb("s_x", [X, P * U], I32)
        df = [st.sb(f"df{n}", [r, P * U]) for n, r in enumerate((128, GB, X))]
        sf = [st.sb(f"sf{n}", [r, P * U]) for n, r in enumerate((128, GB, X))]
        edges = st.sb("edges", [128, X])
        edge_col = st.sb("edge_col", [X, 1])
        win_x = st.sb("win_x", [X, 1], I32)
        ge = [st.sb(f"ge{n}", [128, X]) for n in range(2)]
        lt = [st.sb(f"lt{n}", [128, X]) for n in range(2)]
        wf = [st.sb(f"wf{n}", [128, 1]) for n in range(2)]
        w125 = [st.sb(f"w125{n}", [128, 1]) for n in range(2)]
        wi = [st.sb(f"wi{n}", [128, 1], I32) for n in range(2)]
        ones = st.sb("ones", [128, 1])
        kf, pen = st.sb("kf", [X, 1]), st.sb("pen", [X, 1])
        big8, big4 = st.sb("big8", [X, P * U * 8]), st.sb("big4", [X, P * U * 4])
        grid = [st.sb("gd", [P, J]), st.sb("gs", [P, J])]
        gi = [st.sb("gdi", [P, J], I32), st.sb("gsi", [P, J], I32)]
        hi = [st.sb("hd", [P, J]), st.sb("hs", [P, J])]
        lo = [st.sb("ld", [P, J]), st.sb("ls", [P, J])]
        prev = st.sb("prev", [P, 1], I32)
        prevf = st.sb("prevf", [P, 1])
        diag = st.sb("diag", [P, P])
        low_hot = st.sb("low_hot", [P, 2, U, P], BF16)
        high_hot = st.sb("high_hot", [P, 2, U, W], BF16)
        zb = st.sb("zb", [P, P], BF16)
        tri = st.sb("tri", [P, P])
        tot, before, endf, startf, none = (st.sb(n, [P, W]) for n in ("tot", "before", "endf", "startf", "none"))
        pt = [st.ps(f"pt{u}", [128, 512]) for u in range(U)]
        p_cnt, p_last, p_deg = st.ps("p_cnt", [128, 512]), st.ps("p_last", [128, 512]), st.ps("p_deg", [128, 512])
        z0, zed, loaded, cst, steps, pe_s, gone, ext_i, ext_at, wrote, wback, hot, degs, counted, fx, ptr = (
            st.sem(n) for n in ("z0", "zed", "loaded", "cst", "steps", "pe_s", "gone", "ext_i", "ext_at", "wrote",
                                "wback", "hot", "degs", "counted", "fx", "ptr"))
        pool_s, attr, gt = st.sem("pool_s"), st.sem("attr"), st.sem("gt")
        block = st.block()
        to_zero = [(k.start16, 16), (k.start2, 2), (k.start32, 32), (k.start4, 4)]

        @block.sync
        def _(sp):
            sp.dma_start(d_a[:, :], dst[0:128 * P * U].rearrange("(g e) -> g e", e=P * U)).then_inc(loaded, 16)
            sp.dma_start(d_b[:, :], dst[128 * P * U:E].rearrange("(g e) -> g e", e=P * U)).then_inc(loaded, 16)
            sp.dma_start(s_a[:, :], src[0:128 * P * U].rearrange("(g e) -> g e", e=P * U)).then_inc(loaded, 16)
            sp.dma_start(s_b[:, :], src[128 * P * U:E].rearrange("(g e) -> g e", e=P * U)).then_inc(loaded, 16)
            sp.dma_start(gi[0][:, :], dst.rearrange("(p j) -> p j", j=J)).then_inc(loaded, 16)
            sp.dma_start(gi[1][:, :], src.rearrange("(p j) -> p j", j=J)).then_inc(loaded, 16)
            sp.wait_ge(cst, 1)
            sp.dma_start(prev[1:P, 0:1], dst.rearrange("(p j) -> p j", j=J)[0:P - 1, J - 1:J],
                         allow_slow_non_contiguous=True).then_inc(loaded, 16)
            sp.dma_start(k.ea8x[0:E, :], ea8).then_inc(attr, 16)
            sp.dma_start(k.ea4x[0:E, :], ea4).then_inc(attr, 16)
            sp.wait_ge(z0, 1)
            n_zero = 0
            for dram, c in to_zero:
                view = dram.rearrange("(p j) c -> p (j c)", j=J)
                for at in range(0, J * c, 3300):
                    m = min(3300, J * c - at)
                    sp.dma_start(view[:, at:at + m], zeros[:, 0:m]).then_inc(zed, 16)
                    n_zero += 1
            xz = k.xdst[E:NG * P * U, :].rearrange("(p j) c -> p (j c)", p=P)
            for at in range(0, X * U * D, 1920):
                sp.dma_start(xz[:, at:at + 1920], zeros[:, 0:1920]).then_inc(zed, 16)
                n_zero += 1
            sp.wait_ge(fx, 1)
            sp.dma_start(k.wind[0:128, :], wi[0][:, :]).then_inc(wrote, 16)
            sp.dma_start(k.wind[128:G, :], wi[1][0:GB, :]).then_inc(wrote, 16)
            sp.dma_start(k.wind[G:NG, :], win_x[:, :]).then_inc(wrote, 16)
            sp.wait_ge(wrote, 48)
            sp.dma_start(k.wrow[:, :], k.wind.rearrange("g o -> o g")).then_inc(wback, 16)
            sp.wait_ge(ext_at, 32)
            sp.dma_start(edge_rows(k.ea8x, 8)[G:NG].rearrange("g p c -> g (p c)"), big8[:, :]).then_inc(attr, 16)
            sp.dma_start(edge_rows(k.ea4x, 4)[G:NG].rearrange("g p c -> g (p c)"), big4[:, :]).then_inc(attr, 16)
            sp.wait_ge(attr, 64)
            sp.wait_ge(wback, 16)
            sp.wait_ge(zed, 16 * n_zero)

        @block.gpsimd
        def _(pool):
            s = Steps(pool, pool_s)
            pool.memset(prev[:, :], -1).then_inc(cst, 1)
            pool.memset(zeros[:, :], 0.0).then_inc(z0, 1)
            s.did(pool.memset(k.ident[:, :], 0.0))
            s.did(pool.memset(tri[:, :], 1.0))
            s.did(pool.memset(k.earlier[:, :], 0.0))
            s.link(pool.memset(zb[:, :], 0.0))
            pool.affine_select(out=k.ident[:, :], in_=k.ident[:, :], compare_op=ALU.not_equal, fill=1.0, base=0,
                               pattern=[[-1, 128]], channel_multiplier=1)
            pool.affine_select(out=tri[:, :], in_=tri[:, :], compare_op=ALU.is_ge, fill=0.0, base=0,
                               pattern=[[1, P]], channel_multiplier=-1)
            pool.affine_select(out=k.earlier[:, :], in_=k.earlier[:, :], compare_op=ALU.is_gt, fill=-BIG, base=0,
                               pattern=[[-1, P]], channel_multiplier=1)
            pool.memset(ones[:, :], 1.0)
            pool.memset(k.ones[:, :], 1.0)
            pool.memset(k.srcidx[:, :], 0)
            pool.memset(k.dloc[:, :], 0.0)
            pool.memset(k.negs[:, :], -BIG)
            pool.iota(edges[:, :], [[P, X]], base=P, channel_multiplier=0, allow_small_or_imprecise_dtypes=True)
            pool.iota(edge_col[:, :], [[0, 1]], base=P, channel_multiplier=P, allow_small_or_imprecise_dtypes=True)
            pool.iota(win_x[:, :], [[0, 1]], base=1, channel_multiplier=1)
            pool.iota(k.lane[:, :], [[1, P]], base=0, channel_multiplier=0,
                      allow_small_or_imprecise_dtypes=True).then_inc(cst, 1)
            pool.wait_ge(fx, 1)
            by = bass.IndirectOffsetOnAxis(ap=k.kx[:, :], axis=0)
            pool.indirect_dma_start(out=d_x[:, :], out_offset=None, in_=dst.rearrange("(g e) -> g e", e=P * U),
                                    in_offset=by).then_inc(ext_i, 16)
            pool.indirect_dma_start(out=s_x[:, :], out_offset=None, in_=src.rearrange("(g e) -> g e", e=P * U),
                                    in_offset=by).then_inc(ext_i, 16)
            pool.indirect_dma_start(out=big8[:, :], out_offset=None,
                                    in_=ea8.rearrange("(g e) c -> g (e c)", e=P * U), in_offset=by).then_inc(ext_at, 16)
            pool.indirect_dma_start(out=big4[:, :], out_offset=None,
                                    in_=ea4.rearrange("(g e) c -> g (e c)", e=P * U), in_offset=by).then_inc(ext_at, 16)

        @block.scalar
        def _(act):
            pass

        @block.vector
        def _(dve):
            s = Steps(dve, steps)
            dve.wait_ge(loaded, 16 * 7)
            dve.wait_ge(cst, 2)
            for o, i in ((df[0], d_a), (df[1], d_b), (sf[0], s_a), (sf[1], s_b), (grid[0], gi[0]), (grid[1], gi[1]),
                         (prevf, prev), (k.first_i, gi[0])):
                s.did(dve.tensor_copy(o[:, :], i[:, 0:o.shape[1]]))
            dve.wait_ge(steps, s.n)
            for n, r in ((0, 128), (1, GB)):
                s.link(dve.tensor_scalar(ge[n][0:r, :], edges[0:r, :], df[n][:, 0:1], None, ALU.is_le))
                s.did(dve.tensor_scalar(lt[n][0:r, :], ge[n][0:r, :], -1.0, 1.0, ALU.mult, ALU.add))
                s.link(dve.tensor_reduce(wf[n][0:r, :], ge[n][0:r, :], AX, ALU.add))
                s.did(dve.tensor_copy(wi[n][0:r, :], wf[n][0:r, :]))
                s.link(dve.tensor_scalar(w125[n][0:r, :], wf[n][0:r, :], float(P), None, ALU.mult))
                last = dve.tensor_scalar(df[n][:, :], df[n][:, :], w125[n][0:r, :], None, ALU.subtract)
                if n == 0:
                    s.did(last)
            last.then_inc(gone, 1)
            dve.wait_ge(pe_s, 1)
            s.link(dve.tensor_scalar(kf[:, :], p_cnt[0:X, 0:1], -1.0, 0.0, ALU.add, ALU.max))
            s.did(dve.tensor_scalar(pen[:, :], p_cnt[0:X, 0:1], 0.5, 8192.0, ALU.is_lt, ALU.mult))
            dve.tensor_copy(k.kx[:, :], kf[:, :]).then_inc(fx, 1)
            s.link(dve.tensor_scalar(k.nstart[:, 0:1], grid[0][:, 0:1], prevf[:, 0:1], None, ALU.is_equal))
            s.link(dve.tensor_tensor(k.nstart[:, 1:J], grid[0][:, 1:J], grid[0][:, 0:J - 1], ALU.is_equal))
            s.did(dve.tensor_scalar(k.newseg[:, :], k.nstart[:, :], BIG, -BIG, ALU.mult, ALU.add))
            s.link(dve.tensor_scalar(k.notfirst[:, :], grid[0][:, :], grid[0][:, 0:1], None, ALU.is_equal))
            s.link(dve.tensor_scalar(k.notfirst[:, :], k.notfirst[:, :], BIG, -BIG, ALU.mult, ALU.add))
            dve.tensor_scalar(diag[:, :], k.ident[0:P, 0:P], grid[0][:, J - 1:J], None, ALU.mult).then_inc(gone, 1)
            dve.wait_ge(pe_s, 2)
            s.link(dve.tensor_scalar(diag[:, :], p_last[0:P, 0:P], grid[0][:, 0:1], None, ALU.is_equal))
            s.link(dve.tensor_scalar(diag[:, :], diag[:, :], BIG, -BIG, ALU.mult, ALU.add))
            s.link(dve.tensor_tensor(k.earlier[:, :], k.earlier[:, :], diag[:, :], ALU.min))
            dve.wait_ge(ext_i, 32)
            s.did(dve.tensor_copy(df[2][:, :], d_x[:, :]))
            s.link(dve.tensor_copy(sf[2][:, :], s_x[:, :]))
            dve.tensor_scalar(df[2][:, :], df[2][:, :], edge_col[:, 0:1], pen[:, 0:1],
                              ALU.subtract, ALU.add).then_inc(gone, 1)
            dve.wait_ge(pe_s, 3)
            dl = k.dloc[:, :].rearrange("p (g u) -> p g u", u=U)
            si = k.srcidx[:, :].rearrange("p (g u) -> p g u", u=U)
            for u in range(U):
                s.did(dve.tensor_copy(dl[:, 0:NG, u], pt[u][0:P, 0:NG]))
                s.did(dve.tensor_copy(si[:, 0:NG, u], pt[u][0:P, 256:256 + NG]))
            for a in range(2):
                s.link(dve.memset(hi[a][:, :], 0.0))
                for t in range(1, W):
                    s.link(dve.scalar_tensor_tensor(hi[a][:, :], grid[a][:, :], float(P * t), hi[a][:, :],
                                                    ALU.is_ge, ALU.add))
                s.link(dve.scalar_tensor_tensor(lo[a][:, :], hi[a][:, :], float(-P), grid[a][:, :],
                                                ALU.mult, ALU.add))
            lanes = bcast(k.lane[:, :], 1, U)

            def one_hot(i, first=False):
                for a in range(2):
                    if not first:
                        dve.wait_ge(counted, 2 * i + a - 1)
                    dve.tensor_tensor(low_hot[:, a], lanes, bcast(lo[a][:, bass.ds(i * U, U)], 2, P), ALU.is_equal)
                    dve.tensor_tensor(high_hot[:, a], bcast(k.lane[:, 0:W], 1, U),
                                      bcast(hi[a][:, bass.ds(i * U, U)], 2, W), ALU.is_equal).then_inc(hot, 1)

            one_hot(0, True)
            with dve.Fori(1, G) as i:
                one_hot(i)
            dve.wait_ge(counted, 2 * G)
            s = Steps(dve, degs)
            s.did(dve.tensor_copy(k.indeg[:, :], p_deg[0:P, 0:W]))
            s.link(dve.tensor_copy(k.outdeg[:, :], p_deg[0:P, 64:64 + W]))
            dve.wait_ge(pe_s, 5)
            s.link(dve.tensor_copy(tot[:, :], p_cnt[0:P, 64:64 + W]))
            s.link(dve.tensor_tensor_scan(before[:, :], k.ones[:, 0:W], tot[:, :], 0.0, ALU.mult, ALU.add))
            s.link(dve.tensor_tensor(before[:, :], before[:, :], tot[:, :], ALU.subtract))
            s.link(dve.tensor_tensor(endf[:, :], p_last[0:P, 256:256 + W], before[:, :], ALU.add))
            s.link(dve.tensor_tensor(startf[:, :], endf[:, :], k.indeg[:, :], ALU.subtract))
            s.link(dve.tensor_scalar(endf[:, :], endf[:, :], -1.0, None, ALU.add))
            s.link(dve.tensor_scalar(none[:, :], k.indeg[:, :], 0.5, None, ALU.is_lt))
            for v, o in ((endf, k.end), (startf, k.start)):
                s.link(dve.tensor_scalar(before[:, :], v[:, :], -1.0, float(E), ALU.mult, ALU.add))
                s.link(dve.tensor_tensor(before[:, :], before[:, :], none[:, :], ALU.mult))
                s.link(dve.tensor_tensor(v[:, :], v[:, :], before[:, :], ALU.add))
                s.link(dve.tensor_copy(o[:, :], v[:, :]))

        @block.tensor
        def _(pe):
            pe.wait_ge(cst, 2)
            pe.wait_ge(gone, 1)
            nc.tensor.matmul(p_cnt[0:X, 0:1], lt[0][:, :], ones[:, :], start=True, stop=False)
            nc.tensor.matmul(p_cnt[0:X, 0:1], lt[1][0:GB, :], ones[0:GB, :], start=False, stop=True).then_inc(pe_s, 1)
            pe.wait_ge(gone, 2)
            nc.tensor.matmul(p_last[0:P, 0:P], k.ones[:, :], diag[:, :], start=True, stop=True).then_inc(pe_s, 1)
            pe.wait_ge(gone, 3)
            for u in range(U):
                for c, f in ((0, df), (256, sf)):
                    at = c
                    for b in range(3):
                        r = f[b].shape[0]
                        last = nc.tensor.transpose(pt[u][0:P, at:at + r],
                                                   f[b][:, :].rearrange("g (p u) -> g p u", u=U)[:, :, u],
                                                   k.ident[0:r, 0:r])
                        at += r
            last.then_inc(pe_s, 1)
            for a in range(2):
                nc.tensor.matmul(p_deg[0:P, 64 * a:64 * a + W], zb[:, :], zb[:, 0:W], start=True, stop=False,
                                 skip_group_check=True)
            with pe.Fori(0, G) as i:
                for a in range(2):
                    pe.wait_ge(hot, 2 * i + a + 1)
                    for u in range(U):
                        last = nc.tensor.matmul(p_deg[0:P, 64 * a:64 * a + W], low_hot[:, a, u, :], high_hot[:, a, u, :],
                                                start=False, stop=False, skip_group_check=True)
                    last.then_inc(counted, 1)
            pe.wait_ge(degs, 2)
            nc.tensor.matmul(p_cnt[0:P, 64:64 + W], k.ones[:, :], k.indeg[:, :], start=True, stop=True).then_inc(pe_s, 1)
            nc.tensor.matmul(p_last[0:P, 256:256 + W], tri[:, :], k.indeg[:, :], start=True, stop=True).then_inc(pe_s, 1)


def load(sp, sem, *pairs):
    for o, i in pairs:
        sp.dma_start(o, i, allow_slow_non_contiguous=True).then_inc(sem, 16)
    return 16 * len(pairs)


def stage_windows(nc, k, name, src, parts, size, rhs, out, mid=None, bias=None):
    m = out.shape[2]
    with Stage(nc, name) as st:
        x_w = st.sb("x_w", [P, parts * size])
        x_t = st.sb("x_t", [size, parts, P])
        y_t = st.sb("y_t", [size, parts, P])
        p_t = [st.ps(f"p_t{c}", [128, 512]) for c in range(parts)]
        p_m = [st.ps(f"p_m{c}", [128, 512]) for c in range(parts)]
        p_o = st.ps("p_o", [128, 512])
        picked, turned, copied, mixed, bent, summed, kept = (
            st.sem(n) for n in ("picked", "turned", "copied", "mixed", "bent", "summed", "kept"))
        block = st.block()
        last = y_t if mid else x_t

        @block.tensor
        def _(pe):
            def window(w, first):
                pe.wait_ge(picked, w + 1)
                for c in range(parts):
                    ins = nc.tensor.transpose(p_t[c][0:size, 0:P], x_w[:, size * c:size * (c + 1)], k.ident[0:P, 0:P])
                ins.then_inc(turned, 1)
                pe.wait_ge(copied, w + 1)
                if mid:
                    for c in range(parts):
                        ins = nc.tensor.matmul(p_m[c][0:size, 0:P], mid[:, c, :], x_t[:, c, :], start=True, stop=True)
                    ins.then_inc(mixed, 1)
                    pe.wait_ge(bent, w + 1)
                if not first:
                    pe.wait_ge(kept, w)
                for c in range(parts):
                    ins = nc.tensor.matmul(p_o[0:P, 0:m], last[:, c, :], rhs[:, c, :], start=c == 0, stop=c == parts - 1)
                ins.then_inc(summed, 1)

            window(0, True)
            with pe.Fori(1, W) as w:
                window(w, False)

        @block.scalar
        def _(act):
            with act.Fori(0, W) as w:
                act.wait_ge(turned, w + 1)
                for c in range(parts):
                    ins = nc.scalar.copy(x_t[:, c, :], p_t[c][0:size, 0:P])
                ins.then_inc(copied, 1)
                if mid:
                    act.wait_ge(mixed, w + 1)
                    for c in range(parts):
                        ins = nc.scalar.activation(y_t[:, c, :], p_m[c][0:size, 0:P], ACT.Relu, bias=bias[:, c:c + 1])
                    ins.then_inc(bent, 1)

        @block.vector
        def _(dve):
            def pick(w):
                dve.tensor_copy(x_w[:, :], src[:, bass.ds(w, 1), :].rearrange("p o f -> p (o f)")).then_inc(picked, 1)

            def keep(w):
                dve.wait_ge(summed, w + 1)
                dve.tensor_copy(out[:, bass.ds(w, 1), :].rearrange("p o f -> p (o f)"), p_o[0:P, 0:m]).then_inc(kept, 1)

            pick(0)
            with dve.Fori(0, W - 1) as w:
                dve.wait_ge(turned, w + 1)
                pick(w + 1)
                keep(w)
            keep(W - 1)


def stage_gat_weights(nc, k, t):
    with Stage(nc, "gw") as st:
        w1 = st.sb("w1", [D, H1 * D])
        a1 = st.sb("a1", [D, 2, H1 * D])
        prod = st.sb("prod", [D, 2, H1 * D])
        a2 = st.sb("a2", [128, 2, D])
        prod2 = st.sb("prod2", [128, 2, 2, D])
        got, z, steps = st.sem("got"), st.sem("z"), st.sem("steps")
        block = st.block()

        @block.gpsimd
        def _(pool):
            pool.memset(k.mix1[:, :, :], 0.0).then_inc(z, 1)

        @block.sync
        def _(sp):
            load(sp, got, (w1[:, :], t["L0_gnn_W1"]),
                 (a1[:, 0, :], t["L0_gnn_att_src1"].rearrange("o h c -> o (h c)").broadcast_to([D, H1 * D])),
                 (a1[:, 1, :], t["L0_gnn_att_dst1"].rearrange("o h c -> o (h c)").broadcast_to([D, H1 * D])),
                 (a2[:, 0, :], t["L0_gnn_att_src2"].rearrange("o h c -> o (h c)").broadcast_to([128, D])),
                 (a2[:, 1, :], t["L0_gnn_att_dst2"].rearrange("o h c -> o (h c)").broadcast_to([128, D])),
                 (k.b1[:, :], t["L0_gnn_b1"].rearrange("(c p) -> p c", p=128)),
                 (k.b2[:, :], t["L0_gnn_b2"].unsqueeze(0).broadcast_to([P, D])))
            for c in range(2):
                sp.dma_start(k.w2[:, c, 0:D], t["L0_gnn_W2"][128 * c:128 * (c + 1), :]).then_inc(got, 16)
            sp.wait_ge(z, 1)
            for h in range(H1):
                c, at = h // 4, D * (h % 4)
                sp.dma_start(k.mix1[at:at + D, c, at:at + D], t["L0_gnn_W1"][:, D * h:D * (h + 1)]).then_inc(got, 16)
            sp.wait_ge(got, 16 * 17)

        @block.vector
        def _(dve):
            s = Steps(dve, steps)
            dve.wait_ge(got, 16 * 17)
            s.link(dve.tensor_tensor(prod[:, :, :], bcast(w1[:, :], 1, 2), a1[:, :, :], ALU.mult))
            s.did(dve.tensor_reduce(k.att1[:, 0, :], prod[:, :, :].rearrange("p a (h c) -> p (a h) c", c=D), AX, ALU.add))
            for c in range(2):
                s.link(dve.tensor_tensor(prod2[:, c, :, :], bcast(k.w2[:, c, 0:D], 1, 2), a2[:, :, :], ALU.mult))
                s.did(dve.tensor_reduce(k.w2[:, c, D:D + 2], prod2[:, c, :, :], AX, ALU.add))


def stage_table(nc, k, name, table, cols):
    width = table.shape[1]
    with Stage(nc, name) as st:
        tab = st.sb("tab", [P, W, width])
        made, wrote = st.sem("made"), st.sem("wrote")
        block = st.block()

        @block.vector
        def _(dve):
            at = 0
            for c in cols:
                if c is None:
                    dve.memset(tab[:, :, at:at + 1], 1.0).then_inc(made, 1)
                    at += 1
                else:
                    dve.tensor_copy(tab[:, :, at:at + c.shape[2]], c).then_inc(made, 1)
                    at += c.shape[2]

        @block.sync
        def _(sp):
            sp.wait_ge(made, len(cols))
            sp.dma_start(nodes_view(table), tab[:, :, :]).then_inc(wrote, 16)
            sp.wait_ge(wrote, 16)


def stage_gather(nc, k, name, table, gx, scores=None, n_scores=0, products=False):
    width = table.shape[1]
    c = n_scores
    with Stage(nc, name) as st:
        idx = [st.sb(f"idx{r}", [P, U], I32) for r in range(SLOTS)]
        row = [st.sb(f"row{r}", [P, U * width]) for r in range(SLOTS)]
        fx = [st.sb(f"fx{r}", [P, U * K1]) for r in range(SLOTS)]
        sc = [st.sb(f"sc{r}", [P, U * c]) for r in range(SLOTS)] if c else None
        if products:
            xd = [st.sb(f"xd{r}", [P, U * D]) for r in range(SLOTS)]
            prod = [st.sb(f"prod{r}", [P, U * c * D]) for r in range(SLOTS)]
        named, packed, scored, multiplied, gt = (st.sem(n) for n in ("named", "packed", "scored", "multiplied", "gt"))
        fetched = [st.sem(f"fetched{r}") for r in range(SLOTS)]
        wrote = [st.sem(f"wrote{r}") for r in range(SLOTS)]
        at_dst = [st.sem(f"at_dst{r}") for r in range(SLOTS)]
        block = st.block()
        outs = 2 if c else 1

        def rows(r, a, b):
            return row[r][:, :].rearrange("p (u c) -> p u c", c=width)[:, :, a:b]

        @block.scalar
        def _(act):
            def name_edges(g, r):
                nc.scalar.copy(idx[r][:, :], k.srcidx[:, bass.ds(g * U, U)]).then_inc(named, 1)

            def trip(i, first):
                for r in range(SLOTS):
                    act.wait_ge(fetched[r], 16 * U * i + 16 * U)
                    if not first:
                        act.wait_ge(wrote[r], 16 * outs * i)
                    if c and not products:
                        nc.scalar.copy(sc[r][:, :].rearrange("p (u c) -> p u c", c=c), rows(r, K1, K1 + c))
                    nc.scalar.copy(fx[r][:, :].rearrange("p (u c) -> p u c", c=K1), rows(r, 0, K1)).then_inc(packed, 1)
                    act.wait_ge(packed, i * SLOTS + r + 1)
                    if products:
                        act.wait_ge(multiplied, i * SLOTS + r + 1)
                    name_edges(i * SLOTS + r + SLOTS, r)

            for r in range(SLOTS):
                name_edges(r, r)
            trip(0, True)
            with act.Fori(1, TRIPS) as i:
                trip(i, False)

        @block.gpsimd
        def _(pool):
            with pool.Fori(0, TRIPS) as i:
                for r in range(SLOTS):
                    pool.wait_ge(named, i * SLOTS + r + 1)
                    gate(pool, gt)
                    for u in range(U):
                        pool.indirect_dma_start(
                            out=row[r][:, u * width:(u + 1) * width], out_offset=None, in_=table,
                            in_offset=bass.IndirectOffsetOnAxis(ap=idx[r][:, u:u + 1], axis=0)).then_inc(fetched[r], 16)

        @block.sync
        def _(sp):
            def trip(i, first):
                if products:
                    for r in range(SLOTS):
                        if not first:
                            sp.wait_ge(multiplied, i * SLOTS + r + 1 - SLOTS)
                        sp.dma_start(xd[r][:, :], edge_rows(k.xdst, D)[bass.ds(i * SLOTS + r, 1)]
                                     .rearrange("o p c -> (o p) c")).then_inc(at_dst[r], 16)
                for r in range(SLOTS):
                    sp.wait_ge(packed, i * SLOTS + r + 1)
                    sp.dma_start(edge_rows(gx, K1)[bass.ds(i * SLOTS + r, 1)].rearrange("o p c -> (o p) c"),
                                 fx[r][:, :]).then_inc(wrote[r], 16)
                    if c:
                        if products:
                            sp.wait_ge(scored, i * SLOTS + r + 1)
                        sp.dma_start(edge_rows(scores, c)[bass.ds(i * SLOTS + r, 1)].rearrange("o p c -> (o p) c"),
                                     sc[r][:, :]).then_inc(wrote[r], 16)

            trip(0, True)
            with sp.Fori(1, TRIPS) as i:
                trip(i, False)
            for r in range(SLOTS):
                sp.wait_ge(wrote[r], 16 * outs * TRIPS)

        if products:
            @block.vector
            def _(dve):
                def trip(i, first):
                    for r in range(SLOTS):
                        dve.wait_ge(fetched[r], 16 * U * i + 16 * U)
                        dve.wait_ge(at_dst[r], 16 * i + 16)
                        p4 = prod[r][:, :].rearrange("p (u h f) -> p u h f", h=c, f=D)
                        dve.tensor_tensor(p4, rows(r, K1, K1 + c * D).rearrange("p u (h f) -> p u h f", f=D),
                                          bcast(xd[r][:, :].rearrange("p (u f) -> p u f", f=D), 2, c),
                                          ALU.mult).then_inc(multiplied, 1)
                        dve.wait_ge(multiplied, i * SLOTS + r + 1)
                        if not first:
                            dve.wait_ge(wrote[r], 16 * outs * i)
                        dve.tensor_reduce(sc[r][:, :], prod[r][:, :].rearrange("p (n f) -> p n f", f=D),
                                          AX, ALU.add).then_inc(scored, 1)

                trip(0, True)
                with dve.Fori(1, TRIPS) as i:
                    trip(i, False)


def stage_segmax(nc, k, name, scores, c, scanned, amax):
    with Stage(nc, name) as st:
        v = st.sb("v", [P, J, c])
        diag, room = st.sb("diag", [P, 2, P]), st.sb("room", [P, 2, P])
        carry = st.sb("carry", [P, c])
        p_b = [st.ps(f"p_b{n}", [128, 512]) for n in range(2)]
        got, steps, diags, spread, dumped, fetched = (
            st.sem(n) for n in ("got", "steps", "diags", "spread", "dumped", "fetched"))
        done = st.sem("done")
        block = st.block()

        @block.sync
        def _(sp):
            sp.dma_start(v[:, :, :], scores[0:E, :].rearrange("(p j) c -> p j c", j=J)).then_inc(got, 16)
            sp.wait_ge(done, 1)
            sp.dma_start(scanned[0:E, :].rearrange("(p j) c -> p j c", j=J), v[:, :, :]).then_inc(dumped, 16)
            sp.dma_start(scanned[E:E + 1, :], k.negs[0:1, 0:c]).then_inc(dumped, 16)
            sp.wait_ge(dumped, 32)

        @block.vector
        def _(dve):
            s = Steps(dve, steps)
            dve.wait_ge(got, 16)
            for h in range(c):
                s.did(dve.tensor_tensor_scan(v[:, :, h], k.newseg[:, :], v[:, :, h], -BIG, ALU.add, ALU.max))
            dve.wait_ge(steps, s.n)
            for h in range(c):
                if h >= 2:
                    dve.wait_ge(spread, h - 1)
                dve.tensor_scalar(diag[:, h % 2, :], k.ident[0:P, 0:P], v[:, J - 1, h:h + 1], None,
                                  ALU.mult).then_inc(diags, 1)
                dve.wait_ge(spread, h + 1)
                s.link(dve.tensor_tensor(room[:, h % 2, :], p_b[h % 2][0:P, 0:P], k.earlier[:, :], ALU.add))
                s.did(dve.tensor_reduce(carry[:, h:h + 1], room[:, h % 2, :], AX, ALU.max))
            dve.wait_ge(steps, s.n)
            for h in range(c):
                ins = dve.scalar_tensor_tensor(v[:, :, h], k.notfirst[:, :], carry[:, h:h + 1], v[:, :, h],
                                               ALU.add, ALU.max)
            ins.then_inc(done, 1)

        @block.tensor
        def _(pe):
            for h in range(c):
                pe.wait_ge(diags, h + 1)
                nc.tensor.matmul(p_b[h % 2][0:P, 0:P], k.ones[:, :], diag[:, h % 2, :], start=True,
                                 stop=True).then_inc(spread, 1)

        @block.gpsimd
        def _(pool):
            pool.wait_ge(dumped, 32)
            for w in range(W):
                pool.indirect_dma_start(out=amax[:, w, :], out_offset=None, in_=scanned,
                                        in_offset=bass.IndirectOffsetOnAxis(ap=k.end[:, w:w + 1], axis=0)
                                        ).then_inc(fetched, 16)
            pool.wait_ge(fetched, 16 * W)


def stage_spread(nc, k, name, tab, table, start, xdst=None, scores=None, heads=0, weights=None):
    c = tab.shape[2]
    with Stage(nc, name) as st:
        v = st.sb("v", [P, J, c])
        head = st.sb("head", [P, c])
        if scores is not None:
            z = st.sb("z", [P, J, heads])
            big = st.sb("big", [X, P * U * heads])
        wrote, placed, first, got, steps, ready, expd, ext, ends = (
            st.sem(n) for n in ("wrote", "placed", "first", "got", "steps", "ready", "expd", "ext", "ends"))
        block = st.block()

        @block.sync
        def _(sp):
            sp.dma_start(nodes_view(table), tab[:, :, :]).then_inc(wrote, 16)
            if scores is not None:
                sp.dma_start(z[:, :, :], scores[0:E, :].rearrange("(p j) c -> p j c", j=J)).then_inc(got, 16)
            sp.wait_ge(placed, 16 * W)
            sp.dma_start(v[:, :, :], start.rearrange("(p j) c -> p j c", j=J)).then_inc(got, 16)
            if xdst is not None:
                sp.wait_ge(ready, 1)
                sp.dma_start(xdst[0:E, :].rearrange("(p j) c -> p j c", j=J), v[:, :, :]).then_inc(ends, 16)
                sp.wait_ge(ends, 16)
            else:
                sp.wait_ge(expd, 1)
                sp.dma_start(weights[0:E, :].rearrange("(p j) c -> p j c", j=J), z[:, :, :]).then_inc(ends, 16)
                sp.wait_ge(ext, 16)
                sp.dma_start(edge_rows(weights, heads)[G:NG].rearrange("g p c -> g (p c)"), big[:, :]).then_inc(ends, 16)
                sp.wait_ge(ends, 32)

        @block.gpsimd
        def _(pool):
            for w in range(W):
                pool.indirect_dma_start(out=start, in_=tab[:, w, :], in_offset=None,
                                        out_offset=bass.IndirectOffsetOnAxis(ap=k.start[:, w:w + 1], axis=0),
                                        bounds_check=E - 1, oob_is_err=False).then_inc(placed, 16)
            pool.wait_ge(wrote, 16)
            pool.indirect_dma_start(out=head[:, :], out_offset=None, in_=table,
                                    in_offset=bass.IndirectOffsetOnAxis(ap=k.first_i[:, :], axis=0)).then_inc(first, 16)
            if scores is not None:
                pool.wait_ge(ends, 16)
                pool.indirect_dma_start(
                    out=big[:, :], out_offset=None,
                    in_=weights[0:E, :].rearrange("(g e) c -> g (e c)", e=P * U),
                    in_offset=bass.IndirectOffsetOnAxis(ap=k.kx[:, :], axis=0)).then_inc(ext, 16)

        @block.vector
        def _(dve):
            s = Steps(dve, steps)
            dve.wait_ge(first, 16)
            dve.wait_ge(got, 16 if scores is None else 32)
            for h in range(c):
                ins = dve.tensor_tensor_scan(v[:, :, h], k.nstart[:, :], v[:, :, h], head[:, h:h + 1],
                                             ALU.mult, ALU.add)
                if h < c - 1 or scores is not None:
                    s.did(ins)
            if scores is None:
                ins.then_inc(ready, 1)
                return
            dve.wait_ge(steps, s.n)
            if c == 2 * heads:
                s.link(dve.tensor_tensor(z[:, :, :], z[:, :, :], v[:, :, 0:heads], ALU.add))
                s.link(dve.scalar_tensor_tensor(z[:, :, :], z[:, :, :], 0.2, z[:, :, :], ALU.mult, ALU.max))
            dve.tensor_tensor(z[:, :, :], z[:, :, :], v[:, :, c - heads:c], ALU.subtract).then_inc(ready, 1)

        if scores is not None:
            @block.scalar
            def _(act):
                act.wait_ge(ready, 1)
                nc.scalar.activation(z[:, :, :], z[:, :, :], ACT.Exp).then_inc(expd, 1)


def stage_sum(nc, k, name, gx, weights, heads, acc):
    m = heads * K1
    with Stage(nc, name) as st:
        fx = [st.sb(f"fx{r}", [P, U * K1]) for r in range(SLOTS)]
        wt = [st.sb(f"wt{r}", [P, U * heads]) for r in range(SLOTS)]
        msg = [st.sb(f"msg{r}", [P, U, heads, K1]) for r in range(SLOTS)]
        hot = [st.sb(f"hot{r}", [P, U, P]) for r in range(SLOTS)]
        p_s = [st.ps(f"p_s{r}", [128, 512]) for r in range(SLOTS)]
        got = [st.sem(f"got{r}") for r in range(SLOTS)]
        made, summed, added, marked = (st.sem(n) for n in ("made", "summed", "added", "marked"))
        block = st.block()

        @block.sync
        def _(sp):
            def trip(i, first):
                for r in range(SLOTS):
                    if not first:
                        sp.wait_ge(made, i * SLOTS + r + 1 - SLOTS)
                    for dram, o, c in ((gx, fx, K1), (weights, wt, heads)):
                        sp.dma_start(o[r][:, :], edge_rows(dram, c)[bass.ds(i * SLOTS + r, 1)]
                                     .rearrange("o p c -> (o p) c")).then_inc(got[r], 16)

            trip(0, True)
            with sp.Fori(1, TRIPS) as i:
                trip(i, False)

        @block.vector
        def _(dve):
            def message(i, r, first):
                dve.wait_ge(got[r], 32 * i + 32)
                if not first:
                    dve.wait_ge(summed, i * SLOTS + r + 1 - SLOTS)
                dve.tensor_tensor(msg[r][:, :, :, :],
                                  bcast(fx[r][:, :].rearrange("p (u f) -> p u f", f=K1), 2, heads),
                                  bcast(wt[r][:, :].rearrange("p (u h) -> p u h", h=heads), 3, K1),
                                  ALU.mult).then_inc(made, 1)
                dve.tensor_tensor(hot[r][:, :, :], bcast(k.lane[:, :], 1, U),
                                  bcast(k.dloc[:, bass.ds((i * SLOTS + r) * U, U)], 2, P), ALU.is_equal
                                  ).then_inc(marked, 1)

            def add(g, r, first):
                w = dve.value_load(k.wrow[0:1, bass.ds(g, 1)], min_val=0, max_val=W - 1)
                dve.wait_ge(summed, g + 1)
                a = acc[:, bass.ds(w, 1), :].rearrange("p o m -> p (o m)")
                dve.wait_ge(added, g + 1)
                dve.tensor_tensor(a, a, p_s[r][0:P, 0:m], ALU.add).then_inc(added, 1)

            dve.memset(acc[:, :, :], 0.0).then_inc(added, 1)
            message(0, 0, True)
            message(0, 1, True)
            add(0, 0, True)
            message(0, 2, True)
            add(1, 1, False)
            with dve.Fori(1, TRIPS) as i:
                for r in range(SLOTS):
                    message(i, r, False)
                    add(i * SLOTS + r - 1, (r - 1) % SLOTS, False)
            add(NG - 1, SLOTS - 1, False)

        @block.tensor
        def _(pe):
            def trip(i, first):
                for r in range(SLOTS):
                    pe.wait_ge(made, i * SLOTS + r + 1)
                    pe.wait_ge(marked, i * SLOTS + r + 1)
                    if not first:
                        pe.wait_ge(added, i * SLOTS + r + 2 - SLOTS)
                    for u in range(U):
                        ins = nc.tensor.matmul(p_s[r][0:P, 0:m], hot[r][:, u, :],
                                               msg[r][:, u, :, :].rearrange("p h f -> p (h f)"),
                                               start=u == 0, stop=u == U - 1)
                    ins.then_inc(summed, 1)

            trip(0, True)
            with pe.Fori(1, TRIPS) as i:
                trip(i, False)


def stage_gat_max(nc, k, name, heads, amax, a_src, a_dst, tab, self_w):
    with Stage(nc, name) as st:
        z = st.sb("z", [P, W, heads])
        steps, ready, done = st.sem("steps"), st.sem("ready"), st.sem("done")
        block = st.block()

        @block.vector
        def _(dve):
            s = Steps(dve, steps)
            m = tab[:, :, heads:2 * heads]
            s.did(dve.tensor_copy(tab[:, :, 0:heads], a_dst))
            s.link(dve.tensor_tensor(m, amax[:, :, :], a_src, ALU.max))
            s.did(dve.tensor_tensor(z[:, :, :], a_src, a_dst, ALU.add))
            s.link(dve.tensor_tensor(m, m, a_dst, ALU.add))
            s.did(dve.scalar_tensor_tensor(z[:, :, :], z[:, :, :], 0.2, z[:, :, :], ALU.mult, ALU.max))
            s.link(dve.scalar_tensor_tensor(m, m, 0.2, m, ALU.mult, ALU.max))
            dve.tensor_tensor(z[:, :, :], z[:, :, :], m, ALU.subtract).then_inc(ready, 1)

        @block.scalar
        def _(act):
            act.wait_ge(ready, 1)
            nc.scalar.activation(self_w[:, :, :], z[:, :, :], ACT.Exp).then_inc(done, 1)
            act.wait_ge(done, 1)


def stage_gat_mean(nc, k, name, heads, acc, self_w, feats, out):
    with Stage(nc, name) as st:
        own = st.sb("own", [P, W, heads, D])
        den = st.sb("den", [P, W, heads])
        steps = st.sem("steps")
        block = st.block()

        @block.vector
        def _(dve):
            s = Steps(dve, steps)
            a = acc[:, :, :].rearrange("p w (h f) -> p w h f", f=K1)
            for h in range(heads):
                s.did(dve.tensor_tensor(own[:, :, h, :], feats, self_w[:, :, h:h + 1].broadcast_to([P, W, D]), ALU.mult))
            s.link(dve.tensor_tensor(den[:, :, :], a[:, :, :, D], self_w[:, :, :], ALU.add))
            s.link(dve.tensor_scalar(den[:, :, :], den[:, :, :], 1e-16, None, ALU.add))
            s.link(dve.reciprocal(den[:, :, :], den[:, :, :]))
            for h in range(heads):
                s.link(dve.tensor_tensor(own[:, :, h, :], own[:, :, h, :], a[:, :, h, 0:D], ALU.add))
                s.did(dve.tensor_tensor(out[:, :, h * D:(h + 1) * D], own[:, :, h, :],
                                        den[:, :, h:h + 1].broadcast_to([P, W, D]), ALU.mult))


def stage_norm(nc, k, name, y, scale=1.0, bias=None, twice=False, out=None):
    with Stage(nc, name) as st:
        sq = st.sb("sq", [P, W, D])
        mean, var = st.sb("mean", [P, W]), st.sb("var", [P, W])
        steps, ready, rooted, fin, wrote = (st.sem(n) for n in ("steps", "ready", "rooted", "fin", "wrote"))
        block = st.block()

        @block.vector
        def _(dve):
            s = Steps(dve, steps)
            if twice:
                s.link(dve.tensor_tensor(y, y, k.x[:, :, :], ALU.add))
            s.link(dve.scalar_tensor_tensor(k.x[:, :, :], y, scale, k.x[:, :, :], ALU.mult, ALU.add))
            if bias is not None:
                s.link(dve.tensor_tensor(k.x[:, :, :], k.x[:, :, :], bcast(bias, 1, W), ALU.add))
            s.link(dve.tensor_reduce(mean[:, :], k.x[:, :, :], AX, ALU.add))
            s.link(dve.tensor_scalar(mean[:, :], mean[:, :], 1.0 / D, None, ALU.mult))
            s.link(dve.tensor_tensor(k.x[:, :, :], k.x[:, :, :], bcast(mean[:, :], 2, D), ALU.subtract))
            s.link(dve.tensor_tensor(sq[:, :, :], k.x[:, :, :], k.x[:, :, :], ALU.mult))
            s.link(dve.tensor_reduce(var[:, :], sq[:, :, :], AX, ALU.add))
            dve.tensor_scalar(var[:, :], var[:, :], 1.0 / D, EPS_LN, ALU.mult, ALU.add).then_inc(ready, 1)
            dve.wait_ge(rooted, 1)
            s.link(dve.reciprocal(var[:, :], var[:, :]))
            dve.tensor_tensor(k.x[:, :, :], k.x[:, :, :], bcast(var[:, :], 2, D), ALU.mult).then_inc(fin, 1)

        @block.scalar
        def _(act):
            act.wait_ge(ready, 1)
            nc.scalar.activation(var[:, :], var[:, :], ACT.Sqrt).then_inc(rooted, 1)

        if out is not None:
            @block.sync
            def _(sp):
                sp.wait_ge(fin, 1)
                sp.dma_start(nodes_view(out), k.x[:, :, :]).then_inc(wrote, 16)
                sp.wait_ge(wrote, 16)


def stage_load(nc, k, x):
    with Stage(nc, "ld") as st:
        got = st.sem("got")
        block = st.block()

        @block.sync
        def _(sp):
            sp.dma_start(k.x[:, :, :], nodes_view(x)).then_inc(got, 16)
            sp.wait_ge(got, 16)


def gat(nc, k, t):
    with Stage(nc, "gat") as st:
        k.mix1 = st.sb("mix1", [128, 2, 128])
        k.w2, k.b1, k.b2 = st.sb("w2", [128, 2, D + 2]), st.sb("b1", [128, 2]), st.sb("b2", [P, D])
        k.att1 = st.sb("att1", [D, 1, 2 * H1])
        stage_gat_weights(nc, k, t)
        mean2 = st.sb("mean2", [P, W, D])
        hid = st.sb("hid", [P, W, D + 2])
        with Stage(nc, "gat1") as s1:
            a1 = s1.sb("a1", [P, W, 2 * H1])
            stage_windows(nc, k, "wa", k.x, 1, D, k.att1, a1)
            stage_table(nc, k, "ta", k.table1, (k.x[:, :, :], None, a1[:, :, 0:H1]))
            stage_gather(nc, k, "ga", k.table1, k.gx, k.sc8, H1)
            amax, tab, self_w = s1.sb("amax", [P, W, H1]), s1.sb("tab", [P, W, 2 * H1]), s1.sb("self_w", [P, W, H1])
            stage_segmax(nc, k, "sa", k.sc8, H1, k.scan8, amax)
            stage_gat_max(nc, k, "ma", H1, amax, a1[:, :, 0:H1], a1[:, :, H1:2 * H1], tab, self_w)
            stage_spread(nc, k, "ea", tab, k.node16, k.start16, scores=k.sc8, heads=H1, weights=k.wt8)
            acc, mean = s1.sb("acc", [P, W, H1 * K1]), s1.sb("mean", [P, W, H1 * D])
            stage_sum(nc, k, "ua", k.gx, k.wt8, H1, acc)
            stage_gat_mean(nc, k, "na", H1, acc, self_w, k.x[:, :, :], mean)
            stage_windows(nc, k, "wb", mean, 2, 128, k.w2, hid, mid=k.mix1, bias=k.b1)
        with Stage(nc, "gat2") as s2:
            stage_table(nc, k, "tb", k.table2, (hid[:, :, 0:D], None, hid[:, :, D:D + 1]))
            stage_gather(nc, k, "gb", k.table2, k.gx, k.sc1, H2)
            amax, tab, self_w = s2.sb("amax", [P, W, H2]), s2.sb("tab", [P, W, 2 * H2]), s2.sb("self_w", [P, W, H2])
            stage_segmax(nc, k, "sb", k.sc1, H2, k.scan1, amax)
            stage_gat_max(nc, k, "mb", H2, amax, hid[:, :, D:D + 1], hid[:, :, D + 1:D + 2], tab, self_w)
            stage_spread(nc, k, "eb", tab, k.node2, k.start2, scores=k.sc1, heads=H2, weights=k.wt1)
            acc = s2.sb("acc", [P, W, H2 * K1])
            stage_sum(nc, k, "ub", k.gx, k.wt1, H2, acc)
            stage_gat_mean(nc, k, "nb", H2, acc, self_w, hid[:, :, 0:D], mean2)
        stage_norm(nc, k, "l0", mean2[:, :, :], bias=k.b2[:, :], out=k.out if k.layers == 1 else None)


CHUNK = 4 * P
CHUNKS = -(-N // CHUNK)
RING = 3


def stage_adjacency(nc, k, counts):
    F16 = mybir.dt.float16
    MIDDLE = N // 2
    with Stage(nc, "ad") as st:
        column = st.sb("column", [P, N], F16)
        srcf = st.sb("srcf", [P, NGP * U])
        hot_s = st.sb("hot_s", [P, RING, N], BF16)
        hot_d = st.sb("hot_d", [P, RING, P], BF16)
        p_c = [st.ps(f"p_c{c}", [128, 512]) for c in range(CHUNKS)]
        cst, hot, used, full, added = (st.sem(n) for n in ("cst", "hot", "used", "full", "added"))
        block = st.block()

        @block.gpsimd
        def _(pool):
            pool.iota(column[:, :], [[1, N]], base=-MIDDLE, channel_multiplier=0,
                      allow_small_or_imprecise_dtypes=True).then_inc(cst, 1)

        @block.vector
        def _(dve):
            def one_hot(q, slot, first=False):
                if not first:
                    dve.wait_ge(used, q - RING + 1)
                dve.tensor_scalar(hot_s[:, slot, :], column[:, :], srcf[:, bass.ds(q, 1)], None, ALU.is_equal)
                dve.tensor_scalar(hot_d[:, slot, :], k.lane[:, :], k.dloc[:, bass.ds(q, 1)], None,
                                  ALU.is_equal).then_inc(hot, 1)

            def add(g):
                w = dve.value_load(k.wrow[0:1, bass.ds(g, 1)], min_val=0, max_val=W - 1)
                for c in range(CHUNKS):
                    n = min(CHUNK, N - c * CHUNK)
                    if c == 0:
                        dve.wait_ge(added, g * CHUNKS + 1)
                    if c < CHUNKS - 1:
                        dve.wait_ge(full, g * (CHUNKS - 1) + c + 1)
                    else:
                        dve.wait_ge(used, g * U + U)
                    a = counts[:, bass.ds(w, 1), c * CHUNK:c * CHUNK + n].rearrange("p o n -> p (o n)")
                    dve.tensor_tensor(a, a, p_c[c][0:P, 0:n], ALU.add).then_inc(added, 1)

            def group(g, r, start):
                for q in range(2, U + 2):
                    one_hot(g * U + q, (r * U + q) % RING, start and q < RING)
                add(g)

            dve.wait_ge(cst, 1)
            dve.memset(counts[:, 0:W // 2, :], 0.0)
            dve.memset(counts[:, W // 2:W, :], 0.0)
            dve.tensor_scalar(srcf[:, :], k.srcidx[:, :], float(-MIDDLE), None, ALU.add).then_inc(added, 1)
            dve.wait_ge(added, 1)
            one_hot(0, 0, True)
            one_hot(1, 1, True)
            for r in range(SLOTS):
                group(r, r, r == 0)
            with dve.Fori(1, TRIPS) as i:
                for r in range(SLOTS):
                    group(i * SLOTS + r, r, False)

        @block.tensor
        def _(pe):
            def group(g, r, first):
                for u in range(U):
                    slot = (r * U + u) % RING
                    pe.wait_ge(hot, g * U + u + 1)
                    for c in range(CHUNKS):
                        n = min(CHUNK, N - c * CHUNK)
                        if u == 0 and not first:
                            pe.wait_ge(added, (g - 1) * CHUNKS + c + 2)
                        ins = nc.tensor.matmul(p_c[c][0:P, 0:n], hot_d[:, slot, :],
                                               hot_s[:, slot, c * CHUNK:c * CHUNK + n],
                                               start=u == 0, stop=u == U - 1)
                        if u == U - 1 and c < CHUNKS - 1:
                            ins.then_inc(full, 1)
                    ins.then_inc(used, 1)

            for r in range(SLOTS):
                group(r, r, r == 0)
            with pe.Fori(1, TRIPS) as i:
                for r in range(SLOTS):
                    group(i * SLOTS + r, r, False)

    EVEN = P + 1
    ROOM = [(0, 7), (7, 13), (13, 19), (19, 25)]
    with Stage(nc, "tu") as st:
        ident = st.sb("ident", [P, P], BF16)
        p_t = [st.ps(f"p_t{n}", [128, 1024], BF16) for n in range(4)]
        cst, turned, kept_a, kept_d = (st.sem(n) for n in ("cst", "turned", "kept_a", "kept_d"))
        block = st.block()

        def keep(copy, w, n, sem):
            a, b = ROOM[n]
            copy(counts[:, bass.ds(w, 1), a * P:b * P].rearrange("p o (n e) -> p (o n) e", e=P),
                 p_t[n][0:P, 0:(b - a) * EVEN].rearrange("p (n e) -> p n e", e=EVEN)[:, :, 0:P]).then_inc(sem, 1)

        @block.tensor
        def _(pe):
            pe.wait_ge(cst, 1)

            def window(w, first):
                for n, (a, b) in enumerate(ROOM):
                    if not first and n == 0:
                        pe.wait_ge(kept_a, 2 * w)
                        pe.wait_ge(kept_d, 2 * w)
                    for c in range(a, b):
                        ins = nc.tensor.transpose(p_t[n][0:P, (c - a) * EVEN:(c - a) * EVEN + P],
                                                  counts[:, bass.ds(w, 1), c * P:(c + 1) * P]
                                                  .rearrange("p o n -> p (o n)"), ident[:, :])
                    ins.then_inc(turned, 1)

            window(0, True)
            with pe.Fori(1, W) as w:
                window(w, False)

        @block.vector
        def _(dve):
            dve.tensor_copy(ident[:, :], k.ident[0:P, 0:P]).then_inc(cst, 1)
            with dve.Fori(0, W) as w:
                for n in (0, 2):
                    dve.wait_ge(turned, w * 4 + n + 1)
                    keep(dve.tensor_copy, w, n, kept_d)

        @block.scalar
        def _(act):
            with act.Fori(0, W) as w:
                for n in (1, 3):
                    act.wait_ge(turned, w * 4 + n + 1)
                    keep(nc.scalar.copy, w, n, kept_a)


def stage_appnp(nc, k, counts, out):
    WB = 5
    BANKS = W // WB
    with Stage(nc, "ap") as st:
        sn, dn = st.sb("sn", [P, W]), st.sb("dn", [P, W])
        x0 = st.sb("x0", [P, W, D])
        parts = st.sb("parts", [P, 2, W, 3, D], BF16)
        rest = st.sb("rest", [P, W, D])
        p_f = [st.ps(f"p_f{b}", [128, 512]) for b in range(BANKS)]
        steps, ready, rooted, split, summed, own = (
            st.sem(n) for n in ("steps", "ready", "rooted", "split", "summed", "own"))
        block = st.block()

        @block.scalar
        def _(act):
            act.wait_ge(ready, 2)
            nc.scalar.activation(sn[:, :], sn[:, :], ACT.Sqrt)
            nc.scalar.activation(dn[:, :], dn[:, :], ACT.Sqrt).then_inc(rooted, 1)

        @block.vector
        def _(dve):
            LINKS = 8

            def scale_and_split(at, w0, n, chain):
                f, rs = out[:, w0:w0 + n, :], rest[:, w0:w0 + n, :]
                hi, mid, lo = (parts[:, at, w0:w0 + n, j, :] for j in range(3))
                chain.link(dve.tensor_tensor(rs, f, bcast(sn[:, w0:w0 + n], 2, D), ALU.mult))
                chain.link(dve.tensor_copy(hi, rs))
                chain.link(dve.tensor_tensor(rs, rs, hi, ALU.subtract))
                chain.link(dve.tensor_copy(mid, rs))
                chain.link(dve.tensor_tensor(rs, rs, mid, ALU.subtract))
                dve.tensor_copy(lo, rs).then_inc(split, 1)

            dve.tensor_scalar(sn[:, :], k.outdeg[:, :], 1.0, None, ALU.max).then_inc(ready, 1)
            dve.tensor_scalar(dn[:, :], k.indeg[:, :], 1.0, None, ALU.max).then_inc(ready, 1)
            dve.wait_ge(rooted, 1)
            s = Steps(dve, steps)
            s.did(dve.reciprocal(sn[:, :], sn[:, :]))
            s.link(dve.reciprocal(dn[:, :], dn[:, :]))
            s.did(dve.tensor_scalar(dn[:, :], dn[:, :], 1.0 - ALPHA, None, ALU.mult))
            s.did(dve.tensor_scalar(x0[:, :, :], k.x[:, :, :], ALPHA, None, ALU.mult))
            s.link(dve.tensor_copy(out[:, :, :], k.x[:, :, :]))
            for b in range(BANKS):
                scale_and_split(0, b * WB, WB, s)
            with dve.Fori(0, STEPS_APPNP // 2) as i:
                for half in range(2):
                    for b in range(BANKS):
                        w0 = b * WB
                        step = (i * 2 + half) * BANKS + b
                        chain = Steps(dve, own, step * LINKS)
                        dve.wait_ge(summed, step + 1)
                        f = out[:, w0:w0 + WB, :]
                        chain.link(dve.tensor_reduce(
                            f, p_f[b][0:P, 0:WB * 3 * D].rearrange("p (w j f) -> p w f j", w=WB, j=3), AX, ALU.add))
                        chain.link(dve.tensor_tensor(f, f, bcast(dn[:, w0:w0 + WB], 2, D), ALU.mult))
                        chain.link(dve.tensor_tensor(f, f, x0[:, w0:w0 + WB, :], ALU.add))
                        scale_and_split(1 - half, w0, WB, chain)

        @block.tensor
        def _(pe):
            def bank(i, half, b):
                for w in range(b * WB, (b + 1) * WB):
                    for c in range(W):
                        at = (w - b * WB) * 3 * D
                        ins = nc.tensor.matmul(p_f[b][0:P, at:at + 3 * D], counts[:, w, c * P:(c + 1) * P],
                                               parts[:, half, c, :, :].rearrange("p j f -> p (j f)"),
                                               start=c == 0, stop=c == W - 1)
                ins.then_inc(summed, 1)

            with pe.Fori(0, STEPS_APPNP // 2) as i:
                for half in range(2):
                    pe.wait_ge(split, (i * 2 + half) * BANKS + BANKS)
                    for b in range(BANKS):
                        bank(i, half, b)


def appnp(nc, k):
    with Stage(nc, "pp") as st:
        counts = st.sb("counts", [P, W, N], BF16)
        stage_adjacency(nc, k, counts)
        f = st.sb("f", [P, W, D])
        stage_appnp(nc, k, counts, f)
        stage_norm(nc, k, "l1", f[:, :, :], out=k.out if k.layers == 2 else None)


def stage_attention_weights(nc, k, t, keys, values):
    with Stage(nc, "aw") as st:
        raw = st.sb("raw", [D, 3, HQ, D])
        turned = st.sb("turned", [D, 3, HQ * D])
        wout = st.sb("wout", [D, D])
        p_t, p_k, p_v = (st.ps(n, [128, 512]) for n in ("p_t", "p_k", "p_v"))
        got, flipped, copied, done = (st.sem(n) for n in ("got", "flipped", "copied", "done"))
        block = st.block()

        @block.sync
        def _(sp):
            for n, a in enumerate(("L2_gnn_Wq", "L2_gnn_Wk", "L2_gnn_Wv")):
                sp.dma_start(raw[:, n, :, :], t[a].rearrange("h f o -> f h o")).then_inc(got, 16)
            sp.dma_start(wout[:, :], t["L2_gnn_Wout"]).then_inc(got, 16)

        @block.tensor
        def _(pe):
            pe.wait_ge(got, 64)
            for n in range(3):
                for h in range(HQ):
                    at = (n * HQ + h) * D
                    ins = nc.tensor.transpose(p_t[0:D, at:at + D], raw[:, n, h, :], k.ident[0:D, 0:D])
            ins.then_inc(flipped, 1)
            pe.wait_ge(copied, 1)
            for h in range(HQ):
                ins = nc.tensor.matmul(p_k[0:D, h * D:(h + 1) * D], turned[:, 1, h * D:(h + 1) * D],
                                       turned[:, 0, h * D:(h + 1) * D], start=True, stop=True)
            ins.then_inc(flipped, 1)
            nc.tensor.matmul(p_v[0:HQ * D, 0:D], turned[:, 2, :], wout[:, :], start=True, stop=True).then_inc(flipped, 1)

        @block.vector
        def _(dve):
            dve.wait_ge(flipped, 1)
            dve.tensor_copy(turned[:, :, :], p_t[0:D, 0:3 * HQ * D].rearrange("p (n c) -> p n c", n=3)).then_inc(copied, 1)
            dve.wait_ge(flipped, 3)
            dve.tensor_scalar(keys[:, 0, :], p_k[0:D, 0:HQ * D], float(D) ** -0.5, None, ALU.mult)
            dve.tensor_scalar(values[:, 0, :], p_v[0:HQ * D, 0:D], 1.0 / HQ, None, ALU.mult).then_inc(done, 1)


def stage_divide(nc, k, acc, mean):
    with Stage(nc, "dv") as st:
        den, none = st.sb("den", [P, W, HQ]), st.sb("none", [P, W, HQ])
        steps = st.sem("steps")
        block = st.block()

        @block.vector
        def _(dve):
            s = Steps(dve, steps)
            a = acc[:, :, :].rearrange("p w (h f) -> p w h f", f=K1)
            s.link(dve.tensor_scalar(none[:, :, :], a[:, :, :, D], 0.0, None, ALU.is_le))
            s.link(dve.tensor_tensor(den[:, :, :], a[:, :, :, D], none[:, :, :], ALU.add))
            s.link(dve.reciprocal(den[:, :, :], den[:, :, :]))
            for h in range(HQ):
                s.did(dve.tensor_tensor(mean[:, :, h * D:(h + 1) * D], a[:, :, h, 0:D],
                                        den[:, :, h:h + 1].broadcast_to([P, W, D]), ALU.mult))


def attention(nc, k, t):
    with Stage(nc, "at") as st:
        keys, values = st.sb("keys", [D, 1, HQ * D]), st.sb("values", [HQ * D, 1, D])
        stage_attention_weights(nc, k, t, keys, values)
        with Stage(nc, "at1") as s1:
            y = s1.sb("y", [P, W, HQ * D])
            stage_windows(nc, k, "wk", k.x, 1, D, keys, y)
            stage_table(nc, k, "tk", k.table4, (k.x[:, :, :], None, y[:, :, :]))
        stage_spread(nc, k, "xd", k.x, k.node32, k.start32, xdst=k.xdst)
        stage_gather(nc, k, "gk", k.table4, k.gx, k.sc4, HQ, products=True)
        amax = st.sb("amax", [P, W, HQ])
        stage_segmax(nc, k, "sk", k.sc4, HQ, k.scan4, amax)
        stage_spread(nc, k, "ek", amax, k.node4, k.start4, scores=k.sc4, heads=HQ, weights=k.wt4)
        acc, mean, y = st.sb("acc", [P, W, HQ * K1]), st.sb("mean", [P, W, HQ * D]), st.sb("y", [P, W, D])
        stage_sum(nc, k, "uk", k.gx, k.wt4, HQ, acc)
        stage_divide(nc, k, acc, mean)
        stage_windows(nc, k, "wv", mean, 1, HQ * D, values, y)
        stage_norm(nc, k, "l2", y[:, :, :], twice=True, out=k.out if k.layers == 3 else None)


INV_SQRT3 = float(1.0 / np.sqrt(3.0))
A_SCALAR = float(np.sqrt(1.0 / 128.0))
A_VECTOR = float(np.sqrt(3.0 / 128.0))


def stage_conv(nc, k, t, acc):
    PAIR = [(0, 2), (2, 4), (4, 5)]
    BANKS_H = [(0, 4), (4, 8), (8, 10)]
    KF = 3 * MUL
    with Stage(nc, "cv") as st:
        fc1 = st.sb("fc1", [U * BASIS, U, 2, 128])
        fc2 = st.sb("fc2", [128, 2, HID])
        fx = [st.sb(f"fx{r}", [P, U * K1]) for r in range(SLOTS)]
        e4 = [st.sb(f"e4{r}", [P, U * 4]) for r in range(SLOTS)]
        e8 = [st.sb(f"e8{r}", [P, U * BASIS]) for r in range(SLOTS)]
        e8t = [st.sb(f"e8t{r}", [U * BASIS, P]) for r in range(SLOTS)]
        hid = [st.sb(f"hid{r}", [128, 2 * U, P]) for r in range(SLOTS)]
        q = [st.sb(f"q{r}", [P, 3, U, 4]) for r in range(SLOTS)]
        dot = [st.sb(f"dot{r}", [P, U, 3, MUL]) for r in range(SLOTS)]
        fac = [st.sb(f"fac{r}", [P, U, KF]) for r in range(SLOTS)]
        vec = [st.sb(f"vec{r}", [P, U, 3, MUL]) for r in range(SLOTS)]
        prod = st.sb("prod", [P, U, MUL, 2 * KF])
        red = st.sb("red", [P, U, MUL, 4])
        outer = st.sb("outer", [P, U, MUL, 3])
        msg = [st.sb(f"msg{r}", [P, U, D]) for r in range(SLOTS)]
        hot = [st.sb(f"hot{r}", [P, U, P]) for r in range(SLOTS)]
        p_t, p_s = st.ps("p_t", [128, 512]), st.ps("p_s", [128, 512])
        p_h = [st.ps(f"p_h{n}", [128, 512]) for n in range(3)]
        p_w = [st.ps(f"p_w{n}", [128, 512]) for n in range(3)]
        z, ready, turned, flat, hidden, bent, weighed, read, made, summed, added, factors, steps, own, reads = (
            st.sem(n) for n in ("z", "ready", "turned", "flat", "hidden", "bent", "weighed", "read", "made",
                                "summed", "added", "factors", "steps", "own", "reads"))
        wgot, gt = st.sem("wgot"), st.sem("gt")
        got = [st.sem(f"got{r}") for r in range(SLOTS)]
        block = st.block()

        @block.sync
        def _(sp):
            sp.wait_ge(z, 1)
            for u in range(U):
                sp.dma_start(fc1[u * BASIS:(u + 1) * BASIS, u, :, :],
                             t["L3_gnn_fc_w1"].rearrange("b (c h) -> b c h", c=2)).then_inc(wgot, 16)
            sp.dma_start(fc2[:, :, :], t["L3_gnn_fc_w2"].rearrange("(c h) n -> h c n", c=2)).then_inc(wgot, 16)

            def trip(i, first):
                for r in range(SLOTS):
                    if not first:
                        sp.wait_ge(made, i * SLOTS + r + 1 - SLOTS)
                        sp.wait_ge(flat, i * SLOTS + r + 1 - SLOTS)
                    for dram, o, c in ((k.gx, fx, K1), (k.ea4x, e4, 4), (k.ea8x, e8, BASIS)):
                        sp.dma_start(o[r][:, :], edge_rows(dram, c)[bass.ds(i * SLOTS + r, 1)]
                                     .rearrange("o p c -> (o p) c")).then_inc(got[r], 16)

            trip(0, True)
            with sp.Fori(1, TRIPS) as i:
                trip(i, False)

        @block.gpsimd
        def _(pool):
            pool.memset(fc1[:, :, :, :], 0.0).then_inc(z, 1)
            OPS = 8

            def trip(i, first):
                for r in range(SLOTS):
                    s = Steps(pool, factors, (i * SLOTS + r) * OPS)

                    def after():
                        pool.wait_ge(factors, s.base + s.n)
                        gate(pool, gt)

                    pool.wait_ge(got[r], 48 * i + 48)
                    gate(pool, gt)
                    if not first:
                        pool.wait_ge(made, i * SLOTS + r + 1 - SLOTS)
                        gate(pool, gt)
                    e = e4[r][:, :].rearrange("p (u c) -> p u c", c=4)
                    f = fx[r][:, :].rearrange("p (u c) -> p u c", c=K1)
                    scalars = f[:, :, 0:MUL]
                    vectors = f[:, :, MUL:D].rearrange("p u (m i) -> p u i m", i=3)
                    for n, c in enumerate((A_SCALAR, A_SCALAR * INV_SQRT3, A_VECTOR * INV_SQRT3)):
                        s.did(pool.tensor_scalar(q[r][:, n, :, :], e, c, None, ALU.mult))
                    after()
                    s.did(pool.tensor_tensor(fac[r][:, :, 0:MUL], scalars,
                                             q[r][:, 0, :, 0:1].broadcast_to([P, U, MUL]), ALU.mult))
                    s.did(pool.tensor_tensor(dot[r][:, :, :, :], vectors, bcast(q[r][:, 1, :, 1:4], 3, MUL), ALU.mult))
                    s.did(pool.tensor_tensor(
                        vec[r][:, :, :, :], vectors,
                        bcast(q[r][:, 2, :, 0:1].broadcast_to([P, U, 3]), 3, MUL), ALU.mult))
                    after()
                    s.did(pool.tensor_tensor(fac[r][:, :, MUL:2 * MUL], dot[r][:, :, 0, :], dot[r][:, :, 1, :], ALU.add))
                    after()
                    s.did(pool.tensor_tensor(fac[r][:, :, MUL:2 * MUL], fac[r][:, :, MUL:2 * MUL],
                                             dot[r][:, :, 2, :], ALU.add))
                    pool.tensor_scalar(fac[r][:, :, 2 * MUL:KF], scalars, A_VECTOR * INV_SQRT3, None,
                                       ALU.mult).then_inc(ready, 1)

            trip(0, True)
            with pool.Fori(1, TRIPS) as i:
                trip(i, False)

        @block.scalar
        def _(act):
            act.wait_ge(wgot, 16 * (U + 1))
            nc.scalar.mul(fc1[:, :, :, :], fc1[:, :, :, :], float(BASIS) ** -0.5)
            nc.scalar.mul(fc2[:, :, :], fc2[:, :, :], float(np.sqrt(2.0)) * float(HID) ** -0.5).then_inc(steps, 1)

            def trip(i, first):
                for r in range(SLOTS):
                    g = i * SLOTS + r
                    act.wait_ge(turned, g + 1)
                    nc.scalar.copy(e8t[r][:, :], p_t[0:U * BASIS, 0:P]).then_inc(flat, 1)
                    if not first:
                        act.wait_ge(weighed, (g - SLOTS) * 3 + 3)
                    for n, (a, b) in enumerate(BANKS_H):
                        act.wait_ge(hidden, g * 3 + n + 1)
                        nc.scalar.activation(hid[r][:, a:b, :], p_h[n][:, 0:(b - a) * P]
                                             .rearrange("p (n e) -> p n e", e=P), ACT.Relu).then_inc(bent, 1)

            trip(0, True)
            with act.Fori(1, TRIPS) as i:
                trip(i, False)

        @block.tensor
        def _(pe):
            pe.wait_ge(steps, 1)

            def hide(i, r, g, first):
                pe.wait_ge(got[r], 48 * i + 48)
                gate(pe, gt)
                if not first:
                    pe.wait_ge(flat, g)
                    gate(pe, gt)
                nc.tensor.transpose(p_t[0:U * BASIS, 0:P], e8[r][:, :], k.ident[0:P, 0:P]).then_inc(turned, 1)
                pe.wait_ge(flat, g + 1)
                for n, (a, b) in enumerate(BANKS_H):
                    if not first:
                        pe.wait_ge(bent, (g - 1) * 3 + n + 1)
                    for m in range(a, b):
                        ins = nc.tensor.matmul(p_h[n][:, (m - a) * P:(m - a + 1) * P], fc1[:, m // 2, m % 2, :],
                                               e8t[r][:, :], start=True, stop=True)
                    ins.then_inc(hidden, 1)

            def weigh(g, r, first):
                for n, (a, b) in enumerate(PAIR):
                    if not first:
                        pe.wait_ge(read, (g - 1) * 3 + n + 1)
                    pe.wait_ge(bent, g * 3 + n + 1)
                    for u in range(a, b):
                        for c in range(2):
                            ins = nc.tensor.matmul(p_w[n][0:P, (u - a) * HID:(u - a + 1) * HID],
                                                   hid[r][:, 2 * u + c, :], fc2[:, c, :], start=c == 0, stop=c == 1)
                    ins.then_inc(weighed, 1)

            def gather_up(g, r, first):
                pe.wait_ge(made, g + 1)
                if not first:
                    pe.wait_ge(added, g + 1)
                for u in range(U):
                    ins = nc.tensor.matmul(p_s[0:P, 0:D], hot[r][:, u, :], msg[r][:, u, :],
                                           start=u == 0, stop=u == U - 1)
                ins.then_inc(summed, 1)

            hide(0, 0, 0, True)
            weigh(0, 0, True)
            hide(0, 1, 1, False)
            weigh(1, 1, False)
            gather_up(0, 0, True)
            hide(0, 2, 2, False)
            weigh(2, 2, False)
            gather_up(1, 1, False)
            with pe.Fori(1, TRIPS) as i:
                for r in range(SLOTS):
                    g = i * SLOTS + r
                    hide(i, r, g, False)
                    weigh(g, r, False)
                    gather_up(g - 1, (r - 1) % SLOTS, False)
            gather_up(NG - 1, SLOTS - 1, False)

        @block.vector
        def _(dve):
            OPS = 3 + 3 + 3

            def contract(i, r, g, first):
                s = Steps(dve, own, g * OPS)
                if not first:
                    dve.wait_ge(summed, g - SLOTS + 1)
                dve.tensor_tensor(hot[r][:, :, :], bcast(k.lane[:, :], 1, U),
                                  bcast(k.dloc[:, bass.ds(g * U, U)], 2, P), ALU.is_equal)
                dve.wait_ge(ready, g + 1)
                m = msg[r][:, :, :]
                for n, (a, b) in enumerate(PAIR):
                    dve.wait_ge(weighed, g * 3 + n + 1)
                    wv = p_w[n][0:P, 0:(b - a) * HID].rearrange("p (u k w) -> p u w k", k=4 * MUL, w=MUL)
                    s.did(dve.tensor_tensor(prod[:, a:b, :, 0:KF], wv[:, :, :, 0:KF], bcast(fac[r][:, a:b, :], 2, MUL),
                                            ALU.mult))
                    for j in range(3):
                        ins = dve.tensor_tensor(prod[:, a:b, :, KF + j * MUL:KF + (j + 1) * MUL], wv[:, :, :, KF:4 * MUL],
                                                bcast(vec[r][:, a:b, j, :], 2, MUL), ALU.mult)
                    ins.then_inc(read, 1)
                dve.wait_ge(read, g * 3 + 3)
                s.did(dve.tensor_reduce(m[:, :, 0:MUL], prod[:, :, :, 0:2 * MUL], AX, ALU.add))
                s.link(dve.tensor_reduce(red[:, :, :, :], prod[:, :, :, 2 * MUL:2 * KF]
                                         .rearrange("p u w (j k) -> p u w j k", k=MUL), AX, ALU.add))
                for j in range(3):
                    v2 = e4[r][:, :].rearrange("p (u c) -> p u c", c=4)[:, :, 1 + j:2 + j].broadcast_to([P, U, MUL])
                    s.did(dve.tensor_tensor(outer[:, :, :, j], red[:, :, :, 0], v2, ALU.mult))
                dve.wait_ge(own, s.base + s.n)
                s.did(dve.tensor_tensor(
                    m[:, :, MUL:D].rearrange("p u (w j) -> p u w j", j=3), outer[:, :, :, :], red[:, :, :, 1:4],
                    ALU.add))
                dve.wait_ge(own, s.base + s.n)
                dve.nop().then_inc(made, 1)

            def add(g, first):
                w = dve.value_load(k.wrow[0:1, bass.ds(g, 1)], min_val=0, max_val=W - 1)
                dve.wait_ge(summed, g + 1)
                dve.wait_ge(added, g + 1)
                a = acc[:, bass.ds(w, 1), :].rearrange("p o m -> p (o m)")
                dve.tensor_tensor(a, a, p_s[0:P, 0:D], ALU.add).then_inc(added, 1)

            dve.memset(acc[:, :, :], 0.0).then_inc(added, 1)
            contract(0, 0, 0, True)
            contract(0, 1, 1, True)
            add(0, True)
            contract(0, 2, 2, True)
            add(1, False)
            with dve.Fori(1, TRIPS) as i:
                for r in range(SLOTS):
                    g = i * SLOTS + r
                    contract(i, r, g, False)
                    add(g - 1, False)
            add(NG - 1, False)


def conv(nc, k, t):
    with Stage(nc, "cn") as st:
        acc = st.sb("acc", [P, W, D])
        stage_table(nc, k, "tc", k.table3, (k.x[:, :, :], None))
        stage_gather(nc, k, "gc", k.table3, k.gx)
        stage_conv(nc, k, t, acc)
        stage_norm(nc, k, "l3", acc[:, :, :], scale=float(1.0 / np.sqrt(E / N)), out=k.out)


def build(nc, t, out, debug=None):
    k = Kept()
    with ExitStack() as ctx:
        def sb(name, shape, dt=F32):
            return ctx.enter_context(nc.sbuf_tensor(name, shape, dt))

        def dram(name, shape, dt=F32):
            return nc.dram_tensor(name, shape, dt, kind="Internal").ap()

        k.ident = sb("ident", [128, 128])
        k.ones = sb("ones", [P, P])
        k.lane = sb("lane", [P, P])
        k.earlier = sb("earlier", [P, P])
        k.negs = sb("negs", [1, 8])
        k.srcidx = sb("srcidx", [P, NGP * U], I32)
        k.dloc = sb("dloc", [P, NGP * U])
        k.kx = sb("kx", [X, 1], I32)
        k.wrow = sb("wrow", [1, NG], I32)
        k.first_i = sb("first_i", [P, 1], I32)
        k.nstart, k.newseg, k.notfirst = (sb(n, [P, J]) for n in ("nstart", "newseg", "notfirst"))
        k.indeg, k.outdeg = sb("indeg", [P, W]), sb("outdeg", [P, W])
        k.end, k.start = sb("end", [P, W], I32), sb("start", [P, W], I32)
        k.x = sb("x", [P, W, D])
        k.start16, k.start2, k.start32, k.start4 = (dram(f"start{c}", (E, c)) for c in (16, 2, 32, 4))
        k.xdst = dram("xdst", (NG * P * U, D))
        k.ea8x, k.ea4x = dram("ea8x", (NG * P * U, 8)), dram("ea4x", (NG * P * U, 4))
        k.wind = dram("wind", (NG, 1), I32)
        stage_index(nc, k, t["src"], t["dst"], t["edge_attr_4"], t["edge_attr_8"])
        k.layers = {"l0": 1, "l1": 2, "l2": 3}.get(debug, 4)
        k.out = out
        edges_x = NG * P * U
        k.table1, k.table2 = dram("table1", (N, K1 + H1)), dram("table2", (N, K1 + H2))
        k.table3, k.table4 = dram("table3", (N, K1)), dram("table4", (N, K1 + HQ * D))
        k.gx = dram("gx", (edges_x, K1))
        k.sc8, k.sc1, k.sc4 = (dram(f"sc{c}", (edges_x, c)) for c in (8, 1, 4))
        k.wt8, k.wt1, k.wt4 = (dram(f"wt{c}", (edges_x, c)) for c in (8, 1, 4))
        k.scan8, k.scan1, k.scan4 = (dram(f"scan{c}", (E + 1, c)) for c in (8, 1, 4))
        k.node16, k.node2, k.node32, k.node4 = (dram(f"node{c}", (N, c)) for c in (16, 2, 32, 4))
        if debug != "index":
            stage_load(nc, k, t["x"])
            gat(nc, k, t)
            if k.layers > 1:
                appnp(nc, k)
            if k.layers > 2:
                attention(nc, k, t)
            if k.layers > 3:
                conv(nc, k, t)
        if debug == "index":
            with Stage(nc, "dbg") as st:
                f = st.sb("f", [P, 4 * W + 2 * NG * U])
                done, go = st.sem("done"), st.sem("go")
                block = st.block()

                @block.vector
                def _(dve):
                    at = 0
                    for a, n in ((k.indeg, W), (k.outdeg, W), (k.end, W), (k.start, W), (k.dloc, NG * U), (k.srcidx, NG * U)):
                        dve.tensor_copy(f[:, at:at + n], a[:, 0:n]).then_inc(go, 1)
                        at += n

                @block.sync
                def _(sp):
                    sp.wait_ge(go, 6)
                    sp.dma_start(out, f[:, :]).then_inc(done, 16)
                    sp.wait_ge(done, 16)
            return


_INS = ["x", "src", "dst", "edge_attr_4", "edge_attr_8", "L0_gnn_W1", "L0_gnn_att_src1", "L0_gnn_att_dst1",
        "L0_gnn_b1", "L0_gnn_W2", "L0_gnn_att_src2", "L0_gnn_att_dst2", "L0_gnn_b2", "L2_gnn_Wq", "L2_gnn_Wk",
        "L2_gnn_Wv", "L2_gnn_Wout", "L3_gnn_fc_w1", "L3_gnn_fc_w2"]
OUT_SHAPE, DEBUG = (N, D), None


def kernel(**inputs):
    import concourse.bacc as bacc
    from concourse.bass_utils import run_bass_kernel_spmd

    nc = bacc.Bacc("TRN2", target_bir_lowering=False, num_devices=1)
    arrays, t = {}, {}
    for name in _INS:
        a = np.ascontiguousarray(inputs[name])
        arrays[f"in_{name}"] = a
        t[name] = nc.dram_tensor(f"in_{name}", a.shape, mybir.dt.from_np(a.dtype), kind="ExternalInput").ap()
    out = nc.dram_tensor("out_nodes", OUT_SHAPE, F32, kind="ExternalOutput").ap()
    build(nc, t, out, DEBUG)
    r = run_bass_kernel_spmd(nc, [arrays], core_ids=[0])
    return r.results[0]["out_nodes"]
```

```python
import numpy as np
from contextlib import ExitStack

import concourse.bass as bass
import concourse.mybir as mybir

F32, I32, BF16 = mybir.dt.float32, mybir.dt.int32, mybir.dt.bfloat16
ALU = mybir.AluOpType
ACT = mybir.ActivationFunctionType
AX = mybir.AxisListType.X

N, E, D = 3125, 103125, 32
P = 125
W = N // P
J = E // P
U = 5
G = E // (P * U)
X = W - 1
NG = G + X
SLOTS = 3
TRIPS = NG // SLOTS
TRIPS_G = G // SLOTS
MIDDLE = N // 2
NGP = NG + SLOTS
H1, H2, HQ = 8, 1, 4
K1 = D + 1
BIG = 1e30
EPS_LN = 1e-5
STEPS_APPNP = 10
ALPHA = 0.1
MUL, BASIS, HID = 8, 8, 256


class Steps:

    def __init__(self, eng, sem, base=0, n=0):
        self.eng, self.sem, self.base, self.n = eng, sem, base, n

    def did(self, ins):
        ins.then_inc(self.sem, 1)
        self.n += 1

    def link(self, ins):
        self.did(ins)
        self.eng.wait_ge(self.sem, self.base + self.n)


def gate(eng, gate_sem):
    eng.sem_inc(gate_sem, 1)


def bcast(ap, axis, n):
    shape = list(ap.shape)
    return ap.unsqueeze(axis).broadcast_to(shape[:axis] + [n] + shape[axis:])


class Kept:
    pass


class Stage:

    def __init__(self, nc, name):
        self.nc, self.name, self.ctx, self.sems = nc, name, ExitStack(), []

    def __enter__(self):
        self.ctx.__enter__()
        return self

    def __exit__(self, *a):
        left = self.ctx.__exit__(*a)
        if self.sems:
            self.nc.clear_and_free_semaphores(self.sems)
            self.nc.all_engine_barrier()
        return left

    def sb(self, name, shape, dt=F32):
        return self.ctx.enter_context(self.nc.sbuf_tensor(f"{self.name}_{name}", shape, dt))

    def ps(self, name, shape, dt=F32):
        return self.ctx.enter_context(self.nc.psum_tensor(f"{self.name}_{name}", shape, dt))

    def sem(self, name):
        self.sems.append(self.nc.alloc_semaphore(f"{self.name}_{name}"))
        return self.sems[-1]

    def block(self):
        return self.ctx.enter_context(self.nc.Block())


def edge_rows(dram, c):
    return dram.rearrange("(g p u) c -> g p (u c)", p=P, u=U)


def nodes_view(dram):
    return dram.rearrange("(w d) c -> d w c", d=P)


def stage_index(nc, k, src, dst):
    GB = G - 128
    with Stage(nc, "ix") as st:
        d_a, d_b, d_x = st.sb("d_a", [128, P * U], I32), st.sb("d_b", [GB, P * U], I32), st.sb("d_x", [X, P * U], I32)
        s_a, s_b, s_x = st.sb("s_a", [128, P * U], I32), st.sb("s_b", [GB, P * U], I32), st.sb("s_x", [X, P * U], I32)
        df = [st.sb(f"df{n}", [r, P * U]) for n, r in enumerate((128, GB, X))]
        sf = [st.sb(f"sf{n}", [r, P * U]) for n, r in enumerate((128, GB, X))]
        edges = st.sb("edges", [128, X])
        edge_col = st.sb("edge_col", [X, 1])
        win_x = st.sb("win_x", [X, 1], I32)
        ge = [st.sb(f"ge{n}", [128, X]) for n in range(2)]
        lt = [st.sb(f"lt{n}", [128, X]) for n in range(2)]
        wf = [st.sb(f"wf{n}", [128, 1]) for n in range(2)]
        w125 = [st.sb(f"w125{n}", [128, 1]) for n in range(2)]
        wi = [st.sb(f"wi{n}", [128, 1], I32) for n in range(2)]
        ones = st.sb("ones", [128, 1])
        kf, pen = st.sb("kf", [X, 1]), st.sb("pen", [X, 1])
        kxi = st.sb("kxi", [X, 1], I32)
        grid, gi = st.sb("gd", [P, J]), st.sb("gdi", [P, J], I32)
        prev = st.sb("prev", [P, 1], I32)
        prevf = st.sb("prevf", [P, 1])
        diag = st.sb("diag", [P, P])
        pt = [st.ps(f"pt{u}", [128, 512]) for u in range(U)]
        p_cnt, p_last = st.ps("p_cnt", [128, 512]), st.ps("p_last", [128, 512])
        loaded, cst, steps, pe_s, gone, ext_i, wrote, wback, fx, pool_s = (
            st.sem(n) for n in ("loaded", "cst", "steps", "pe_s", "gone", "ext_i", "wrote", "wback", "fx", "pool_s"))
        block = st.block()

        @block.sync
        def _(sp):
            sp.dma_start(d_a[:, :], dst[0:128 * P * U].rearrange("(g e) -> g e", e=P * U)).then_inc(loaded, 16)
            sp.dma_start(d_b[:, :], dst[128 * P * U:E].rearrange("(g e) -> g e", e=P * U)).then_inc(loaded, 16)
            sp.dma_start(s_a[:, :], src[0:128 * P * U].rearrange("(g e) -> g e", e=P * U)).then_inc(loaded, 16)
            sp.dma_start(s_b[:, :], src[128 * P * U:E].rearrange("(g e) -> g e", e=P * U)).then_inc(loaded, 16)
            sp.dma_start(gi[:, :], dst.rearrange("(p j) -> p j", j=J)).then_inc(loaded, 16)
            sp.wait_ge(cst, 1)
            sp.dma_start(prev[1:P, 0:1], dst.rearrange("(p j) -> p j", j=J)[0:P - 1, J - 1:J],
                         allow_slow_non_contiguous=True).then_inc(loaded, 16)
            sp.wait_ge(fx, 1)
            sp.dma_start(k.wind[0:128, :], wi[0][:, :]).then_inc(wrote, 16)
            sp.dma_start(k.wind[128:G, :], wi[1][0:GB, :]).then_inc(wrote, 16)
            sp.dma_start(k.wind[G:NG, :], win_x[:, :]).then_inc(wrote, 16)
            sp.dma_start(k.kxd, kxi[:, :]).then_inc(wrote, 16)
            sp.wait_ge(wrote, 64)
            sp.dma_start(k.wrow[:, :], k.wind.rearrange("g o -> o g")).then_inc(wback, 16)
            sp.dma_start(k.grow[:, G:NG], k.kxd.rearrange("g o -> o g")).then_inc(wback, 16)
            sp.wait_ge(wback, 32)

        @block.gpsimd
        def _(pool):
            s = Steps(pool, pool_s)
            pool.memset(prev[:, :], -1).then_inc(cst, 1)
            s.did(pool.memset(k.ident[:, :], 0.0))
            s.link(pool.memset(k.earlier[:, :], 0.0))
            pool.affine_select(out=k.ident[:, :], in_=k.ident[:, :], compare_op=ALU.not_equal, fill=1.0, base=0,
                               pattern=[[-1, 128]], channel_multiplier=1)
            pool.affine_select(out=k.earlier[:, :], in_=k.earlier[:, :], compare_op=ALU.is_gt, fill=-BIG, base=0,
                               pattern=[[-1, P]], channel_multiplier=1)
            pool.memset(ones[:, :], 1.0)
            pool.memset(k.ones[:, :], 1.0)
            pool.memset(k.srcf[:, :], 0.0)
            pool.memset(k.dloc[:, :], 0.0)
            pool.memset(k.negs[:, :], -BIG)
            pool.iota(edges[:, :], [[P, X]], base=P, channel_multiplier=0, allow_small_or_imprecise_dtypes=True)
            pool.iota(edge_col[:, :], [[0, 1]], base=P, channel_multiplier=P, allow_small_or_imprecise_dtypes=True)
            pool.iota(k.grow[:, 0:G], [[1, G]], base=0, channel_multiplier=0)
            pool.iota(win_x[:, :], [[0, 1]], base=1, channel_multiplier=1)
            pool.iota(k.lane[:, :], [[1, P]], base=0, channel_multiplier=0,
                      allow_small_or_imprecise_dtypes=True).then_inc(cst, 1)
            pool.wait_ge(fx, 1)
            by = bass.IndirectOffsetOnAxis(ap=kxi[:, :], axis=0)
            pool.indirect_dma_start(out=d_x[:, :], out_offset=None, in_=dst.rearrange("(g e) -> g e", e=P * U),
                                    in_offset=by).then_inc(ext_i, 16)
            pool.indirect_dma_start(out=s_x[:, :], out_offset=None, in_=src.rearrange("(g e) -> g e", e=P * U),
                                    in_offset=by).then_inc(ext_i, 16)

        @block.vector
        def _(dve):
            s = Steps(dve, steps)
            dve.wait_ge(loaded, 16 * 6)
            dve.wait_ge(cst, 2)
            for o, i in ((df[0], d_a), (df[1], d_b), (sf[0], s_a), (sf[1], s_b), (grid, gi),
                         (prevf, prev), (k.first_i, gi)):
                s.did(dve.tensor_copy(o[:, :], i[:, 0:o.shape[1]]))
            dve.wait_ge(steps, s.n)
            for n, r in ((0, 128), (1, GB)):
                s.link(dve.tensor_scalar(ge[n][0:r, :], edges[0:r, :], df[n][:, 0:1], None, ALU.is_le))
                s.did(dve.tensor_scalar(lt[n][0:r, :], ge[n][0:r, :], -1.0, 1.0, ALU.mult, ALU.add))
                s.link(dve.tensor_reduce(wf[n][0:r, :], ge[n][0:r, :], AX, ALU.add))
                s.did(dve.tensor_copy(wi[n][0:r, :], wf[n][0:r, :]))
                s.link(dve.tensor_scalar(w125[n][0:r, :], wf[n][0:r, :], float(P), None, ALU.mult))
                last = dve.tensor_scalar(df[n][:, :], df[n][:, :], w125[n][0:r, :], None, ALU.subtract)
                if n == 0:
                    s.did(last)
            last.then_inc(gone, 1)
            dve.wait_ge(pe_s, 1)
            s.link(dve.tensor_scalar(kf[:, :], p_cnt[0:X, 0:1], -1.0, 0.0, ALU.add, ALU.max))
            s.did(dve.tensor_scalar(pen[:, :], p_cnt[0:X, 0:1], 0.5, 8192.0, ALU.is_lt, ALU.mult))
            dve.tensor_copy(kxi[:, :], kf[:, :]).then_inc(fx, 1)
            s.link(dve.tensor_scalar(k.nstart[:, 0:1], grid[:, 0:1], prevf[:, 0:1], None, ALU.is_equal))
            s.link(dve.tensor_tensor(k.nstart[:, 1:J], grid[:, 1:J], grid[:, 0:J - 1], ALU.is_equal))
            s.link(dve.tensor_scalar(k.infirst[:, :], grid[:, :], grid[:, 0:1], None, ALU.is_equal))
            dve.tensor_scalar(diag[:, :], k.ident[0:P, 0:P], grid[:, J - 1:J], None, ALU.mult).then_inc(gone, 1)
            dve.wait_ge(pe_s, 2)
            s.link(dve.tensor_scalar(diag[:, :], p_last[0:P, 0:P], grid[:, 0:1], None, ALU.is_equal))
            s.link(dve.tensor_scalar(diag[:, :], diag[:, :], BIG, -BIG, ALU.mult, ALU.add))
            s.link(dve.tensor_tensor(k.earlier[:, :], k.earlier[:, :], diag[:, :], ALU.min))
            dve.wait_ge(ext_i, 32)
            s.did(dve.tensor_copy(df[2][:, :], d_x[:, :]))
            s.link(dve.tensor_copy(sf[2][:, :], s_x[:, :]))
            dve.tensor_scalar(df[2][:, :], df[2][:, :], edge_col[:, 0:1], pen[:, 0:1],
                              ALU.subtract, ALU.add).then_inc(gone, 1)
            dve.wait_ge(pe_s, 3)
            dl = k.dloc[:, :].rearrange("p (g u) -> p g u", u=U)
            si = k.srcf[:, :].rearrange("p (g u) -> p g u", u=U)
            for u in range(U):
                s.did(dve.tensor_copy(dl[:, 0:NG, u], pt[u][0:P, 0:NG]))
                s.did(dve.tensor_scalar(si[:, 0:NG, u], pt[u][0:P, 256:256 + NG], float(-MIDDLE), None, ALU.add))

        @block.tensor
        def _(pe):
            pe.wait_ge(cst, 2)
            pe.wait_ge(gone, 1)
            nc.tensor.matmul(p_cnt[0:X, 0:1], lt[0][:, :], ones[:, :], start=True, stop=False)
            nc.tensor.matmul(p_cnt[0:X, 0:1], lt[1][0:GB, :], ones[0:GB, :], start=False, stop=True).then_inc(pe_s, 1)
            pe.wait_ge(gone, 2)
            nc.tensor.matmul(p_last[0:P, 0:P], k.ones[:, :], diag[:, :], start=True, stop=True).then_inc(pe_s, 1)
            pe.wait_ge(gone, 3)
            for u in range(U):
                for c, f in ((0, df), (256, sf)):
                    at = c
                    for b in range(3):
                        r = f[b].shape[0]
                        last = nc.tensor.transpose(pt[u][0:P, at:at + r],
                                                   f[b][:, :].rearrange("g (p u) -> g p u", u=U)[:, :, u],
                                                   k.ident[0:r, 0:r])
                        at += r
            last.then_inc(pe_s, 1)


class Degrees:

    GROUPS = G

    def __init__(self, nc, k, src, dst):
        self.nc, self.k, self.ends = nc, k, (dst, src)

    def scalar(self, act, g):
        pass

    def room(self, st):
        self.gi = [st.sb(f"gi{a}", [P, J], I32) for a in range(2)]
        self.lo, self.hi = ([st.sb(f"{n}{a}", [P, J], BF16) for a in range(2)] for n in ("lo", "hi"))
        self.lanes = st.sb("lanes", [P, P], BF16)
        self.low_hot, self.high_hot = st.sb("low_hot", [P, 2, U, P], BF16), st.sb("high_hot", [P, 2, U, W], BF16)
        self.zb = st.sb("zb", [P, P], BF16)
        self.grid, self.part = st.sb("grid", [P, J]), st.sb("part", [P, J])
        self.tri = st.sb("tri", [P, P])
        self.room_w = {n: st.sb(n, [P, W]) for n in ("tot", "before", "endf", "startf", "none")}
        self.p_deg, self.p_tot, self.p_tri = (st.ps(n, [128, 512]) for n in ("p_deg", "p_tot", "p_tri"))
        self.loaded, self.cst, self.hot, self.counted, self.degs, self.summed, self.steps = (
            st.sem(n) for n in ("loaded", "cst", "hot", "counted", "degs", "summed", "dsteps"))

    def sync(self, sp):
        for a in range(2):
            sp.dma_start(self.gi[a][:, :], self.ends[a].rearrange("(p j) -> p j", j=J)).then_inc(self.loaded, 16)

    def gpsimd(self, pool):
        pool.memset(self.zb[:, :], 0.0)
        pool.memset(self.tri[:, :], 1.0).then_inc(self.cst, 1)
        pool.wait_ge(self.cst, 1)
        pool.affine_select(out=self.tri[:, :], in_=self.tri[:, :], compare_op=ALU.is_ge, fill=0.0, base=0,
                           pattern=[[1, P]], channel_multiplier=-1).then_inc(self.cst, 1)

    def vector(self, dve):
        k, lo, hi, part, grid = self.k, self.lo, self.hi, self.part, self.grid
        low_hot, high_hot = self.low_hot, self.high_hot
        s = Steps(dve, self.steps)
        s.did(dve.tensor_copy(self.lanes[:, :], k.lane[:, :]))
        dve.wait_ge(self.loaded, 32)
        for a in range(2):
            s.did(dve.tensor_copy(grid[:, :], self.gi[a][:, :]))
            s.link(dve.memset(part[:, :], 0.0))
            for t in range(1, W):
                s.link(dve.scalar_tensor_tensor(part[:, :], grid[:, :], float(P * t), part[:, :], ALU.is_ge, ALU.add))
            s.did(dve.tensor_copy(hi[a][:, :], part[:, :]))
            s.link(dve.scalar_tensor_tensor(lo[a][:, :], part[:, :], float(-P), grid[:, :], ALU.mult, ALU.add))

        def one_hot(i, first=False):
            for a in range(2):
                if not first:
                    dve.wait_ge(self.counted, 2 * i + a - 1)
                dve.tensor_tensor(low_hot[:, a], bcast(self.lanes[:, :], 1, U),
                                  bcast(lo[a][:, bass.ds(i * U, U)], 2, P), ALU.is_equal)
                dve.tensor_tensor(high_hot[:, a], bcast(self.lanes[:, 0:W], 1, U),
                                  bcast(hi[a][:, bass.ds(i * U, U)], 2, W), ALU.is_equal).then_inc(self.hot, 1)

        one_hot(0, True)
        with dve.Fori(1, G) as i:
            one_hot(i)
        dve.wait_ge(self.counted, 2 * G)
        s = Steps(dve, self.degs)
        s.did(dve.tensor_copy(k.indeg[:, :], self.p_deg[0:P, 0:W]))
        s.link(dve.tensor_copy(k.outdeg[:, :], self.p_deg[0:P, 64:64 + W]))
        dve.wait_ge(self.summed, 2)
        tot, before, endf, startf, none = (self.room_w[n] for n in ("tot", "before", "endf", "startf", "none"))
        s.link(dve.tensor_copy(tot[:, :], self.p_tot[0:P, 0:W]))
        s.link(dve.tensor_tensor_scan(before[:, :], k.ones[:, 0:W], tot[:, :], 0.0, ALU.mult, ALU.add))
        s.link(dve.tensor_tensor(before[:, :], before[:, :], tot[:, :], ALU.subtract))
        s.link(dve.tensor_tensor(endf[:, :], self.p_tri[0:P, 0:W], before[:, :], ALU.add))
        s.link(dve.tensor_tensor(startf[:, :], endf[:, :], k.indeg[:, :], ALU.subtract))
        s.link(dve.tensor_scalar(endf[:, :], endf[:, :], -1.0, None, ALU.add))
        s.link(dve.tensor_scalar(none[:, :], k.indeg[:, :], 0.5, None, ALU.is_lt))
        for v, o in ((endf, k.end), (startf, k.start)):
            s.link(dve.tensor_scalar(before[:, :], v[:, :], -1.0, float(E), ALU.mult, ALU.add))
            s.link(dve.tensor_tensor(before[:, :], before[:, :], none[:, :], ALU.mult))
            s.link(dve.tensor_tensor(v[:, :], v[:, :], before[:, :], ALU.add))
            s.link(dve.tensor_copy(o[:, :], v[:, :]))

    def tensor(self, pe):
        nc, k = self.nc, self.k
        pe.wait_ge(self.cst, 2)
        for a in range(2):
            nc.tensor.matmul(self.p_deg[0:P, 64 * a:64 * a + W], self.zb[:, :], self.zb[:, 0:W], start=True,
                             stop=False, skip_group_check=True)
        with pe.Fori(0, G) as i:
            for a in range(2):
                pe.wait_ge(self.hot, 2 * i + a + 1)
                for u in range(U):
                    last = nc.tensor.matmul(self.p_deg[0:P, 64 * a:64 * a + W], self.low_hot[:, a, u, :],
                                            self.high_hot[:, a, u, :], start=False, stop=False, skip_group_check=True)
                last.then_inc(self.counted, 1)
        pe.wait_ge(self.degs, 2)
        nc.tensor.matmul(self.p_tot[0:P, 0:W], k.ones[:, :], k.indeg[:, :], start=True, stop=True).then_inc(self.summed, 1)
        nc.tensor.matmul(self.p_tri[0:P, 0:W], self.tri[:, :], k.indeg[:, :], start=True, stop=True).then_inc(self.summed, 1)


def load(sp, sem, *pairs):
    for o, i in pairs:
        sp.dma_start(o, i, allow_slow_non_contiguous=True).then_inc(sem, 16)
    return 16 * len(pairs)


def stage_windows(nc, k, name, src, parts, size, rhs, out, mid=None, bias=None):
    m = out.shape[2]
    with Stage(nc, name) as st:
        x_w = st.sb("x_w", [P, parts * size])
        x_t = st.sb("x_t", [size, parts, P])
        y_t = st.sb("y_t", [size, parts, P])
        p_t = [st.ps(f"p_t{c}", [128, 512]) for c in range(parts)]
        p_m = [st.ps(f"p_m{c}", [128, 512]) for c in range(parts)]
        p_o = st.ps("p_o", [128, 512])
        picked, turned, copied, mixed, bent, summed, kept = (
            st.sem(n) for n in ("picked", "turned", "copied", "mixed", "bent", "summed", "kept"))
        block = st.block()
        last = y_t if mid else x_t

        @block.tensor
        def _(pe):
            def window(w, first):
                pe.wait_ge(picked, w + 1)
                for c in range(parts):
                    ins = nc.tensor.transpose(p_t[c][0:size, 0:P], x_w[:, size * c:size * (c + 1)], k.ident[0:P, 0:P])
                ins.then_inc(turned, 1)
                pe.wait_ge(copied, w + 1)
                if mid:
                    for c in range(parts):
                        ins = nc.tensor.matmul(p_m[c][0:size, 0:P], mid[:, c, :], x_t[:, c, :], start=True, stop=True)
                    ins.then_inc(mixed, 1)
                    pe.wait_ge(bent, w + 1)
                if not first:
                    pe.wait_ge(kept, w)
                for c in range(parts):
                    ins = nc.tensor.matmul(p_o[0:P, 0:m], last[:, c, :], rhs[:, c, :], start=c == 0, stop=c == parts - 1)
                ins.then_inc(summed, 1)

            window(0, True)
            with pe.Fori(1, W) as w:
                window(w, False)

        @block.scalar
        def _(act):
            with act.Fori(0, W) as w:
                act.wait_ge(turned, w + 1)
                for c in range(parts):
                    ins = nc.scalar.copy(x_t[:, c, :], p_t[c][0:size, 0:P])
                ins.then_inc(copied, 1)
                if mid:
                    act.wait_ge(mixed, w + 1)
                    for c in range(parts):
                        ins = nc.scalar.activation(y_t[:, c, :], p_m[c][0:size, 0:P], ACT.Relu, bias=bias[:, c:c + 1])
                    ins.then_inc(bent, 1)

        @block.vector
        def _(dve):
            def pick(w):
                dve.tensor_copy(x_w[:, :], src[:, bass.ds(w, 1), :].rearrange("p o f -> p (o f)")).then_inc(picked, 1)

            def keep(w):
                dve.wait_ge(summed, w + 1)
                dve.tensor_copy(out[:, bass.ds(w, 1), :].rearrange("p o f -> p (o f)"), p_o[0:P, 0:m]).then_inc(kept, 1)

            pick(0)
            with dve.Fori(0, W - 1) as w:
                dve.wait_ge(turned, w + 1)
                pick(w + 1)
                keep(w)
            keep(W - 1)


def stage_gat_weights(nc, k, t):
    with Stage(nc, "gw") as st:
        w1 = st.sb("w1", [D, H1 * D])
        a1 = st.sb("a1", [D, 2, H1 * D])
        prod = st.sb("prod", [D, 2, H1 * D])
        a2 = st.sb("a2", [128, 2, D])
        prod2 = st.sb("prod2", [128, 2, 2, D])
        got, z, steps = st.sem("got"), st.sem("z"), st.sem("steps")
        block = st.block()

        @block.gpsimd
        def _(pool):
            pool.memset(k.mix1[:, :, :], 0.0).then_inc(z, 1)

        @block.sync
        def _(sp):
            load(sp, got, (w1[:, :], t["L0_gnn_W1"]),
                 (a1[:, 0, :], t["L0_gnn_att_src1"].rearrange("o h c -> o (h c)").broadcast_to([D, H1 * D])),
                 (a1[:, 1, :], t["L0_gnn_att_dst1"].rearrange("o h c -> o (h c)").broadcast_to([D, H1 * D])),
                 (a2[:, 0, :], t["L0_gnn_att_src2"].rearrange("o h c -> o (h c)").broadcast_to([128, D])),
                 (a2[:, 1, :], t["L0_gnn_att_dst2"].rearrange("o h c -> o (h c)").broadcast_to([128, D])),
                 (k.b1[:, :], t["L0_gnn_b1"].rearrange("(c p) -> p c", p=128)),
                 (k.b2[:, :], t["L0_gnn_b2"].unsqueeze(0).broadcast_to([P, D])))
            for c in range(2):
                sp.dma_start(k.w2[:, c, 0:D], t["L0_gnn_W2"][128 * c:128 * (c + 1), :]).then_inc(got, 16)
            sp.wait_ge(z, 1)
            for h in range(H1):
                c, at = h // 4, D * (h % 4)
                sp.dma_start(k.mix1[at:at + D, c, at:at + D], t["L0_gnn_W1"][:, D * h:D * (h + 1)]).then_inc(got, 16)
            sp.wait_ge(got, 16 * 17)

        @block.vector
        def _(dve):
            s = Steps(dve, steps)
            dve.wait_ge(got, 16 * 17)
            s.link(dve.tensor_tensor(prod[:, :, :], bcast(w1[:, :], 1, 2), a1[:, :, :], ALU.mult))
            s.did(dve.tensor_reduce(k.att1[:, 0, :], prod[:, :, :].rearrange("p a (h c) -> p (a h) c", c=D), AX, ALU.add))
            for c in range(2):
                s.link(dve.tensor_tensor(prod2[:, c, :, :], bcast(k.w2[:, c, 0:D], 1, 2), a2[:, :, :], ALU.mult))
                s.did(dve.tensor_reduce(k.w2[:, c, D:D + 2], prod2[:, c, :, :], AX, ALU.add))


def stage_table(nc, k, name, table, cols):
    width = table.shape[1]
    with Stage(nc, name) as st:
        tab = st.sb("tab", [P, W, width])
        made, wrote = st.sem("made"), st.sem("wrote")
        block = st.block()

        @block.vector
        def _(dve):
            at = 0
            for c in cols:
                if c is None:
                    dve.memset(tab[:, :, at:at + 1], 1.0).then_inc(made, 1)
                    at += 1
                else:
                    dve.tensor_copy(tab[:, :, at:at + c.shape[2]], c).then_inc(made, 1)
                    at += c.shape[2]

        @block.sync
        def _(sp):
            sp.wait_ge(made, len(cols))
            sp.dma_start(nodes_view(table), tab[:, :, :]).then_inc(wrote, 16)
            sp.wait_ge(wrote, 16)


def stage_gather(nc, k, name, table, gx, scores=None, n_scores=0, products=False,
                 beside=None):
    width = table.shape[1]
    c = n_scores
    with Stage(nc, name) as st:
        idx = [st.sb(f"idx{r}", [P, U], I32) for r in range(SLOTS)]
        row = [st.sb(f"row{r}", [P, U * width]) for r in range(SLOTS)]
        fx = [st.sb(f"fx{r}", [P, U * K1]) for r in range(SLOTS)]
        sc = [st.sb(f"sc{r}", [P, U * c]) for r in range(SLOTS)] if c else None
        if products:
            xd = [st.sb(f"xd{r}", [P, U * D]) for r in range(SLOTS)]
            prod = [st.sb(f"prod{r}", [P, U * c * D]) for r in range(SLOTS)]
        named, packed, scored, multiplied, gt = (st.sem(n) for n in ("named", "packed", "scored", "multiplied", "gt"))
        fetched = [st.sem(f"fetched{r}") for r in range(SLOTS)]
        wrote = [st.sem(f"wrote{r}") for r in range(SLOTS)]
        at_dst = [st.sem(f"at_dst{r}") for r in range(SLOTS)]
        if beside:
            beside.room(st)
        block = st.block()
        outs = 2 if c else 1

        def rows(r, a, b):
            return row[r][:, :].rearrange("p (u c) -> p u c", c=width)[:, :, a:b]

        @block.scalar
        def _(act):
            def name_edges(g, r):
                nc.scalar.activation(idx[r][:, :], k.srcf[:, bass.ds(g * U, U)], ACT.Copy,
                                     bias=float(MIDDLE)).then_inc(named, 1)

            def trip(i, first):
                for r in range(SLOTS):
                    act.wait_ge(fetched[r], 16 * U * i + 16 * U)
                    if not first:
                        act.wait_ge(wrote[r], 16 * outs * i)
                    if c and not products:
                        nc.scalar.copy(sc[r][:, :].rearrange("p (u c) -> p u c", c=c), rows(r, K1, K1 + c))
                    nc.scalar.copy(fx[r][:, :].rearrange("p (u c) -> p u c", c=K1), rows(r, 0, K1)).then_inc(packed, 1)
                    act.wait_ge(packed, i * SLOTS + r + 1)
                    if products:
                        act.wait_ge(multiplied, i * SLOTS + r + 1)
                    name_edges(i * SLOTS + r + SLOTS, r)
                    if beside:
                        beside.scalar(act, i * SLOTS + r)

            for r in range(SLOTS):
                name_edges(r, r)
            trip(0, True)
            with act.Fori(1, TRIPS_G) as i:
                trip(i, False)
            if beside and beside.GROUPS > G:
                with act.Fori(G, beside.GROUPS) as g:
                    beside.scalar(act, g)

        @block.gpsimd
        def _(pool):
            if beside:
                beside.gpsimd(pool)
            with pool.Fori(0, TRIPS_G) as i:
                for r in range(SLOTS):
                    pool.wait_ge(named, i * SLOTS + r + 1)
                    gate(pool, gt)
                    for u in range(U):
                        pool.indirect_dma_start(
                            out=row[r][:, u * width:(u + 1) * width], out_offset=None, in_=table,
                            in_offset=bass.IndirectOffsetOnAxis(ap=idx[r][:, u:u + 1], axis=0)).then_inc(fetched[r], 16)

        @block.sync
        def _(sp):
            if beside:
                beside.sync(sp)

            def trip(i, first):
                if products:
                    for r in range(SLOTS):
                        if not first:
                            sp.wait_ge(multiplied, i * SLOTS + r + 1 - SLOTS)
                        sp.dma_start(xd[r][:, :], edge_rows(k.xdst, D)[bass.ds(i * SLOTS + r, 1)]
                                     .rearrange("o p c -> (o p) c")).then_inc(at_dst[r], 16)
                for r in range(SLOTS):
                    sp.wait_ge(packed, i * SLOTS + r + 1)
                    sp.dma_start(edge_rows(gx, K1)[bass.ds(i * SLOTS + r, 1)].rearrange("o p c -> (o p) c"),
                                 fx[r][:, :]).then_inc(wrote[r], 16)
                    if c:
                        if products:
                            sp.wait_ge(scored, i * SLOTS + r + 1)
                        sp.dma_start(edge_rows(scores, c)[bass.ds(i * SLOTS + r, 1)].rearrange("o p c -> (o p) c"),
                                     sc[r][:, :]).then_inc(wrote[r], 16)

            trip(0, True)
            with sp.Fori(1, TRIPS_G) as i:
                trip(i, False)
            for r in range(SLOTS):
                sp.wait_ge(wrote[r], 16 * outs * TRIPS_G)

        if beside:
            @block.vector
            def _(dve):
                beside.vector(dve)

            @block.tensor
            def _(pe):
                beside.tensor(pe)

        if products:
            @block.vector
            def _(dve):
                def trip(i, first):
                    for r in range(SLOTS):
                        dve.wait_ge(fetched[r], 16 * U * i + 16 * U)
                        dve.wait_ge(at_dst[r], 16 * i + 16)
                        p4 = prod[r][:, :].rearrange("p (u h f) -> p u h f", h=c, f=D)
                        dve.tensor_tensor(p4, rows(r, K1, K1 + c * D).rearrange("p u (h f) -> p u h f", f=D),
                                          bcast(xd[r][:, :].rearrange("p (u f) -> p u f", f=D), 2, c),
                                          ALU.mult).then_inc(multiplied, 1)
                        dve.wait_ge(multiplied, i * SLOTS + r + 1)
                        if not first:
                            dve.wait_ge(wrote[r], 16 * outs * i)
                        dve.tensor_reduce(sc[r][:, :], prod[r][:, :].rearrange("p (n f) -> p n f", f=D),
                                          AX, ALU.add).then_inc(scored, 1)

                trip(0, True)
                with dve.Fori(1, TRIPS_G) as i:
                    trip(i, False)


def stage_segmax(nc, k, name, scores, c, scanned, amax):
    with Stage(nc, name) as st:
        v = st.sb("v", [P, J, c])
        mask = st.sb("mask", [P, J])
        diag, room = st.sb("diag", [P, 2, P]), st.sb("room", [P, 2, P])
        carry = st.sb("carry", [P, c])
        p_b = [st.ps(f"p_b{n}", [128, 512]) for n in range(2)]
        got, steps, diags, spread, dumped, fetched = (
            st.sem(n) for n in ("got", "steps", "diags", "spread", "dumped", "fetched"))
        done = st.sem("done")
        block = st.block()

        @block.sync
        def _(sp):
            sp.dma_start(v[:, :, :], scores[0:E, :].rearrange("(p j) c -> p j c", j=J)).then_inc(got, 16)
            sp.wait_ge(done, 1)
            sp.dma_start(scanned[0:E, :].rearrange("(p j) c -> p j c", j=J), v[:, :, :]).then_inc(dumped, 16)
            sp.dma_start(scanned[E:E + 1, :], k.negs[0:1, 0:c]).then_inc(dumped, 16)
            sp.wait_ge(dumped, 32)

        @block.vector
        def _(dve):
            s = Steps(dve, steps)
            s.link(dve.tensor_scalar(mask[:, :], k.nstart[:, :], BIG, -BIG, ALU.mult, ALU.add))
            dve.wait_ge(got, 16)
            for h in range(c):
                s.did(dve.tensor_tensor_scan(v[:, :, h], mask[:, :], v[:, :, h], -BIG, ALU.add, ALU.max))
            dve.wait_ge(steps, s.n)
            s.did(dve.tensor_scalar(mask[:, :], k.infirst[:, :], BIG, -BIG, ALU.mult, ALU.add))
            for h in range(c):
                if h >= 2:
                    dve.wait_ge(spread, h - 1)
                dve.tensor_scalar(diag[:, h % 2, :], k.ident[0:P, 0:P], v[:, J - 1, h:h + 1], None,
                                  ALU.mult).then_inc(diags, 1)
                dve.wait_ge(spread, h + 1)
                s.link(dve.tensor_tensor(room[:, h % 2, :], p_b[h % 2][0:P, 0:P], k.earlier[:, :], ALU.add))
                s.did(dve.tensor_reduce(carry[:, h:h + 1], room[:, h % 2, :], AX, ALU.max))
            dve.wait_ge(steps, s.n)
            for h in range(c):
                ins = dve.scalar_tensor_tensor(v[:, :, h], mask[:, :], carry[:, h:h + 1], v[:, :, h],
                                               ALU.add, ALU.max)
            ins.then_inc(done, 1)

        @block.tensor
        def _(pe):
            for h in range(c):
                pe.wait_ge(diags, h + 1)
                nc.tensor.matmul(p_b[h % 2][0:P, 0:P], k.ones[:, :], diag[:, h % 2, :], start=True,
                                 stop=True).then_inc(spread, 1)

        @block.gpsimd
        def _(pool):
            pool.wait_ge(dumped, 32)
            for w in range(W):
                pool.indirect_dma_start(out=amax[:, w, :], out_offset=None, in_=scanned,
                                        in_offset=bass.IndirectOffsetOnAxis(ap=k.end[:, w:w + 1], axis=0)
                                        ).then_inc(fetched, 16)
            pool.wait_ge(fetched, 16 * W)


def stage_spread(nc, k, name, tab, table, start, xdst=None, scores=None, heads=0, weights=None):
    c = tab.shape[2]
    with Stage(nc, name) as st:
        v = st.sb("v", [P, J, c])
        head = st.sb("head", [P, c])
        if scores is not None:
            z = st.sb("z", [P, J, heads])
        wrote, placed, first, got, steps, ready, expd, ends = (
            st.sem(n) for n in ("wrote", "placed", "first", "got", "steps", "ready", "expd", "ends"))
        block = st.block()

        @block.sync
        def _(sp):
            sp.dma_start(nodes_view(table), tab[:, :, :]).then_inc(wrote, 16)
            if scores is not None:
                sp.dma_start(z[:, :, :], scores[0:E, :].rearrange("(p j) c -> p j c", j=J)).then_inc(got, 16)
            sp.wait_ge(placed, 16 * W)
            sp.dma_start(v[:, :, :], start.rearrange("(p j) c -> p j c", j=J)).then_inc(got, 16)
            if xdst is not None:
                sp.wait_ge(ready, 1)
                sp.dma_start(xdst[0:E, :].rearrange("(p j) c -> p j c", j=J), v[:, :, :]).then_inc(ends, 16)
                sp.wait_ge(ends, 16)
            else:
                sp.wait_ge(expd, 1)
                sp.dma_start(weights[0:E, :].rearrange("(p j) c -> p j c", j=J), z[:, :, :]).then_inc(ends, 16)
                sp.wait_ge(ends, 16)

        @block.gpsimd
        def _(pool):
            for w in range(W):
                pool.indirect_dma_start(out=start, in_=tab[:, w, :], in_offset=None,
                                        out_offset=bass.IndirectOffsetOnAxis(ap=k.start[:, w:w + 1], axis=0),
                                        bounds_check=E - 1, oob_is_err=False).then_inc(placed, 16)
            pool.wait_ge(wrote, 16)
            pool.indirect_dma_start(out=head[:, :], out_offset=None, in_=table,
                                    in_offset=bass.IndirectOffsetOnAxis(ap=k.first_i[:, :], axis=0)).then_inc(first, 16)

        @block.vector
        def _(dve):
            s = Steps(dve, steps)
            dve.wait_ge(first, 16)
            dve.wait_ge(got, 16 if scores is None else 32)
            for h in range(c):
                ins = dve.tensor_tensor_scan(v[:, :, h], k.nstart[:, :], v[:, :, h], head[:, h:h + 1],
                                             ALU.mult, ALU.add)
                if h < c - 1 or scores is not None:
                    s.did(ins)
            if scores is None:
                ins.then_inc(ready, 1)
                return
            dve.wait_ge(steps, s.n)
            if c == 2 * heads:
                s.link(dve.tensor_tensor(z[:, :, :], z[:, :, :], v[:, :, 0:heads], ALU.add))
                s.link(dve.scalar_tensor_tensor(z[:, :, :], z[:, :, :], 0.2, z[:, :, :], ALU.mult, ALU.max))
            dve.tensor_tensor(z[:, :, :], z[:, :, :], v[:, :, c - heads:c], ALU.subtract).then_inc(ready, 1)

        if scores is not None:
            @block.scalar
            def _(act):
                act.wait_ge(ready, 1)
                nc.scalar.activation(z[:, :, :], z[:, :, :], ACT.Exp).then_inc(expd, 1)


def stage_sum(nc, k, name, gx, weights, heads, acc):
    m = heads * K1
    with Stage(nc, name) as st:
        fx = [st.sb(f"fx{r}", [P, U * K1]) for r in range(SLOTS)]
        wt = [st.sb(f"wt{r}", [P, U * heads]) for r in range(SLOTS)]
        msg = [st.sb(f"msg{r}", [P, U, heads, K1]) for r in range(SLOTS)]
        hot = [st.sb(f"hot{r}", [P, U, P]) for r in range(SLOTS)]
        p_s = [st.ps(f"p_s{r}", [128, 512]) for r in range(SLOTS)]
        got = [st.sem(f"got{r}") for r in range(SLOTS)]
        made, summed, added, marked = (st.sem(n) for n in ("made", "summed", "added", "marked"))
        block = st.block()

        @block.sync
        def _(sp):
            def trip(i, first):
                for r in range(SLOTS):
                    group = sp.value_load(k.grow[0:1, bass.ds(i * SLOTS + r, 1)], min_val=0, max_val=G - 1)
                    if not first:
                        sp.wait_ge(made, i * SLOTS + r + 1 - SLOTS)
                    for dram, o, c in ((gx, fx, K1), (weights, wt, heads)):
                        sp.dma_start(o[r][:, :], edge_rows(dram, c)[bass.ds(group, 1)]
                                     .rearrange("o p c -> (o p) c")).then_inc(got[r], 16)

            trip(0, True)
            with sp.Fori(1, TRIPS) as i:
                trip(i, False)

        @block.vector
        def _(dve):
            def message(i, r, first):
                dve.wait_ge(got[r], 32 * i + 32)
                if not first:
                    dve.wait_ge(summed, i * SLOTS + r + 1 - SLOTS)
                dve.tensor_tensor(msg[r][:, :, :, :],
                                  bcast(fx[r][:, :].rearrange("p (u f) -> p u f", f=K1), 2, heads),
                                  bcast(wt[r][:, :].rearrange("p (u h) -> p u h", h=heads), 3, K1),
                                  ALU.mult).then_inc(made, 1)
                dve.tensor_tensor(hot[r][:, :, :], bcast(k.lane[:, :], 1, U),
                                  bcast(k.dloc[:, bass.ds((i * SLOTS + r) * U, U)], 2, P), ALU.is_equal
                                  ).then_inc(marked, 1)

            def add(g, r, first):
                w = dve.value_load(k.wrow[0:1, bass.ds(g, 1)], min_val=0, max_val=W - 1)
                dve.wait_ge(summed, g + 1)
                a = acc[:, bass.ds(w, 1), :].rearrange("p o m -> p (o m)")
                dve.wait_ge(added, g + 1)
                dve.tensor_tensor(a, a, p_s[r][0:P, 0:m], ALU.add).then_inc(added, 1)

            dve.memset(acc[:, :, :], 0.0).then_inc(added, 1)
            message(0, 0, True)
            message(0, 1, True)
            add(0, 0, True)
            message(0, 2, True)
            add(1, 1, False)
            with dve.Fori(1, TRIPS) as i:
                for r in range(SLOTS):
                    message(i, r, False)
                    add(i * SLOTS + r - 1, (r - 1) % SLOTS, False)
            add(NG - 1, SLOTS - 1, False)

        @block.tensor
        def _(pe):
            def trip(i, first):
                for r in range(SLOTS):
                    pe.wait_ge(made, i * SLOTS + r + 1)
                    pe.wait_ge(marked, i * SLOTS + r + 1)
                    if not first:
                        pe.wait_ge(added, i * SLOTS + r + 2 - SLOTS)
                    for u in range(U):
                        ins = nc.tensor.matmul(p_s[r][0:P, 0:m], hot[r][:, u, :],
                                               msg[r][:, u, :, :].rearrange("p h f -> p (h f)"),
                                               start=u == 0, stop=u == U - 1)
                    ins.then_inc(summed, 1)

            trip(0, True)
            with pe.Fori(1, TRIPS) as i:
                trip(i, False)


def stage_gat_max(nc, k, name, heads, amax, a_src, a_dst, tab, self_w):
    with Stage(nc, name) as st:
        z = st.sb("z", [P, W, heads])
        steps, ready, done = st.sem("steps"), st.sem("ready"), st.sem("done")
        block = st.block()

        @block.vector
        def _(dve):
            s = Steps(dve, steps)
            m = tab[:, :, heads:2 * heads]
            s.did(dve.tensor_copy(tab[:, :, 0:heads], a_dst))
            s.link(dve.tensor_tensor(m, amax[:, :, :], a_src, ALU.max))
            s.did(dve.tensor_tensor(z[:, :, :], a_src, a_dst, ALU.add))
            s.link(dve.tensor_tensor(m, m, a_dst, ALU.add))
            s.did(dve.scalar_tensor_tensor(z[:, :, :], z[:, :, :], 0.2, z[:, :, :], ALU.mult, ALU.max))
            s.link(dve.scalar_tensor_tensor(m, m, 0.2, m, ALU.mult, ALU.max))
            dve.tensor_tensor(z[:, :, :], z[:, :, :], m, ALU.subtract).then_inc(ready, 1)

        @block.scalar
        def _(act):
            act.wait_ge(ready, 1)
            nc.scalar.activation(self_w[:, :, :], z[:, :, :], ACT.Exp).then_inc(done, 1)
            act.wait_ge(done, 1)


def stage_gat_mean(nc, k, name, heads, acc, self_w, feats, out):
    with Stage(nc, name) as st:
        own = st.sb("own", [P, W, heads, D])
        den = st.sb("den", [P, W, heads])
        steps = st.sem("steps")
        block = st.block()

        @block.vector
        def _(dve):
            s = Steps(dve, steps)
            a = acc[:, :, :].rearrange("p w (h f) -> p w h f", f=K1)
            for h in range(heads):
                s.did(dve.tensor_tensor(own[:, :, h, :], feats, self_w[:, :, h:h + 1].broadcast_to([P, W, D]), ALU.mult))
            s.link(dve.tensor_tensor(den[:, :, :], a[:, :, :, D], self_w[:, :, :], ALU.add))
            s.link(dve.tensor_scalar(den[:, :, :], den[:, :, :], 1e-16, None, ALU.add))
            s.link(dve.reciprocal(den[:, :, :], den[:, :, :]))
            for h in range(heads):
                s.link(dve.tensor_tensor(own[:, :, h, :], own[:, :, h, :], a[:, :, h, 0:D], ALU.add))
                s.did(dve.tensor_tensor(out[:, :, h * D:(h + 1) * D], own[:, :, h, :],
                                        den[:, :, h:h + 1].broadcast_to([P, W, D]), ALU.mult))


def stage_norm(nc, k, name, y, scale=1.0, bias=None, twice=False, out=None):
    with Stage(nc, name) as st:
        sq = st.sb("sq", [P, W, D])
        mean, var = st.sb("mean", [P, W]), st.sb("var", [P, W])
        steps, ready, rooted, fin, wrote = (st.sem(n) for n in ("steps", "ready", "rooted", "fin", "wrote"))
        block = st.block()

        @block.vector
        def _(dve):
            s = Steps(dve, steps)
            if twice:
                s.link(dve.tensor_tensor(y, y, k.x[:, :, :], ALU.add))
            s.link(dve.scalar_tensor_tensor(k.x[:, :, :], y, scale, k.x[:, :, :], ALU.mult, ALU.add))
            if bias is not None:
                s.link(dve.tensor_tensor(k.x[:, :, :], k.x[:, :, :], bcast(bias, 1, W), ALU.add))
            s.link(dve.tensor_reduce(mean[:, :], k.x[:, :, :], AX, ALU.add))
            s.link(dve.tensor_scalar(mean[:, :], mean[:, :], 1.0 / D, None, ALU.mult))
            s.link(dve.tensor_tensor(k.x[:, :, :], k.x[:, :, :], bcast(mean[:, :], 2, D), ALU.subtract))
            s.link(dve.tensor_tensor(sq[:, :, :], k.x[:, :, :], k.x[:, :, :], ALU.mult))
            s.link(dve.tensor_reduce(var[:, :], sq[:, :, :], AX, ALU.add))
            dve.tensor_scalar(var[:, :], var[:, :], 1.0 / D, EPS_LN, ALU.mult, ALU.add).then_inc(ready, 1)
            dve.wait_ge(rooted, 1)
            s.link(dve.reciprocal(var[:, :], var[:, :]))
            dve.tensor_tensor(k.x[:, :, :], k.x[:, :, :], bcast(var[:, :], 2, D), ALU.mult).then_inc(fin, 1)

        @block.scalar
        def _(act):
            act.wait_ge(ready, 1)
            nc.scalar.activation(var[:, :], var[:, :], ACT.Sqrt).then_inc(rooted, 1)

        if out is not None:
            @block.sync
            def _(sp):
                sp.wait_ge(fin, 1)
                sp.dma_start(nodes_view(out), k.x[:, :, :]).then_inc(wrote, 16)
                sp.wait_ge(wrote, 16)


def stage_zero(nc, k):
    with Stage(nc, "zr") as st:
        zeros = st.sb("zeros", [P, J * 16])
        made, wrote = st.sem("made"), st.sem("wrote")
        block = st.block()

        @block.vector
        def _(dve):
            dve.memset(zeros[:, :], 0.0).then_inc(made, 1)

        @block.sync
        def _(sp):
            sp.wait_ge(made, 1)
            n = 0
            for dram, c in ((k.start16, 16), (k.start2, 2), (k.start32, 32), (k.start4, 4)):
                view = dram.rearrange("(p j) c -> p (j c)", j=J)
                for at in range(0, J * c, J * 16):
                    m = min(J * 16, J * c - at)
                    sp.dma_start(view[:, at:at + m], zeros[:, 0:m]).then_inc(wrote, 16)
                    n += 1
            sp.wait_ge(wrote, 16 * n)


def stage_load(nc, k, x):
    with Stage(nc, "ld") as st:
        got = st.sem("got")
        block = st.block()

        @block.sync
        def _(sp):
            sp.dma_start(k.x[:, :, :], nodes_view(x)).then_inc(got, 16)
            sp.wait_ge(got, 16)


def gat(nc, k, t):
    with Stage(nc, "gat") as st:
        hid = st.sb("hid", [P, W, D + 2])
        b2 = st.sb("b2", [P, D])
        with Stage(nc, "gat1") as s1:
            k.mix1 = s1.sb("mix1", [128, 2, 128])
            k.w2, k.b1, k.b2 = s1.sb("w2", [128, 2, D + 2]), s1.sb("b1", [128, 2]), b2
            k.att1 = s1.sb("att1", [D, 1, 2 * H1])
            stage_gat_weights(nc, k, t)
            a1 = s1.sb("a1", [P, W, 2 * H1])
            stage_windows(nc, k, "wa", k.x, 1, D, k.att1, a1)
            stage_table(nc, k, "ta", k.table1, (k.x[:, :, :], None, a1[:, :, 0:H1]))
            stage_gather(nc, k, "ga", k.table1, k.gx, k.sc8, H1, beside=Degrees(nc, k, t["src"], t["dst"]))
            amax, tab, self_w = s1.sb("amax", [P, W, H1]), s1.sb("tab", [P, W, 2 * H1]), s1.sb("self_w", [P, W, H1])
            stage_segmax(nc, k, "sa", k.sc8, H1, k.scan8, amax)
            stage_gat_max(nc, k, "ma", H1, amax, a1[:, :, 0:H1], a1[:, :, H1:2 * H1], tab, self_w)
            stage_spread(nc, k, "ea", tab, k.node16, k.start16, scores=k.sc8, heads=H1, weights=k.wt8)
            acc, mean = s1.sb("acc", [P, W, H1 * K1]), s1.sb("mean", [P, W, H1 * D])
            stage_sum(nc, k, "ua", k.gx, k.wt8, H1, acc)
            stage_gat_mean(nc, k, "na", H1, acc, self_w, k.x[:, :, :], mean)
            stage_windows(nc, k, "wb", mean, 2, 128, k.w2, hid, mid=k.mix1, bias=k.b1)
        with Stage(nc, "gat2") as s2:
            counts = s2.sb("counts", [P, W, N], BF16)
            stage_table(nc, k, "tb", k.table2, (hid[:, :, 0:D], None, hid[:, :, D:D + 1]))
            stage_gather(nc, k, "gb", k.table2, k.gx, k.sc1, H2, beside=Adjacency(nc, k, counts))
            with Stage(nc, "gat3") as s3:
                amax, tab, self_w = s3.sb("amax", [P, W, H2]), s3.sb("tab", [P, W, 2 * H2]), s3.sb("self_w", [P, W, H2])
                stage_segmax(nc, k, "sb", k.sc1, H2, k.scan1, amax)
                stage_gat_max(nc, k, "mb", H2, amax, hid[:, :, D:D + 1], hid[:, :, D + 1:D + 2], tab, self_w)
                stage_spread(nc, k, "eb", tab, k.node2, k.start2, scores=k.sc1, heads=H2, weights=k.wt1)
                acc, mean2 = s3.sb("acc", [P, W, H2 * K1]), s3.sb("mean2", [P, W, D])
                stage_sum(nc, k, "ub", k.gx, k.wt1, H2, acc)
                stage_gat_mean(nc, k, "nb", H2, acc, self_w, hid[:, :, 0:D], mean2)
                stage_norm(nc, k, "l0", mean2[:, :, :], bias=k.b2[:, :], out=k.out if k.layers == 1 else None)
            if k.layers > 1:
                appnp(nc, k, counts)


CHUNK = 4 * P
CHUNKS = -(-N // CHUNK)
RING = 3


class Adjacency:
    GROUPS = NG

    def __init__(self, nc, k, counts):
        self.nc, self.k, self.counts = nc, k, counts

    def room(self, st):
        self.column = st.sb("column", [P, N], mybir.dt.float16)
        self.hot_s = st.sb("hot_s", [P, RING, N], BF16)
        self.hot_d = st.sb("hot_d", [P, RING, P], BF16)
        self.ident, self.lane = st.sb("ident", [P, P], BF16), st.sb("lane", [P, P], BF16)
        self.p_c = [st.ps(f"p_c{c}", [128, 512]) for c in range(CHUNKS)]
        self.cst, self.hot, self.used, self.full, self.kept_a, self.kept_d, self.zeros = (
            st.sem(n) for n in ("cst", "hot", "used", "full", "kept_a", "kept_d", "zeros"))

    def bank(self, w, c):
        n = min(CHUNK, N - c * CHUNK)
        return (self.counts[:, bass.ds(w, 1), c * CHUNK:c * CHUNK + n].rearrange("p o n -> p (o n)"),
                self.p_c[c][0:P, 0:n])

    def sync(self, sp):
        pass

    def gpsimd(self, pool):
        pool.iota(self.column[:, :], [[1, N]], base=-MIDDLE, channel_multiplier=0,
                  allow_small_or_imprecise_dtypes=True).then_inc(self.cst, 1)
        pool.memset(self.counts[:, W // 2:W, :], 0.0).then_inc(self.zeros, 1)

    def scalar(self, act, g):
        w = act.value_load(self.k.wrow[0:1, bass.ds(g, 1)], min_val=0, max_val=W - 1)
        for c in range(0, CHUNKS, 2):
            act.wait_ge(self.full, g * CHUNKS + c + 1)
            a, p = self.bank(w, c)
            self.nc.scalar.copy(a, p).then_inc(self.kept_a, 1)

    def vector(self, dve):
        k, hot_s, hot_d = self.k, self.hot_s, self.hot_d

        def one_hot(q, slot, first=False):
            if not first:
                dve.wait_ge(self.used, q - RING + 1)
            dve.tensor_scalar(hot_s[:, slot, :], self.column[:, :], k.srcf[:, bass.ds(q, 1)], None, ALU.is_equal)
            dve.tensor_scalar(hot_d[:, slot, :], self.lane[:, :], k.dloc[:, bass.ds(q, 1)], None,
                              ALU.is_equal).then_inc(self.hot, 1)

        def keep(g):
            w = dve.value_load(k.wrow[0:1, bass.ds(g, 1)], min_val=0, max_val=W - 1)
            for c in range(1, CHUNKS, 2):
                dve.wait_ge(self.full, g * CHUNKS + c + 1)
                a, p = self.bank(w, c)
                dve.tensor_copy(a, p).then_inc(self.kept_d, 1)

        def group(g, r, start):
            for q in range(2, U + 2):
                one_hot(g * U + q, (r * U + q) % RING, start and q < RING)
            keep(g)

        dve.tensor_copy(self.ident[:, :], k.ident[0:P, 0:P]).then_inc(self.cst, 1)
        dve.tensor_copy(self.lane[:, :], k.lane[:, :]).then_inc(self.cst, 1)
        dve.wait_ge(self.cst, 3)
        one_hot(0, 0, True)
        one_hot(1, 1, True)
        dve.memset(self.counts[:, 0:W // 2, :], 0.0).then_inc(self.zeros, 1)
        for r in range(SLOTS):
            group(r, r, r == 0)
        with dve.Fori(1, TRIPS) as i:
            for r in range(SLOTS):
                group(i * SLOTS + r, r, False)

    def tensor(self, pe):
        evens, odds = (CHUNKS + 1) // 2, CHUNKS // 2

        def group(g, r, first):
            w = pe.value_load(self.k.wrow[0:1, bass.ds(g, 1)], min_val=0, max_val=W - 1)
            for u in range(U):
                slot = (r * U + u) % RING
                pe.wait_ge(self.hot, g * U + u + 1)
                for c in range(CHUNKS):
                    n = min(CHUNK, N - c * CHUNK)
                    if u == 0 and not first:
                        if c % 2 == 0:
                            pe.wait_ge(self.kept_a, (g - 1) * evens + c // 2 + 1)
                        else:
                            pe.wait_ge(self.kept_d, (g - 1) * odds + c // 2 + 1)
                    ins = self.nc.tensor.matmul(self.p_c[c][0:P, 0:n], self.hot_d[:, slot, :],
                                                self.hot_s[:, slot, c * CHUNK:c * CHUNK + n], start=u == 0, stop=False)
                ins.then_inc(self.used, 1)
            for c in range(CHUNKS):
                a, p = self.bank(w, c)
                self.nc.tensor.matmul(p, self.ident[:, :], a, start=False, stop=True).then_inc(self.full, 1)

        pe.wait_ge(self.cst, 3)
        pe.wait_ge(self.zeros, 2)
        for r in range(SLOTS):
            group(r, r, r == 0)
        with pe.Fori(1, TRIPS) as i:
            for r in range(SLOTS):
                group(i * SLOTS + r, r, False)


def stage_turn(nc, k, counts):
    EVEN = P + 1
    ROOM = [(0, 7), (7, 13), (13, 19), (19, 25)]
    with Stage(nc, "tu") as st:
        ident = st.sb("ident", [P, P], BF16)
        p_t = [st.ps(f"p_t{n}", [128, 1024], BF16) for n in range(4)]
        cst, turned, kept_a, kept_d = (st.sem(n) for n in ("cst", "turned", "kept_a", "kept_d"))
        block = st.block()

        def keep(copy, w, n, sem):
            a, b = ROOM[n]
            copy(counts[:, bass.ds(w, 1), a * P:b * P].rearrange("p o (n e) -> p (o n) e", e=P),
                 p_t[n][0:P, 0:(b - a) * EVEN].rearrange("p (n e) -> p n e", e=EVEN)[:, :, 0:P]).then_inc(sem, 1)

        @block.tensor
        def _(pe):
            pe.wait_ge(cst, 1)

            def window(w, first):
                for n, (a, b) in enumerate(ROOM):
                    if not first and n == 0:
                        pe.wait_ge(kept_a, 2 * w)
                        pe.wait_ge(kept_d, 2 * w)
                    for c in range(a, b):
                        ins = nc.tensor.transpose(p_t[n][0:P, (c - a) * EVEN:(c - a) * EVEN + P],
                                                  counts[:, bass.ds(w, 1), c * P:(c + 1) * P]
                                                  .rearrange("p o n -> p (o n)"), ident[:, :])
                    ins.then_inc(turned, 1)

            window(0, True)
            with pe.Fori(1, W) as w:
                window(w, False)

        @block.vector
        def _(dve):
            dve.tensor_copy(ident[:, :], k.ident[0:P, 0:P]).then_inc(cst, 1)
            with dve.Fori(0, W) as w:
                for n in (0, 2):
                    dve.wait_ge(turned, w * 4 + n + 1)
                    keep(dve.tensor_copy, w, n, kept_d)

        @block.scalar
        def _(act):
            with act.Fori(0, W) as w:
                for n in (1, 3):
                    act.wait_ge(turned, w * 4 + n + 1)
                    keep(nc.scalar.copy, w, n, kept_a)


def stage_appnp(nc, k, counts, out):
    WB = 5
    BANKS = W // WB
    with Stage(nc, "ap") as st:
        sn, dn = st.sb("sn", [P, W]), st.sb("dn", [P, W])
        x0 = st.sb("x0", [P, W, D])
        parts = st.sb("parts", [P, 2, W, 3, D], BF16)
        rest = st.sb("rest", [P, W, D])
        p_f = [st.ps(f"p_f{b}", [128, 512]) for b in range(BANKS)]
        steps, ready, rooted, split, summed, own = (
            st.sem(n) for n in ("steps", "ready", "rooted", "split", "summed", "own"))
        block = st.block()

        @block.scalar
        def _(act):
            act.wait_ge(ready, 2)
            nc.scalar.activation(sn[:, :], sn[:, :], ACT.Sqrt)
            nc.scalar.activation(dn[:, :], dn[:, :], ACT.Sqrt).then_inc(rooted, 1)

        @block.vector
        def _(dve):
            LINKS = 8

            def scale_and_split(at, w0, n, chain):
                f, rs = out[:, w0:w0 + n, :], rest[:, w0:w0 + n, :]
                hi, mid, lo = (parts[:, at, w0:w0 + n, j, :] for j in range(3))
                chain.link(dve.tensor_tensor(rs, f, bcast(sn[:, w0:w0 + n], 2, D), ALU.mult))
                chain.link(dve.tensor_copy(hi, rs))
                chain.link(dve.tensor_tensor(rs, rs, hi, ALU.subtract))
                chain.link(dve.tensor_copy(mid, rs))
                chain.link(dve.tensor_tensor(rs, rs, mid, ALU.subtract))
                dve.tensor_copy(lo, rs).then_inc(split, 1)

            dve.tensor_scalar(sn[:, :], k.outdeg[:, :], 1.0, None, ALU.max).then_inc(ready, 1)
            dve.tensor_scalar(dn[:, :], k.indeg[:, :], 1.0, None, ALU.max).then_inc(ready, 1)
            dve.wait_ge(rooted, 1)
            s = Steps(dve, steps)
            s.did(dve.reciprocal(sn[:, :], sn[:, :]))
            s.link(dve.reciprocal(dn[:, :], dn[:, :]))
            s.did(dve.tensor_scalar(dn[:, :], dn[:, :], 1.0 - ALPHA, None, ALU.mult))
            s.did(dve.tensor_scalar(x0[:, :, :], k.x[:, :, :], ALPHA, None, ALU.mult))
            s.link(dve.tensor_copy(out[:, :, :], k.x[:, :, :]))
            for b in range(BANKS):
                scale_and_split(0, b * WB, WB, s)
            with dve.Fori(0, STEPS_APPNP // 2) as i:
                for half in range(2):
                    for b in range(BANKS):
                        w0 = b * WB
                        step = (i * 2 + half) * BANKS + b
                        chain = Steps(dve, own, step * LINKS)
                        dve.wait_ge(summed, step + 1)
                        f = out[:, w0:w0 + WB, :]
                        chain.link(dve.tensor_reduce(
                            f, p_f[b][0:P, 0:WB * 3 * D].rearrange("p (w j f) -> p w f j", w=WB, j=3), AX, ALU.add))
                        chain.link(dve.tensor_tensor(f, f, bcast(dn[:, w0:w0 + WB], 2, D), ALU.mult))
                        chain.link(dve.tensor_tensor(f, f, x0[:, w0:w0 + WB, :], ALU.add))
                        scale_and_split(1 - half, w0, WB, chain)

        @block.tensor
        def _(pe):
            def bank(i, half, b):
                for w in range(b * WB, (b + 1) * WB):
                    for c in range(W):
                        at = (w - b * WB) * 3 * D
                        ins = nc.tensor.matmul(p_f[b][0:P, at:at + 3 * D], counts[:, w, c * P:(c + 1) * P],
                                               parts[:, half, c, :, :].rearrange("p j f -> p (j f)"),
                                               start=c == 0, stop=c == W - 1)
                ins.then_inc(summed, 1)

            with pe.Fori(0, STEPS_APPNP // 2) as i:
                for half in range(2):
                    pe.wait_ge(split, (i * 2 + half) * BANKS + BANKS)
                    for b in range(BANKS):
                        bank(i, half, b)


def appnp(nc, k, counts):
    with Stage(nc, "pp") as st:
        stage_turn(nc, k, counts)
        f = st.sb("f", [P, W, D])
        stage_appnp(nc, k, counts, f)
        stage_norm(nc, k, "l1", f[:, :, :], out=k.out if k.layers == 2 else None)


def stage_attention_weights(nc, k, t, keys, values):
    with Stage(nc, "aw") as st:
        raw = st.sb("raw", [D, 3, HQ, D])
        turned = st.sb("turned", [D, 3, HQ * D])
        wout = st.sb("wout", [D, D])
        p_t, p_k, p_v = (st.ps(n, [128, 512]) for n in ("p_t", "p_k", "p_v"))
        got, flipped, copied, done = (st.sem(n) for n in ("got", "flipped", "copied", "done"))
        block = st.block()

        @block.sync
        def _(sp):
            for n, a in enumerate(("L2_gnn_Wq", "L2_gnn_Wk", "L2_gnn_Wv")):
                sp.dma_start(raw[:, n, :, :], t[a].rearrange("h f o -> f h o")).then_inc(got, 16)
            sp.dma_start(wout[:, :], t["L2_gnn_Wout"]).then_inc(got, 16)

        @block.tensor
        def _(pe):
            pe.wait_ge(got, 64)
            for n in range(3):
                for h in range(HQ):
                    at = (n * HQ + h) * D
                    ins = nc.tensor.transpose(p_t[0:D, at:at + D], raw[:, n, h, :], k.ident[0:D, 0:D])
            ins.then_inc(flipped, 1)
            pe.wait_ge(copied, 1)
            for h in range(HQ):
                ins = nc.tensor.matmul(p_k[0:D, h * D:(h + 1) * D], turned[:, 1, h * D:(h + 1) * D],
                                       turned[:, 0, h * D:(h + 1) * D], start=True, stop=True)
            ins.then_inc(flipped, 1)
            nc.tensor.matmul(p_v[0:HQ * D, 0:D], turned[:, 2, :], wout[:, :], start=True, stop=True).then_inc(flipped, 1)

        @block.vector
        def _(dve):
            dve.wait_ge(flipped, 1)
            dve.tensor_copy(turned[:, :, :], p_t[0:D, 0:3 * HQ * D].rearrange("p (n c) -> p n c", n=3)).then_inc(copied, 1)
            dve.wait_ge(flipped, 3)
            dve.tensor_scalar(keys[:, 0, :], p_k[0:D, 0:HQ * D], float(D) ** -0.5, None, ALU.mult)
            dve.tensor_scalar(values[:, 0, :], p_v[0:HQ * D, 0:D], 1.0 / HQ, None, ALU.mult).then_inc(done, 1)


def stage_divide(nc, k, acc, mean):
    with Stage(nc, "dv") as st:
        den, none = st.sb("den", [P, W, HQ]), st.sb("none", [P, W, HQ])
        steps = st.sem("steps")
        block = st.block()

        @block.vector
        def _(dve):
            s = Steps(dve, steps)
            a = acc[:, :, :].rearrange("p w (h f) -> p w h f", f=K1)
            s.link(dve.tensor_scalar(none[:, :, :], a[:, :, :, D], 0.0, None, ALU.is_le))
            s.link(dve.tensor_tensor(den[:, :, :], a[:, :, :, D], none[:, :, :], ALU.add))
            s.link(dve.reciprocal(den[:, :, :], den[:, :, :]))
            for h in range(HQ):
                s.did(dve.tensor_tensor(mean[:, :, h * D:(h + 1) * D], a[:, :, h, 0:D],
                                        den[:, :, h:h + 1].broadcast_to([P, W, D]), ALU.mult))


def attention(nc, k, t):
    with Stage(nc, "at") as st:
        keys, values = st.sb("keys", [D, 1, HQ * D]), st.sb("values", [HQ * D, 1, D])
        stage_attention_weights(nc, k, t, keys, values)
        with Stage(nc, "at1") as s1:
            y = s1.sb("y", [P, W, HQ * D])
            stage_windows(nc, k, "wk", k.x, 1, D, keys, y)
            stage_table(nc, k, "tk", k.table4, (k.x[:, :, :], None, y[:, :, :]))
        stage_spread(nc, k, "xd", k.x, k.node32, k.start32, xdst=k.xdst)
        stage_gather(nc, k, "gk", k.table4, k.gx, k.sc4, HQ, products=True)
        amax = st.sb("amax", [P, W, HQ])
        stage_segmax(nc, k, "sk", k.sc4, HQ, k.scan4, amax)
        stage_spread(nc, k, "ek", amax, k.node4, k.start4, scores=k.sc4, heads=HQ, weights=k.wt4)
        acc, mean, y = st.sb("acc", [P, W, HQ * K1]), st.sb("mean", [P, W, HQ * D]), st.sb("y", [P, W, D])
        stage_sum(nc, k, "uk", k.gx, k.wt4, HQ, acc)
        stage_divide(nc, k, acc, mean)
        stage_windows(nc, k, "wv", mean, 1, HQ * D, values, y)
        stage_norm(nc, k, "l2", y[:, :, :], twice=True, out=k.out if k.layers == 3 else None)


INV_SQRT3 = float(1.0 / np.sqrt(3.0))
A_SCALAR = float(np.sqrt(1.0 / 128.0))
A_VECTOR = float(np.sqrt(3.0 / 128.0))
PARTS_EDGE = (0, 0, 0, 1, 1, 2)
PARTS_FC = (0, 1, 2, 0, 1, 0)
ROWS = 6 * BASIS


def split(link, dve, value, rest, parts):
    link(dve.tensor_copy(parts[0], value))
    link(dve.tensor_tensor(rest, value, parts[0], ALU.subtract))
    link(dve.tensor_copy(parts[1], rest))
    link(dve.tensor_tensor(rest, rest, parts[1], ALU.subtract))
    link(dve.tensor_copy(parts[2], rest))


def stage_attributes(nc, k, ea4, ea8):
    PIECE = 33
    with Stage(nc, "et") as st:
        e8 = [st.sb(f"e8{n}", [P, PIECE, U * BASIS]) for n in range(2)]
        e4 = [st.sb(f"e4{n}", [P, PIECE, U * 4]) for n in range(2)]
        rest = st.sb("rest", [P, PIECE, U * BASIS])
        eas = [st.sb(f"eas{n}", [P, PIECE, U, 6, BASIS], BF16) for n in range(2)]
        eav = [st.sb(f"eav{n}", [P, PIECE, U, 8]) for n in range(2)]
        got = [st.sem(f"got{n}") for n in range(2)]
        wrote = [st.sem(f"wrote{n}") for n in range(2)]
        made, steps = st.sem("made"), st.sem("steps")
        block = st.block()
        n_pieces = G // PIECE

        @block.sync
        def _(sp):
            for n in range(n_pieces):
                if n >= 2:
                    sp.wait_ge(made, n - 1)
                part = slice(n * PIECE, (n + 1) * PIECE)
                sp.dma_start(e8[n % 2][:, :, :], edge_rows(ea8, BASIS)[part].rearrange("g p c -> p g c")).then_inc(got[n % 2], 16)
                sp.dma_start(e4[n % 2][:, :, :], edge_rows(ea4, 4)[part].rearrange("g p c -> p g c")).then_inc(got[n % 2], 16)

        @block.scalar
        def _(act):
            for n in range(n_pieces):
                act.wait_ge(made, n + 1)
                part = slice(n * PIECE, (n + 1) * PIECE)
                act.dma_start(k.eas[part].rearrange("g p c -> p g c"),
                              eas[n % 2][:, :, :, :, :].rearrange("p g u j b -> p g (u j b)")).then_inc(wrote[n % 2], 16)
                act.dma_start(k.eav[part].rearrange("g p c -> p g c"),
                              eav[n % 2][:, :, :, :].rearrange("p g u c -> p g (u c)")).then_inc(wrote[n % 2], 16)
            for n in range(2):
                act.wait_ge(wrote[n], 32 * ((n_pieces + 1 - n) // 2))

        @block.vector
        def _(dve):
            s = Steps(dve, steps)
            for n in range(n_pieces):
                dve.wait_ge(got[n % 2], 32 * (n // 2 + 1))
                if n >= 2:
                    dve.wait_ge(wrote[n % 2], 32 * (n // 2))
                o = eas[n % 2][:, :, :, :, :].rearrange("p g u j b -> p (g u) j b")
                v = e8[n % 2][:, :, :].rearrange("p g (u b) -> p (g u) b", b=BASIS)
                r = rest[:, :, :].rearrange("p g (u b) -> p (g u) b", b=BASIS)
                split(s.link, dve, v, r, (o[:, :, 0, :], o[:, :, 3, :], o[:, :, 5, :]))
                s.did(dve.tensor_copy(o[:, :, 1:3, :], bcast(o[:, :, 0, :], 2, 2)))
                s.did(dve.tensor_copy(o[:, :, 4, :], o[:, :, 3, :]))
                e = e4[n % 2][:, :, :].rearrange("p g (u c) -> p (g u) c", c=4)
                q = eav[n % 2][:, :, :, :].rearrange("p g u c -> p (g u) c")
                s.did(dve.tensor_scalar(q[:, :, 0:1], e[:, :, 0:1], A_SCALAR, None, ALU.mult))
                s.did(dve.tensor_scalar(q[:, :, 1:2], e[:, :, 0:1], A_VECTOR * INV_SQRT3, None, ALU.mult))
                s.did(dve.tensor_scalar(q[:, :, 2:5], e[:, :, 1:4], A_SCALAR * INV_SQRT3, None, ALU.mult))
                dve.tensor_scalar(q[:, :, 5:8], e[:, :, 1:4], A_VECTOR * INV_SQRT3, None, ALU.mult).then_inc(made, 1)


def stage_conv_weights(nc, k, t, fc1, fc2):
    with Stage(nc, "cw") as st:
        raw, rest = st.sb("raw", [BASIS, HID]), st.sb("rest", [BASIS, HID])
        parts = st.sb("parts", [BASIS, 3, HID], BF16)
        got, z, steps, made, placed = (st.sem(n) for n in ("got", "z", "steps", "made", "placed"))
        block = st.block()

        @block.gpsimd
        def _(pool):
            pool.memset(fc1[:, :, :, :], 0.0).then_inc(z, 1)

        @block.sync
        def _(sp):
            sp.dma_start(raw[:, :], t["L3_gnn_fc_w1"]).then_inc(got, 16)
            sp.dma_start(fc2[:, :, :], t["L3_gnn_fc_w2"].rearrange("(c h) n -> h c n", c=2)).then_inc(got, 16)
            sp.wait_ge(z, 1)
            sp.wait_ge(made, 1)
            for u in range(2):
                for j, part in enumerate(PARTS_FC):
                    at = u * ROWS + j * BASIS
                    sp.dma_start(fc1[at:at + BASIS, u, :, :], parts[:, part, :].rearrange("b (c h) -> b c h", c=2)
                                 ).then_inc(placed, 16)
            sp.wait_ge(placed, 16 * 12)

        @block.vector
        def _(dve):
            s = Steps(dve, steps)
            dve.wait_ge(got, 32)
            s.did(dve.tensor_scalar(fc2[:, :, :], fc2[:, :, :], float(np.sqrt(2.0)) * float(HID) ** -0.5, None, ALU.mult))
            s.link(dve.tensor_scalar(raw[:, :], raw[:, :], float(BASIS) ** -0.5, None, ALU.mult))
            split(s.link, dve, raw[:, :], rest[:, :], [parts[:, j, :] for j in range(3)])
            dve.memset(rest[:, :], 0.0).then_inc(made, 1)


def stage_conv(nc, k, fc1, fc2, acc):
    PAIR = [(0, 2), (2, 4), (4, 5)]
    BANKS_H = [(0, 4), (4, 8), (8, 10)]
    KF = 3 * MUL
    EVEN = P + 1
    with Stage(nc, "cv") as st:
        idx = [st.sb(f"idx{r}", [P, U], I32) for r in range(SLOTS)]
        row = [st.sb(f"row{r}", [P, U * D]) for r in range(SLOTS)]
        vecs = [st.sb(f"vecs{r}", [P, U * 8]) for r in range(SLOTS)]
        scal = [st.sb(f"scal{r}", [P, U * ROWS], BF16) for r in range(SLOTS)]
        scal_t = [st.sb(f"scal_t{r}", [2 * ROWS, 3, EVEN], BF16) for r in range(SLOTS)]
        ident = st.sb("ident", [P, P], BF16)
        hid = [st.sb(f"hid{r}", [128, 2 * U, P]) for r in range(SLOTS)]
        dot = [st.sb(f"dot{r}", [P, U, MUL, 3]) for r in range(SLOTS)]
        fac = [st.sb(f"fac{r}", [P, U, KF]) for r in range(SLOTS)]
        vec = [st.sb(f"vec{r}", [P, U, 3, MUL]) for r in range(SLOTS)]
        prod = st.sb("prod", [P, U, MUL, 2 * KF])
        red = st.sb("red", [P, U, MUL, 4])
        outer = st.sb("outer", [P, U, MUL, 3])
        msg = st.sb("msg", [P, G * U, D])
        hot, far = [st.sb(f"hot{r}", [P, U, P]) for r in range(SLOTS)], st.sb("far", [P, U, P])
        p_t, p_s = st.ps("p_t", [128, 1024], BF16), st.ps("p_s", [128, 512])
        p_h = [st.ps(f"p_h{n}", [128, 512]) for n in range(3)]
        p_w = [st.ps(f"p_w{n}", [128, 512]) for n in range(3)]
        (named, ready, turned, flat, hidden, bent, weighed, read, made, summed, added, own, cst, copied, apart,
         marked, gt) = (st.sem(n) for n in ("named", "ready", "turned", "flat", "hidden", "bent", "weighed", "read", "made",
                                    "summed", "added", "own", "cst", "copied", "apart", "marked",
                                    "gt"))
        fetched = [st.sem(f"fetched{r}") for r in range(SLOTS)]
        got, got_s = ([st.sem(f"{n}{r}") for r in range(SLOTS)] for n in ("got", "got_s"))
        block = st.block()

        @block.sync
        def _(sp):
            def fetch(dram, o, r, g, sem):
                sp.dma_start(o[r][:, :], dram[bass.ds(g, 1)].rearrange("o p c -> (o p) c")).then_inc(sem[r], 16)

            def trip(i, first, last=False):
                for r in range(SLOTS):
                    g = i * SLOTS + r
                    if not first:
                        sp.wait_ge(made, g + 1 - SLOTS)
                    fetch(k.eav, vecs, r, g, got)
                    if not last:
                        sp.wait_ge(turned, g + 1)
                        fetch(k.eas, scal, r, g + SLOTS, got_s)

            for r in range(SLOTS):
                fetch(k.eas, scal, r, r, got_s)
            trip(0, True)
            with sp.Fori(1, TRIPS_G - 1) as i:
                trip(i, False)
            trip(TRIPS_G - 1, False, True)

        @block.gpsimd
        def _(pool):
            with pool.Fori(0, TRIPS_G) as i:
                for r in range(SLOTS):
                    pool.wait_ge(named, i * SLOTS + r + 1)
                    gate(pool, gt)
                    for u in range(U):
                        pool.indirect_dma_start(
                            out=row[r][:, u * D:(u + 1) * D], out_offset=None, in_=k.table3,
                            in_offset=bass.IndirectOffsetOnAxis(ap=idx[r][:, u:u + 1], axis=0)).then_inc(fetched[r], 16)

        @block.scalar
        def _(act):
            def name_edges(g, r):
                nc.scalar.activation(idx[r][:, :], k.srcf[:, bass.ds(g * U, U)], ACT.Copy,
                                     bias=float(MIDDLE)).then_inc(named, 1)

            def mark(j, r, first=False):
                if not first:
                    act.wait_ge(summed, j - SLOTS + 1)
                if not first or r > 0:
                    act.wait_ge(marked, j)
                for u in range(U):
                    ins = nc.scalar.activation(far[:, u, :], k.lane[:, :], ACT.Abs, scale=-1.0,
                                               bias=k.dloc[:, bass.ds(j * U + u, 1)])
                ins.then_inc(apart, 1)
                act.wait_ge(apart, j + 1)
                nc.scalar.activation(hot[r][:, :, :], far[:, :, :], ACT.Relu, scale=-1.0, bias=k.ones[:, 0:1]
                                     ).then_inc(marked, 1)

            def units(i, r, first):
                g = i * SLOTS + r
                act.wait_ge(turned, g + 1)
                nc.scalar.copy(scal_t[r][:, 0:2, 0:P], p_t[0:2 * ROWS, 0:2 * EVEN]
                               .rearrange("k (n e) -> k n e", e=EVEN)[:, :, 0:P])
                nc.scalar.copy(scal_t[r][0:ROWS, 2, 0:P], p_t[0:ROWS, 2 * EVEN:2 * EVEN + P]).then_inc(flat, 1)
                if not first:
                    act.wait_ge(weighed, (g - SLOTS) * 3 + 3)
                for n, (a, b) in enumerate(BANKS_H):
                    act.wait_ge(hidden, g * 3 + n + 1)
                    nc.scalar.activation(hid[r][:, a:b, :], p_h[n][:, 0:(b - a) * P]
                                         .rearrange("p (n e) -> p n e", e=P), ACT.Relu).then_inc(bent, 1)
                act.wait_ge(fetched[r], 16 * U * i + 16 * U)
                if not first:
                    act.wait_ge(read, (g - SLOTS) * 3 + 3)
                nc.scalar.copy(fac[r][:, :, 2 * MUL:KF], row[r][:, :].rearrange("p (u c) -> p u c", c=D)[:, :, 0:MUL]
                               ).then_inc(copied, 1)

            def trip(i, first, last=False):
                for r in range(SLOTS):
                    g = i * SLOTS + r
                    if r < SLOTS - 1:
                        units(i, r + 1, first)
                    elif not last:
                        units(i + 1, 0, False)
                    mark(g, r, first)
                    act.wait_ge(ready, g + 1)
                    act.wait_ge(copied, g + 1)
                    name_edges(g + SLOTS, r)

            for r in range(SLOTS):
                name_edges(r, r)
            units(0, 0, True)
            trip(0, True)
            with act.Fori(1, TRIPS_G - 1) as i:
                trip(i, False)
            trip(TRIPS_G - 1, False, True)
            with act.Fori(TRIPS_G, TRIPS) as i:
                for r in range(SLOTS):
                    mark(i * SLOTS + r, r)

        @block.tensor
        def _(pe):
            pe.wait_ge(cst, 1)
            gate(pe, gt)

            def hide(i, r, g, first):
                pe.wait_ge(got_s[r], 16 * i + 16)
                gate(pe, gt)
                if not first:
                    pe.wait_ge(flat, g)
                    gate(pe, gt)
                for n in range(3):
                    rows = 2 * ROWS if n < 2 else ROWS
                    ins = nc.tensor.transpose(p_t[0:rows, n * EVEN:n * EVEN + P],
                                              scal[r][:, n * 2 * ROWS:n * 2 * ROWS + rows], ident[:, :])
                ins.then_inc(turned, 1)

            def hide2(g, r, first):
                pe.wait_ge(flat, g + 1)
                for n, (a, b) in enumerate(BANKS_H):
                    rows = 2 * ROWS if n < 2 else ROWS
                    if not first:
                        pe.wait_ge(bent, (g - 1) * 3 + n + 1)
                    for m in range(a, b):
                        ins = nc.tensor.matmul(p_h[n][:, (m - a) * P:(m - a + 1) * P],
                                               fc1[0:rows, (m // 2) % 2, m % 2, :], scal_t[r][0:rows, n, 0:P],
                                               start=True, stop=True)
                    ins.then_inc(hidden, 1)

            def look(j):
                return pe.value_load(k.grow[0:1, bass.ds(j, 1)], min_val=0, max_val=G - 1)

            def weigh(g, r, first, j=None):
                for n, (a, b) in enumerate(PAIR):
                    if n == len(PAIR) - 1 and j is not None:
                        group = look(j)
                    if not first:
                        pe.wait_ge(read, (g - 1) * 3 + n + 1)
                    pe.wait_ge(bent, g * 3 + n + 1)
                    for u in range(a, b):
                        for c in range(2):
                            ins = nc.tensor.matmul(p_w[n][0:P, (u - a) * HID:(u - a + 1) * HID],
                                                   hid[r][:, 2 * u + c, :], fc2[:, c, :], start=c == 0, stop=c == 1)
                    ins.then_inc(weighed, 1)
                return group if j is not None else None

            def gather_up(j, r, first, group):
                pe.wait_ge(marked, j + 1)
                if not first:
                    pe.wait_ge(added, j + 1)
                for u in range(U):
                    ins = nc.tensor.matmul(p_s[0:P, 0:D], hot[r][:, u, :],
                                           msg[:, bass.ds(group * U + u, 1), :].rearrange("p o d -> p (o d)"),
                                           start=u == 0, stop=u == U - 1)
                ins.then_inc(summed, 1)

            def trip(i, first, last=False):
                for r in range(SLOTS):
                    g = i * SLOTS + r
                    more, most = divmod(r + 1, SLOTS), divmod(r + 2, SLOTS)
                    if not last or more[0] == 0:
                        hide2(g + 1, more[1], False)
                    if not last or most[0] == 0:
                        hide(i + most[0], most[1], g + 2, False)
                    if first and r == 0:
                        weigh(g, r, True)
                        continue
                    group = weigh(g, r, False, g - 1)
                    pe.wait_ge(made, g)
                    gather_up(g - 1, (r - 1) % SLOTS, first and r == 1, group)

            hide(0, 0, 0, True)
            hide2(0, 0, True)
            hide(0, 1, 1, False)
            trip(0, True)
            with pe.Fori(1, TRIPS_G - 1) as i:
                trip(i, False)
            trip(TRIPS_G - 1, False, True)
            pe.wait_ge(made, G)
            gather_up(G - 1, SLOTS - 1, False, look(G - 1))
            with pe.Fori(TRIPS_G, TRIPS) as i:
                for r in range(SLOTS):
                    gather_up(i * SLOTS + r, r, False, look(i * SLOTS + r))

        @block.vector
        def _(dve):
            OPS = 6

            def window(j):
                return dve.value_load(k.wrow[0:1, bass.ds(j, 1)], min_val=0, max_val=W - 1)

            def contract(i, r, g, first, j=None):
                s = Steps(dve, own, g * OPS)
                rw = row[r][:, :].rearrange("p (u c) -> p u c", c=D)
                e = vecs[r][:, :].rearrange("p (u c) -> p u c", c=8)
                scalars, vectors = rw[:, :, 0:MUL], rw[:, :, MUL:D].rearrange("p u (m i) -> p u m i", i=3)
                dve.wait_ge(fetched[r], 16 * U * i + 16 * U)
                dve.wait_ge(got[r], 16 * i + 16)
                s.did(dve.tensor_tensor(dot[r][:, :, :, :], vectors, bcast(e[:, :, 2:5], 2, MUL), ALU.mult))
                s.did(dve.tensor_tensor(fac[r][:, :, 0:MUL], scalars, e[:, :, 0:1].broadcast_to([P, U, MUL]), ALU.mult))
                dve.tensor_tensor(vec[r][:, :, :, :], vectors.rearrange("p u m i -> p u i m"),
                                  bcast(e[:, :, 1:2].broadcast_to([P, U, 3]), 3, MUL), ALU.mult
                                  ).then_inc(ready, 1)
                w = window(j) if j is not None else None
                dve.wait_ge(own, s.base + s.n)
                s.link(dve.tensor_reduce(fac[r][:, :, MUL:2 * MUL], dot[r][:, :, :, :], AX, ALU.add))
                dve.wait_ge(ready, g + 1)
                dve.wait_ge(copied, g + 1)
                m, pr = msg[:, bass.ds(g * U, U), :], prod
                for n, (a, b) in enumerate(PAIR):
                    dve.wait_ge(weighed, g * 3 + n + 1)
                    wv = p_w[n][0:P, 0:(b - a) * HID].rearrange("p (u k w) -> p u w k", k=4 * MUL, w=MUL)
                    dve.tensor_tensor(pr[:, a:b, :, 0:KF], wv[:, :, :, 0:KF], bcast(fac[r][:, a:b, :], 2, MUL), ALU.mult)
                    for j in range(3):
                        ins = dve.tensor_tensor(pr[:, a:b, :, KF + j * MUL:KF + (j + 1) * MUL], wv[:, :, :, KF:4 * MUL],
                                                bcast(vec[r][:, a:b, j, :], 2, MUL), ALU.mult)
                    ins.then_inc(read, 1)
                dve.wait_ge(read, g * 3 + 3)
                s.did(dve.tensor_reduce(red[:, :, :, :], pr[:, :, :, 2 * MUL:2 * KF]
                                        .rearrange("p u w (j k) -> p u w j k", k=MUL), AX, ALU.add))
                s.did(dve.tensor_reduce(m[:, :, 0:MUL], pr[:, :, :, 0:2 * MUL], AX, ALU.add))
                dve.wait_ge(own, s.base + s.n)
                s.link(dve.tensor_tensor(outer[:, :, :, :], red[:, :, :, 0:1].broadcast_to([P, U, MUL, 3]),
                                         bcast(e[:, :, 5:8], 2, MUL), ALU.mult))
                dve.tensor_tensor(m[:, :, MUL:D].rearrange("p u (w j) -> p u w j", j=3), outer[:, :, :, :],
                                  red[:, :, :, 1:4], ALU.add).then_inc(made, 1)
                assert s.n == OPS
                return w

            def add(g, w):
                dve.wait_ge(summed, g + 1)
                dve.wait_ge(added, g + 1)
                a = acc[:, bass.ds(w, 1), :].rearrange("p o m -> p (o m)")
                dve.tensor_tensor(a, a, p_s[0:P, 0:D], ALU.add).then_inc(added, 1)

            dve.tensor_copy(ident[:, :], k.ident[0:P, 0:P]).then_inc(cst, 1)
            dve.memset(acc[:, :, :], 0.0).then_inc(added, 1)
            contract(0, 0, 0, True)
            for r in range(1, SLOTS):
                contract(0, r, r, True)
                add(r - 1, window(r - 1))
            with dve.Fori(1, TRIPS_G) as i:
                for r in range(SLOTS):
                    g = i * SLOTS + r
                    w = contract(i, r, g, False, g - 1)
                    add(g - 1, w)
            with dve.Fori(G - 1, NG) as j:
                add(j, window(j))


def conv(nc, k, t):
    with Stage(nc, "cn") as st:
        acc = st.sb("acc", [P, W, D])
        fc1 = st.sb("fc1", [2 * ROWS, 2, 2, 128], BF16)
        fc2 = st.sb("fc2", [128, 2, HID])
        stage_attributes(nc, k, t["edge_attr_4"], t["edge_attr_8"])
        stage_conv_weights(nc, k, t, fc1, fc2)
        stage_table(nc, k, "tc", k.table3, (k.x[:, :, :],))
        stage_conv(nc, k, fc1, fc2, acc)
        stage_norm(nc, k, "l3", acc[:, :, :], scale=float(1.0 / np.sqrt(E / N)), out=k.out)


def build(nc, t, out, debug=None):
    k = Kept()
    with ExitStack() as ctx:
        def sb(name, shape, dt=F32):
            return ctx.enter_context(nc.sbuf_tensor(name, shape, dt))

        def dram(name, shape, dt=F32):
            return nc.dram_tensor(name, shape, dt, kind="Internal").ap()

        k.ident = sb("ident", [128, 128])
        k.ones = sb("ones", [P, P])
        k.lane = sb("lane", [P, P])
        k.earlier = sb("earlier", [P, P])
        k.negs = sb("negs", [1, 8])
        k.srcf = sb("srcf", [P, NGP * U])
        k.dloc = sb("dloc", [P, NGP * U])
        k.wrow, k.grow = sb("wrow", [1, NG], I32), sb("grow", [1, NG], I32)
        k.first_i = sb("first_i", [P, 1], I32)
        k.nstart, k.infirst = sb("nstart", [P, J], BF16), sb("infirst", [P, J], BF16)
        k.indeg, k.outdeg = sb("indeg", [P, W]), sb("outdeg", [P, W])
        k.end, k.start = sb("end", [P, W], I32), sb("start", [P, W], I32)
        k.x = sb("x", [P, W, D])
        k.start16, k.start2, k.start32, k.start4 = (dram(f"start{c}", (E, c)) for c in (16, 2, 32, 4))
        k.xdst = dram("xdst", (E, D))
        k.wind, k.kxd = dram("wind", (NG, 1), I32), dram("kxd", (X, 1), I32)
        stage_index(nc, k, t["src"], t["dst"])
        k.layers = {"l0": 1, "l1": 2, "l2": 3}.get(debug, 4)
        k.out = out
        k.table1, k.table2 = dram("table1", (N, K1 + H1)), dram("table2", (N, K1 + H2))
        k.eas, k.eav = dram("eas", (G, P, U * ROWS), BF16), dram("eav", (G, P, U * 8))
        k.table3, k.table4 = dram("table3", (N, D)), dram("table4", (N, K1 + HQ * D))
        k.gx = dram("gx", (E, K1))
        k.sc8, k.sc1, k.sc4 = (dram(f"sc{c}", (E, c)) for c in (8, 1, 4))
        k.wt8, k.wt1, k.wt4 = (dram(f"wt{c}", (E, c)) for c in (8, 1, 4))
        k.scan8, k.scan1, k.scan4 = (dram(f"scan{c}", (E + 1, c)) for c in (8, 1, 4))
        k.node16, k.node2, k.node32, k.node4 = (dram(f"node{c}", (N, c)) for c in (16, 2, 32, 4))
        stage_load(nc, k, t["x"])
        stage_zero(nc, k)
        gat(nc, k, t)
        if k.layers > 2:
            attention(nc, k, t)
        if k.layers > 3:
            conv(nc, k, t)


_INS = ["x", "src", "dst", "edge_attr_4", "edge_attr_8", "L0_gnn_W1", "L0_gnn_att_src1", "L0_gnn_att_dst1",
        "L0_gnn_b1", "L0_gnn_W2", "L0_gnn_att_src2", "L0_gnn_att_dst2", "L0_gnn_b2", "L2_gnn_Wq", "L2_gnn_Wk",
        "L2_gnn_Wv", "L2_gnn_Wout", "L3_gnn_fc_w1", "L3_gnn_fc_w2"]
OUT_SHAPE, DEBUG = (N, D), None


def kernel(**inputs):
    import concourse.bacc as bacc
    from concourse.bass_utils import run_bass_kernel_spmd

    nc = bacc.Bacc("TRN2", target_bir_lowering=False, num_devices=1)
    arrays, t = {}, {}
    for name in _INS:
        a = np.ascontiguousarray(inputs[name])
        arrays[f"in_{name}"] = a
        t[name] = nc.dram_tensor(f"in_{name}", a.shape, mybir.dt.from_np(a.dtype), kind="ExternalInput").ap()
    out = nc.dram_tensor("out_nodes", OUT_SHAPE, F32, kind="ExternalOutput").ap()
    build(nc, t, out, DEBUG)
    r = run_bass_kernel_spmd(nc, [arrays], core_ids=[0])
    return r.results[0]["out_nodes"]
```

```python
import numpy as np
from contextlib import ExitStack

import concourse.bass as bass
import concourse.mybir as mybir

F32, I32, BF16 = mybir.dt.float32, mybir.dt.int32, mybir.dt.bfloat16
ALU = mybir.AluOpType
ACT = mybir.ActivationFunctionType
AX = mybir.AxisListType.X

N, E, D = 3125, 103125, 32
P = 125
W = N // P
J = E // P
U = 5
G = E // (P * U)
X = W - 1
NG = G + X
SLOTS = 3
TRIPS = NG // SLOTS
TRIPS_G = G // SLOTS
MIDDLE = N // 2
NGP = NG + SLOTS
H1, H2, HQ = 8, 1, 4
K1 = D + 1
BIG = 1e30
EPS_LN = 1e-5
STEPS_APPNP = 10
ALPHA = 0.1
MUL, BASIS, HID = 8, 8, 256


class Steps:

    def __init__(self, eng, sem, base=0, n=0):
        self.eng, self.sem, self.base, self.n = eng, sem, base, n

    def did(self, ins):
        ins.then_inc(self.sem, 1)
        self.n += 1

    def link(self, ins):
        self.did(ins)
        self.eng.wait_ge(self.sem, self.base + self.n)


def gate(eng, gate_sem):
    eng.sem_inc(gate_sem, 1)


def bcast(ap, axis, n):
    shape = list(ap.shape)
    return ap.unsqueeze(axis).broadcast_to(shape[:axis] + [n] + shape[axis:])


class Kept:
    pass


class Stage:

    def __init__(self, nc, name):
        self.nc, self.name, self.ctx, self.sems = nc, name, ExitStack(), []

    def __enter__(self):
        self.ctx.__enter__()
        return self

    def __exit__(self, *a):
        left = self.ctx.__exit__(*a)
        if self.sems:
            self.nc.clear_and_free_semaphores(self.sems)
            self.nc.all_engine_barrier()
        return left

    def sb(self, name, shape, dt=F32):
        return self.ctx.enter_context(self.nc.sbuf_tensor(f"{self.name}_{name}", shape, dt))

    def ps(self, name, shape, dt=F32):
        return self.ctx.enter_context(self.nc.psum_tensor(f"{self.name}_{name}", shape, dt))

    def sem(self, name):
        self.sems.append(self.nc.alloc_semaphore(f"{self.name}_{name}"))
        return self.sems[-1]

    def block(self):
        return self.ctx.enter_context(self.nc.Block())


def edge_rows(dram, c):
    return dram.rearrange("(g p u) c -> g p (u c)", p=P, u=U)


def nodes_view(dram):
    return dram.rearrange("(w d) c -> d w c", d=P)


def stage_index(nc, k, src, dst):
    GB = G - 128
    with Stage(nc, "ix") as st:
        d_a, d_b, d_x = st.sb("d_a", [128, P * U], I32), st.sb("d_b", [GB, P * U], I32), st.sb("d_x", [X, P * U], I32)
        s_a, s_b, s_x = st.sb("s_a", [128, P * U], I32), st.sb("s_b", [GB, P * U], I32), st.sb("s_x", [X, P * U], I32)
        df = [st.sb(f"df{n}", [r, P * U]) for n, r in enumerate((128, GB, X))]
        sf = [st.sb(f"sf{n}", [r, P * U]) for n, r in enumerate((128, GB, X))]
        edges = st.sb("edges", [128, X])
        edge_col = st.sb("edge_col", [X, 1])
        win_x = st.sb("win_x", [X, 1], I32)
        ge = [st.sb(f"ge{n}", [128, X]) for n in range(2)]
        lt = [st.sb(f"lt{n}", [128, X]) for n in range(2)]
        wf = [st.sb(f"wf{n}", [128, 1]) for n in range(2)]
        w125 = [st.sb(f"w125{n}", [128, 1]) for n in range(2)]
        wi = [st.sb(f"wi{n}", [128, 1], I32) for n in range(2)]
        ones = st.sb("ones", [128, 1])
        kf, pen = st.sb("kf", [X, 1]), st.sb("pen", [X, 1])
        kxi = st.sb("kxi", [X, 1], I32)
        grid, gi = st.sb("gd", [P, J]), st.sb("gdi", [P, J], I32)
        prev = st.sb("prev", [P, 1], I32)
        prevf = st.sb("prevf", [P, 1])
        diag = st.sb("diag", [P, P])
        pt = [st.ps(f"pt{u}", [128, 512]) for u in range(U)]
        p_cnt, p_last = st.ps("p_cnt", [128, 512]), st.ps("p_last", [128, 512])
        loaded, cst, steps, pe_s, gone, ext_i, wrote, wback, fx, pool_s = (
            st.sem(n) for n in ("loaded", "cst", "steps", "pe_s", "gone", "ext_i", "wrote", "wback", "fx", "pool_s"))
        block = st.block()

        @block.sync
        def _(sp):
            sp.dma_start(d_a[:, :], dst[0:128 * P * U].rearrange("(g e) -> g e", e=P * U)).then_inc(loaded, 16)
            sp.dma_start(d_b[:, :], dst[128 * P * U:E].rearrange("(g e) -> g e", e=P * U)).then_inc(loaded, 16)
            sp.dma_start(s_a[:, :], src[0:128 * P * U].rearrange("(g e) -> g e", e=P * U)).then_inc(loaded, 16)
            sp.dma_start(s_b[:, :], src[128 * P * U:E].rearrange("(g e) -> g e", e=P * U)).then_inc(loaded, 16)
            sp.dma_start(gi[:, :], dst.rearrange("(p j) -> p j", j=J)).then_inc(loaded, 16)
            sp.wait_ge(cst, 1)
            sp.dma_start(prev[1:P, 0:1], dst.rearrange("(p j) -> p j", j=J)[0:P - 1, J - 1:J],
                         allow_slow_non_contiguous=True).then_inc(loaded, 16)
            sp.wait_ge(fx, 1)
            sp.dma_start(k.wind[0:128, :], wi[0][:, :]).then_inc(wrote, 16)
            sp.dma_start(k.wind[128:G, :], wi[1][0:GB, :]).then_inc(wrote, 16)
            sp.dma_start(k.wind[G:NG, :], win_x[:, :]).then_inc(wrote, 16)
            sp.dma_start(k.kxd, kxi[:, :]).then_inc(wrote, 16)
            sp.wait_ge(wrote, 64)
            sp.dma_start(k.wrow[:, :], k.wind.rearrange("g o -> o g")).then_inc(wback, 16)
            sp.dma_start(k.grow[:, G:NG], k.kxd.rearrange("g o -> o g")).then_inc(wback, 16)
            sp.wait_ge(wback, 32)

        @block.gpsimd
        def _(pool):
            s = Steps(pool, pool_s)
            pool.memset(prev[:, :], -1).then_inc(cst, 1)
            s.did(pool.memset(k.ident[:, :], 0.0))
            s.link(pool.memset(k.earlier[:, :], 0.0))
            pool.affine_select(out=k.ident[:, :], in_=k.ident[:, :], compare_op=ALU.not_equal, fill=1.0, base=0,
                               pattern=[[-1, 128]], channel_multiplier=1)
            pool.affine_select(out=k.earlier[:, :], in_=k.earlier[:, :], compare_op=ALU.is_gt, fill=-BIG, base=0,
                               pattern=[[-1, P]], channel_multiplier=1)
            pool.memset(ones[:, :], 1.0)
            pool.memset(k.ones[:, :], 1.0)
            pool.memset(k.srcf[:, :], 0.0)
            pool.memset(k.dloc[:, :], 0.0)
            pool.memset(k.negs[:, :], -BIG)
            pool.iota(edges[:, :], [[P, X]], base=P, channel_multiplier=0, allow_small_or_imprecise_dtypes=True)
            pool.iota(edge_col[:, :], [[0, 1]], base=P, channel_multiplier=P, allow_small_or_imprecise_dtypes=True)
            pool.iota(k.grow[:, 0:G], [[1, G]], base=0, channel_multiplier=0)
            pool.iota(win_x[:, :], [[0, 1]], base=1, channel_multiplier=1)
            pool.iota(k.lane[:, :], [[1, P]], base=0, channel_multiplier=0,
                      allow_small_or_imprecise_dtypes=True).then_inc(cst, 1)
            pool.wait_ge(fx, 1)
            by = bass.IndirectOffsetOnAxis(ap=kxi[:, :], axis=0)
            pool.indirect_dma_start(out=d_x[:, :], out_offset=None, in_=dst.rearrange("(g e) -> g e", e=P * U),
                                    in_offset=by).then_inc(ext_i, 16)
            pool.indirect_dma_start(out=s_x[:, :], out_offset=None, in_=src.rearrange("(g e) -> g e", e=P * U),
                                    in_offset=by).then_inc(ext_i, 16)

        @block.vector
        def _(dve):
            s = Steps(dve, steps)
            dve.wait_ge(loaded, 16 * 6)
            dve.wait_ge(cst, 2)
            for o, i in ((df[0], d_a), (df[1], d_b), (sf[0], s_a), (sf[1], s_b), (grid, gi),
                         (prevf, prev), (k.first_i, gi)):
                s.did(dve.tensor_copy(o[:, :], i[:, 0:o.shape[1]]))
            dve.wait_ge(steps, s.n)
            for n, r in ((0, 128), (1, GB)):
                s.link(dve.tensor_scalar(ge[n][0:r, :], edges[0:r, :], df[n][:, 0:1], None, ALU.is_le))
                s.did(dve.tensor_scalar(lt[n][0:r, :], ge[n][0:r, :], -1.0, 1.0, ALU.mult, ALU.add))
                s.link(dve.tensor_reduce(wf[n][0:r, :], ge[n][0:r, :], AX, ALU.add))
                s.did(dve.tensor_copy(wi[n][0:r, :], wf[n][0:r, :]))
                s.link(dve.tensor_scalar(w125[n][0:r, :], wf[n][0:r, :], float(P), None, ALU.mult))
                last = dve.tensor_scalar(df[n][:, :], df[n][:, :], w125[n][0:r, :], None, ALU.subtract)
                if n == 0:
                    s.did(last)
            last.then_inc(gone, 1)
            dve.wait_ge(pe_s, 1)
            s.link(dve.tensor_scalar(kf[:, :], p_cnt[0:X, 0:1], -1.0, 0.0, ALU.add, ALU.max))
            s.did(dve.tensor_scalar(pen[:, :], p_cnt[0:X, 0:1], 0.5, 8192.0, ALU.is_lt, ALU.mult))
            dve.tensor_copy(kxi[:, :], kf[:, :]).then_inc(fx, 1)
            s.link(dve.tensor_scalar(k.nstart[:, 0:1], grid[:, 0:1], prevf[:, 0:1], None, ALU.is_equal))
            s.link(dve.tensor_tensor(k.nstart[:, 1:J], grid[:, 1:J], grid[:, 0:J - 1], ALU.is_equal))
            s.link(dve.tensor_scalar(k.infirst[:, :], grid[:, :], grid[:, 0:1], None, ALU.is_equal))
            dve.tensor_scalar(diag[:, :], k.ident[0:P, 0:P], grid[:, J - 1:J], None, ALU.mult).then_inc(gone, 1)
            dve.wait_ge(pe_s, 2)
            s.link(dve.tensor_scalar(diag[:, :], p_last[0:P, 0:P], grid[:, 0:1], None, ALU.is_equal))
            s.link(dve.tensor_scalar(diag[:, :], diag[:, :], BIG, -BIG, ALU.mult, ALU.add))
            s.link(dve.tensor_tensor(k.earlier[:, :], k.earlier[:, :], diag[:, :], ALU.min))
            dve.wait_ge(ext_i, 32)
            s.did(dve.tensor_copy(df[2][:, :], d_x[:, :]))
            s.link(dve.tensor_copy(sf[2][:, :], s_x[:, :]))
            dve.tensor_scalar(df[2][:, :], df[2][:, :], edge_col[:, 0:1], pen[:, 0:1],
                              ALU.subtract, ALU.add).then_inc(gone, 1)
            dve.wait_ge(pe_s, 3)
            dl = k.dloc[:, :].rearrange("p (g u) -> p g u", u=U)
            si = k.srcf[:, :].rearrange("p (g u) -> p g u", u=U)
            for u in range(U):
                s.did(dve.tensor_copy(dl[:, 0:NG, u], pt[u][0:P, 0:NG]))
                s.did(dve.tensor_scalar(si[:, 0:NG, u], pt[u][0:P, 256:256 + NG], float(-MIDDLE), None, ALU.add))

        @block.tensor
        def _(pe):
            pe.wait_ge(cst, 2)
            pe.wait_ge(gone, 1)
            nc.tensor.matmul(p_cnt[0:X, 0:1], lt[0][:, :], ones[:, :], start=True, stop=False)
            nc.tensor.matmul(p_cnt[0:X, 0:1], lt[1][0:GB, :], ones[0:GB, :], start=False, stop=True).then_inc(pe_s, 1)
            pe.wait_ge(gone, 2)
            nc.tensor.matmul(p_last[0:P, 0:P], k.ones[:, :], diag[:, :], start=True, stop=True).then_inc(pe_s, 1)
            pe.wait_ge(gone, 3)
            for u in range(U):
                for c, f in ((0, df), (256, sf)):
                    at = c
                    for b in range(3):
                        r = f[b].shape[0]
                        last = nc.tensor.transpose(pt[u][0:P, at:at + r],
                                                   f[b][:, :].rearrange("g (p u) -> g p u", u=U)[:, :, u],
                                                   k.ident[0:r, 0:r])
                        at += r
            last.then_inc(pe_s, 1)


INV_SQRT3 = float(1.0 / np.sqrt(3.0))
A_SCALAR = float(np.sqrt(1.0 / 128.0))
A_VECTOR = float(np.sqrt(3.0 / 128.0))
PARTS_EDGE = (0, 0, 0, 1, 1, 2)
PARTS_FC = (0, 1, 2, 0, 1, 0)
ROWS = 6 * BASIS


def split(link, dve, value, rest, parts):
    link(dve.tensor_copy(parts[0], value))
    link(dve.tensor_tensor(rest, value, parts[0], ALU.subtract))
    link(dve.tensor_copy(parts[1], rest))
    link(dve.tensor_tensor(rest, rest, parts[1], ALU.subtract))
    link(dve.tensor_copy(parts[2], rest))


class Attributes:
    CHUNK = 11
    CHUNKS = G // CHUNK
    LAG = 17
    ZEROS = 2 * J

    def __init__(self, k, ea4, ea8):
        self.k, self.ea4, self.ea8 = k, ea4, ea8

    def room(self, st):
        self.e8, self.e4 = st.sb("e8", [P, G, U * BASIS]), st.sb("e4", [P, G, U * 4])
        self.rest = st.sb("rest", [P, self.CHUNK * U, BASIS])
        self.eas, self.eav = st.sb("eas", [P, G * U, 6, BASIS], BF16), st.sb("eav", [P, G * U, 8])
        self.zeros = st.sb("zeros", [P, self.ZEROS])
        self.got, self.made, self.steps, self.wrote, self.zeroed, self.wiped = (
            st.sem(n) for n in ("a_got", "a_made", "a_steps", "a_wrote", "zeroed", "wiped"))

    def load(self, sp, n):
        at = bass.ds(n * self.CHUNK, self.CHUNK)
        for dram, o, c in ((self.ea8, self.e8, BASIS), (self.ea4, self.e4, 4)):
            sp.dma_start(o[:, at, :], edge_rows(dram, c)[at].rearrange("g p c -> p g c")).then_inc(self.got, 16)

    def wipe(self, sp, start, c, n):
        view, m, z = start.rearrange("(p j) c -> p (j c)", j=J), min(2, c // 2), self.ZEROS
        for half in range(m):
            sp.dma_start(view[:, bass.ds((n * m + half) * z, z)], self.zeros[:, :]).then_inc(self.wiped, 16)

    def sync(self, sp):
        self.load(sp, 0)
        sp.wait_ge(self.zeroed, 1)

    def spans(self):
        k = self.k

        def load(sp, i):
            sp.wait_ge(self.got, i * 32 + 32)
            self.load(sp, i + 1)

        out = [(0, 1, load), (1, self.CHUNKS - 1, load), (self.CHUNKS - 1, self.LAG, None),
               (self.LAG, self.CHUNKS + self.LAG, lambda sp, i: self.write(sp, i - self.LAG))]
        at, self.wipes = self.CHUNKS + self.LAG, 0
        for start, c in ((k.start16, 16), (k.start2, 2), (k.start32, 32), (k.start4, 4)):
            n = -(-c // 4)
            out.append((at, at + n, lambda sp, i, start=start, c=c, at=at: self.wipe(sp, start, c, i - at)))
            at, self.wipes = at + n, self.wipes + c // 2
        return out + [(at, TRIPS_G, None)]

    def write(self, sp, n):
        sp.wait_ge(self.made, n + 1)
        m = self.CHUNK * U
        for dram, o in ((self.k.eas, self.eas[:, bass.ds(n * m, m), :, :].rearrange("p n j b -> p n (j b)")),
                        (self.k.eav, self.eav[:, bass.ds(n * m, m), :])):
            sp.dma_start(dram[bass.ds(n * self.CHUNK, self.CHUNK)].rearrange("g p (u c) -> p g u c", u=U),
                         o.rearrange("p (g u) c -> p g u c", u=U)).then_inc(self.wrote, 16)

    def sync_end(self, sp):
        sp.wait_ge(self.wrote, 32 * self.CHUNKS)
        sp.wait_ge(self.wiped, 16 * self.wipes)

    def vector(self, dve, n):
        s = Steps(dve, self.steps, n * 10)
        dve.wait_ge(self.got, n * 32 + 32)
        m, at = self.CHUNK * U, bass.ds(n * self.CHUNK, self.CHUNK)
        o, q = self.eas[:, bass.ds(n * m, m), :, :], self.eav[:, bass.ds(n * m, m), :]
        v = self.e8[:, at, :].rearrange("p g (u b) -> p (g u) b", b=BASIS)
        e = self.e4[:, at, :].rearrange("p g (u c) -> p (g u) c", c=4)
        split(s.link, dve, v, self.rest[:, :, :], (o[:, :, 0, :], o[:, :, 3, :], o[:, :, 5, :]))
        s.did(dve.tensor_copy(o[:, :, 1:3, :], bcast(o[:, :, 0, :], 2, 2)))
        s.did(dve.tensor_copy(o[:, :, 4, :], o[:, :, 3, :]))
        s.did(dve.tensor_scalar(q[:, :, 0:1], e[:, :, 0:1], A_SCALAR, None, ALU.mult))
        s.did(dve.tensor_scalar(q[:, :, 1:2], e[:, :, 0:1], A_VECTOR * INV_SQRT3, None, ALU.mult))
        s.did(dve.tensor_scalar(q[:, :, 2:5], e[:, :, 1:4], A_SCALAR * INV_SQRT3, None, ALU.mult))
        dve.tensor_scalar(q[:, :, 5:8], e[:, :, 1:4], A_VECTOR * INV_SQRT3, None, ALU.mult).then_inc(self.made, 1)
        assert s.n == 10


class Degrees:

    GROUPS = G

    def __init__(self, nc, k, src, dst, attributes):
        self.nc, self.k, self.ends, self.attributes = nc, k, (dst, src), attributes

    def scalar(self, act, g):
        pass

    def room(self, st):
        self.attributes.room(st)
        self.gi = [st.sb(f"gi{a}", [P, J], I32) for a in range(2)]
        self.lo, self.hi = ([st.sb(f"{n}{a}", [P, J], BF16) for a in range(2)] for n in ("lo", "hi"))
        self.lanes = st.sb("lanes", [P, P], BF16)
        self.low_hot, self.high_hot = st.sb("low_hot", [P, 2, U, P], BF16), st.sb("high_hot", [P, 2, U, W], BF16)
        self.zb = st.sb("zb", [P, P], BF16)
        self.grid, self.part = st.sb("grid", [P, J]), st.sb("part", [P, J])
        self.tri = st.sb("tri", [P, P])
        self.room_w = {n: st.sb(n, [P, W]) for n in ("tot", "before", "endf", "startf", "none")}
        self.p_deg, self.p_tot, self.p_tri = (st.ps(n, [128, 512]) for n in ("p_deg", "p_tot", "p_tri"))
        self.loaded, self.cst, self.hot, self.counted, self.degs, self.summed, self.steps = (
            st.sem(n) for n in ("loaded", "cst", "hot", "counted", "degs", "summed", "dsteps"))

    def sync(self, sp):
        for a in range(2):
            sp.dma_start(self.gi[a][:, :], self.ends[a].rearrange("(p j) -> p j", j=J)).then_inc(self.loaded, 16)
        self.attributes.sync(sp)

    def spans(self):
        return self.attributes.spans()

    def sync_end(self, sp):
        self.attributes.sync_end(sp)

    def gpsimd(self, pool):
        pool.memset(self.zb[:, :], 0.0)
        pool.memset(self.tri[:, :], 1.0).then_inc(self.cst, 1)
        pool.wait_ge(self.cst, 1)
        pool.affine_select(out=self.tri[:, :], in_=self.tri[:, :], compare_op=ALU.is_ge, fill=0.0, base=0,
                           pattern=[[1, P]], channel_multiplier=-1).then_inc(self.cst, 1)

    def vector(self, dve):
        k, lo, hi, part, grid = self.k, self.lo, self.hi, self.part, self.grid
        low_hot, high_hot = self.low_hot, self.high_hot
        s = Steps(dve, self.steps)
        dve.memset(self.attributes.zeros[:, :], 0.0).then_inc(self.attributes.zeroed, 1)
        s.did(dve.tensor_copy(self.lanes[:, :], k.lane[:, :]))
        dve.wait_ge(self.loaded, 32)
        for a in range(2):
            s.did(dve.tensor_copy(grid[:, :], self.gi[a][:, :]))
            s.link(dve.memset(part[:, :], 0.0))
            for t in range(1, W):
                s.link(dve.scalar_tensor_tensor(part[:, :], grid[:, :], float(P * t), part[:, :], ALU.is_ge, ALU.add))
            s.did(dve.tensor_copy(hi[a][:, :], part[:, :]))
            s.link(dve.scalar_tensor_tensor(lo[a][:, :], part[:, :], float(-P), grid[:, :], ALU.mult, ALU.add))

        def one_hot(i, first=False):
            for a in range(2):
                if not first:
                    dve.wait_ge(self.counted, 2 * i + a - 1)
                dve.tensor_tensor(low_hot[:, a], bcast(self.lanes[:, :], 1, U),
                                  bcast(lo[a][:, bass.ds(i * U, U)], 2, P), ALU.is_equal)
                dve.tensor_tensor(high_hot[:, a], bcast(self.lanes[:, 0:W], 1, U),
                                  bcast(hi[a][:, bass.ds(i * U, U)], 2, W), ALU.is_equal).then_inc(self.hot, 1)

        one_hot(0, True)
        m = Attributes.CHUNK
        with dve.Fori(1, m) as i:
            one_hot(i)
        self.attributes.vector(dve, 0)
        with dve.Fori(1, Attributes.CHUNKS) as n:
            with dve.Fori(0, m) as i:
                one_hot(n * m + i)
            self.attributes.vector(dve, n)
        dve.wait_ge(self.counted, 2 * G)
        s = Steps(dve, self.degs)
        s.did(dve.tensor_copy(k.indeg[:, :], self.p_deg[0:P, 0:W]))
        s.link(dve.tensor_copy(k.outdeg[:, :], self.p_deg[0:P, 64:64 + W]))
        dve.wait_ge(self.summed, 2)
        tot, before, endf, startf, none = (self.room_w[n] for n in ("tot", "before", "endf", "startf", "none"))
        s.link(dve.tensor_copy(tot[:, :], self.p_tot[0:P, 0:W]))
        s.link(dve.tensor_tensor_scan(before[:, :], k.ones[:, 0:W], tot[:, :], 0.0, ALU.mult, ALU.add))
        s.link(dve.tensor_tensor(before[:, :], before[:, :], tot[:, :], ALU.subtract))
        s.link(dve.tensor_tensor(endf[:, :], self.p_tri[0:P, 0:W], before[:, :], ALU.add))
        s.link(dve.tensor_tensor(startf[:, :], endf[:, :], k.indeg[:, :], ALU.subtract))
        s.link(dve.tensor_scalar(endf[:, :], endf[:, :], -1.0, None, ALU.add))
        s.link(dve.tensor_scalar(none[:, :], k.indeg[:, :], 0.5, None, ALU.is_lt))
        for v, o in ((endf, k.end), (startf, k.start)):
            s.link(dve.tensor_scalar(before[:, :], v[:, :], -1.0, float(E), ALU.mult, ALU.add))
            s.link(dve.tensor_tensor(before[:, :], before[:, :], none[:, :], ALU.mult))
            s.link(dve.tensor_tensor(v[:, :], v[:, :], before[:, :], ALU.add))
            s.link(dve.tensor_copy(o[:, :], v[:, :]))

    def tensor(self, pe):
        nc, k = self.nc, self.k
        pe.wait_ge(self.cst, 2)
        for a in range(2):
            nc.tensor.matmul(self.p_deg[0:P, 64 * a:64 * a + W], self.zb[:, :], self.zb[:, 0:W], start=True,
                             stop=False, skip_group_check=True)
        with pe.Fori(0, G) as i:
            for a in range(2):
                pe.wait_ge(self.hot, 2 * i + a + 1)
                for u in range(U):
                    last = nc.tensor.matmul(self.p_deg[0:P, 64 * a:64 * a + W], self.low_hot[:, a, u, :],
                                            self.high_hot[:, a, u, :], start=False, stop=False, skip_group_check=True)
                last.then_inc(self.counted, 1)
        pe.wait_ge(self.degs, 2)
        nc.tensor.matmul(self.p_tot[0:P, 0:W], k.ones[:, :], k.indeg[:, :], start=True, stop=True).then_inc(self.summed, 1)
        nc.tensor.matmul(self.p_tri[0:P, 0:W], self.tri[:, :], k.indeg[:, :], start=True, stop=True).then_inc(self.summed, 1)


def load(sp, sem, *pairs):
    for o, i in pairs:
        sp.dma_start(o, i, allow_slow_non_contiguous=True).then_inc(sem, 16)
    return 16 * len(pairs)


def stage_windows(nc, k, name, src, parts, size, rhs, out, mid=None, bias=None):
    m = out.shape[2]
    with Stage(nc, name) as st:
        x_w = st.sb("x_w", [P, parts * size])
        x_t = [st.sb(f"x_t{n}", [size, parts, P]) for n in range(2)]
        y_t = [st.sb(f"y_t{n}", [size, parts, P]) for n in range(2)] if mid else x_t
        p_t = [st.ps(f"p_t{c}", [128, 512]) for c in range(parts)]
        p_m = [st.ps(f"p_m{c}", [128, 512]) for c in range(parts)]
        p_o = st.ps("p_o", [128, 512])
        picked, turned, copied, mixed, bent, summed, kept = (
            st.sem(n) for n in ("picked", "turned", "copied", "mixed", "bent", "summed", "kept"))
        block = st.block()

        def steps(eng, step):
            step(0, 0)
            step(1, 1)
            with eng.Fori(1, W // 2 - 1) as i:
                for half in range(2):
                    step(i * 2 + half, half)
            for n in range(W // 2 * 2 - 2, W + 1):
                step(n, n % 2)

        def starts(n):
            return isinstance(n, int) and n == 0

        def ends(n, at):
            return isinstance(n, int) and n >= at

        @block.tensor
        def _(pe):
            def turn(w):
                pe.wait_ge(picked, w + 1)
                if not starts(w):
                    pe.wait_ge(copied, w)
                for c in range(parts):
                    ins = nc.tensor.transpose(p_t[c][0:size, 0:P], x_w[:, size * c:size * (c + 1)], k.ident[0:P, 0:P])
                ins.then_inc(turned, 1)

            def mix(w, slot):
                pe.wait_ge(copied, w + 1)
                if not starts(w):
                    pe.wait_ge(bent, w)
                for c in range(parts):
                    ins = nc.tensor.matmul(p_m[c][0:size, 0:P], mid[:, c, :], x_t[slot][:, c, :], start=True, stop=True)
                ins.then_inc(mixed, 1)

            def add_up(w, slot):
                pe.wait_ge(bent if mid else copied, w + 1)
                if not starts(w):
                    pe.wait_ge(kept, w)
                for c in range(parts):
                    ins = nc.tensor.matmul(p_o[0:P, 0:m], y_t[slot][:, c, :], rhs[:, c, :], start=c == 0, stop=c == parts - 1)
                ins.then_inc(summed, 1)

            def step(n, slot):
                if not ends(n, W - 1):
                    turn(n + 1)
                if mid and not ends(n, W):
                    mix(n, slot)
                if not starts(n):
                    add_up(n - 1, 1 - slot)

            turn(0)
            steps(pe, step)

        @block.scalar
        def _(act):
            def copy(w, slot):
                act.wait_ge(turned, w + 1)
                if not mid and not (isinstance(w, int) and w < 2):
                    act.wait_ge(summed, w - 1)
                for c in range(parts):
                    ins = nc.scalar.copy(x_t[slot][:, c, :], p_t[c][0:size, 0:P])
                ins.then_inc(copied, 1)

            def bend(w, slot):
                act.wait_ge(mixed, w + 1)
                if not (isinstance(w, int) and w < 2):
                    act.wait_ge(summed, w - 1)
                for c in range(parts):
                    ins = nc.scalar.activation(y_t[slot][:, c, :], p_m[c][0:size, 0:P], ACT.Relu, bias=bias[:, c:c + 1])
                ins.then_inc(bent, 1)

            def step(n, slot):
                if not ends(n, W - 1):
                    copy(n + 1, 1 - slot)
                if mid and not ends(n, W):
                    bend(n, slot)

            copy(0, 0)
            steps(act, step)

        @block.vector
        def _(dve):
            def pick(w):
                if not starts(w):
                    dve.wait_ge(turned, w)
                dve.tensor_copy(x_w[:, :], src[:, bass.ds(w, 1), :].rearrange("p o f -> p (o f)")).then_inc(picked, 1)

            def keep(w):
                dve.wait_ge(summed, w + 1)
                dve.tensor_copy(out[:, bass.ds(w, 1), :].rearrange("p o f -> p (o f)"), p_o[0:P, 0:m]).then_inc(kept, 1)

            def step(n, slot):
                if not ends(n, W - 2):
                    pick(n + 2)
                if not starts(n):
                    keep(n - 1)

            pick(0)
            pick(1)
            steps(dve, step)


def stage_gat_weights(nc, k, t):
    with Stage(nc, "gw") as st:
        w1 = st.sb("w1", [D, H1 * D])
        a1 = st.sb("a1", [D, 2, H1 * D])
        prod = st.sb("prod", [D, 2, H1 * D])
        a2 = st.sb("a2", [128, 2, D])
        prod2 = st.sb("prod2", [128, 2, 2, D])
        got, z, steps = st.sem("got"), st.sem("z"), st.sem("steps")
        block = st.block()

        @block.gpsimd
        def _(pool):
            pool.memset(k.mix1[:, :, :], 0.0).then_inc(z, 1)

        @block.sync
        def _(sp):
            load(sp, got, (w1[:, :], t["L0_gnn_W1"]),
                 (a1[:, 0, :], t["L0_gnn_att_src1"].rearrange("o h c -> o (h c)").broadcast_to([D, H1 * D])),
                 (a1[:, 1, :], t["L0_gnn_att_dst1"].rearrange("o h c -> o (h c)").broadcast_to([D, H1 * D])),
                 (a2[:, 0, :], t["L0_gnn_att_src2"].rearrange("o h c -> o (h c)").broadcast_to([128, D])),
                 (a2[:, 1, :], t["L0_gnn_att_dst2"].rearrange("o h c -> o (h c)").broadcast_to([128, D])),
                 (k.b1[:, :], t["L0_gnn_b1"].rearrange("(c p) -> p c", p=128)),
                 (k.b2[:, :], t["L0_gnn_b2"].unsqueeze(0).broadcast_to([P, D])))
            for c in range(2):
                sp.dma_start(k.w2[:, c, 0:D], t["L0_gnn_W2"][128 * c:128 * (c + 1), :]).then_inc(got, 16)
            sp.wait_ge(z, 1)
            for h in range(H1):
                c, at = h // 4, D * (h % 4)
                sp.dma_start(k.mix1[at:at + D, c, at:at + D], t["L0_gnn_W1"][:, D * h:D * (h + 1)]).then_inc(got, 16)
            sp.wait_ge(got, 16 * 17)

        @block.vector
        def _(dve):
            s = Steps(dve, steps)
            dve.wait_ge(got, 16 * 17)
            s.link(dve.tensor_tensor(prod[:, :, :], bcast(w1[:, :], 1, 2), a1[:, :, :], ALU.mult))
            s.did(dve.tensor_reduce(k.att1[:, 0, :], prod[:, :, :].rearrange("p a (h c) -> p (a h) c", c=D), AX, ALU.add))
            for c in range(2):
                s.link(dve.tensor_tensor(prod2[:, c, :, :], bcast(k.w2[:, c, 0:D], 1, 2), a2[:, :, :], ALU.mult))
                s.did(dve.tensor_reduce(k.w2[:, c, D:D + 2], prod2[:, c, :, :], AX, ALU.add))


def stage_table(nc, k, name, table, cols):
    width = table.shape[1]
    with Stage(nc, name) as st:
        tab = st.sb("tab", [P, W, width])
        made, wrote = st.sem("made"), st.sem("wrote")
        block = st.block()

        @block.vector
        def _(dve):
            at = 0
            for c in cols:
                if c is None:
                    dve.memset(tab[:, :, at:at + 1], 1.0).then_inc(made, 1)
                    at += 1
                else:
                    dve.tensor_copy(tab[:, :, at:at + c.shape[2]], c).then_inc(made, 1)
                    at += c.shape[2]

        @block.sync
        def _(sp):
            sp.wait_ge(made, len(cols))
            sp.dma_start(nodes_view(table), tab[:, :, :]).then_inc(wrote, 16)
            sp.wait_ge(wrote, 16)


def stage_gather(nc, k, name, table, gx, scores=None, n_scores=0, products=False,
                 beside=None):
    width = table.shape[1]
    c = n_scores
    with Stage(nc, name) as st:
        idx = [st.sb(f"idx{r}", [P, U], I32) for r in range(SLOTS)]
        row = [st.sb(f"row{r}", [P, U * width]) for r in range(SLOTS)]
        fx = [st.sb(f"fx{r}", [P, U * K1]) for r in range(SLOTS)]
        sc = [st.sb(f"sc{r}", [P, U * c]) for r in range(SLOTS)] if c else None
        if products:
            xd = [st.sb(f"xd{r}", [P, U * D]) for r in range(SLOTS)]
            prod = [st.sb(f"prod{r}", [P, U * c * D]) for r in range(SLOTS)]
        named, packed, scored, multiplied, gt = (st.sem(n) for n in ("named", "packed", "scored", "multiplied", "gt"))
        fetched = [st.sem(f"fetched{r}") for r in range(SLOTS)]
        wrote = [st.sem(f"wrote{r}") for r in range(SLOTS)]
        at_dst = [st.sem(f"at_dst{r}") for r in range(SLOTS)]
        if beside:
            beside.room(st)
        block = st.block()
        outs = 2 if c else 1

        def rows(r, a, b):
            return row[r][:, :].rearrange("p (u c) -> p u c", c=width)[:, :, a:b]

        @block.scalar
        def _(act):
            def name_edges(g, r):
                nc.scalar.activation(idx[r][:, :], k.srcf[:, bass.ds(g * U, U)], ACT.Copy,
                                     bias=float(MIDDLE)).then_inc(named, 1)

            def trip(i, first):
                for r in range(SLOTS):
                    act.wait_ge(fetched[r], 16 * U * i + 16 * U)
                    if not first:
                        act.wait_ge(wrote[r], 16 * outs * i)
                    if c and not products:
                        nc.scalar.copy(sc[r][:, :].rearrange("p (u c) -> p u c", c=c), rows(r, K1, K1 + c))
                    nc.scalar.copy(fx[r][:, :].rearrange("p (u c) -> p u c", c=K1), rows(r, 0, K1)).then_inc(packed, 1)
                    act.wait_ge(packed, i * SLOTS + r + 1)
                    if products:
                        act.wait_ge(multiplied, i * SLOTS + r + 1)
                    name_edges(i * SLOTS + r + SLOTS, r)
                    if beside:
                        beside.scalar(act, i * SLOTS + r)

            for r in range(SLOTS):
                name_edges(r, r)
            trip(0, True)
            with act.Fori(1, TRIPS_G) as i:
                trip(i, False)
            if beside and beside.GROUPS > G:
                with act.Fori(G, beside.GROUPS) as g:
                    beside.scalar(act, g)

        @block.gpsimd
        def _(pool):
            if beside:
                beside.gpsimd(pool)
            with pool.Fori(0, TRIPS_G) as i:
                for r in range(SLOTS):
                    pool.wait_ge(named, i * SLOTS + r + 1)
                    gate(pool, gt)
                    for u in range(U):
                        pool.indirect_dma_start(
                            out=row[r][:, u * width:(u + 1) * width], out_offset=None, in_=table,
                            in_offset=bass.IndirectOffsetOnAxis(ap=idx[r][:, u:u + 1], axis=0)).then_inc(fetched[r], 16)

        @block.sync
        def _(sp):
            if beside:
                beside.sync(sp)

            def trip(i, first):
                if products:
                    for r in range(SLOTS):
                        if not first:
                            sp.wait_ge(multiplied, i * SLOTS + r + 1 - SLOTS)
                        sp.dma_start(xd[r][:, :], edge_rows(k.xdst, D)[bass.ds(i * SLOTS + r, 1)]
                                     .rearrange("o p c -> (o p) c")).then_inc(at_dst[r], 16)
                for r in range(SLOTS):
                    sp.wait_ge(packed, i * SLOTS + r + 1)
                    sp.dma_start(edge_rows(gx, K1)[bass.ds(i * SLOTS + r, 1)].rearrange("o p c -> (o p) c"),
                                 fx[r][:, :]).then_inc(wrote[r], 16)
                    if c:
                        if products:
                            sp.wait_ge(scored, i * SLOTS + r + 1)
                        sp.dma_start(edge_rows(scores, c)[bass.ds(i * SLOTS + r, 1)].rearrange("o p c -> (o p) c"),
                                     sc[r][:, :]).then_inc(wrote[r], 16)

            for a, b, also in beside.spans() if beside else [(0, 1, None), (1, TRIPS_G, None)]:
                if b - a == 1:
                    trip(a, a == 0)
                    if also:
                        also(sp, a)
                    continue
                with sp.Fori(a, b) as i:
                    trip(i, False)
                    if also:
                        also(sp, i)
            if beside:
                beside.sync_end(sp)
            for r in range(SLOTS):
                sp.wait_ge(wrote[r], 16 * outs * TRIPS_G)

        if beside:
            @block.vector
            def _(dve):
                beside.vector(dve)

            @block.tensor
            def _(pe):
                beside.tensor(pe)

        if products:
            @block.vector
            def _(dve):
                def trip(i, first):
                    for r in range(SLOTS):
                        dve.wait_ge(fetched[r], 16 * U * i + 16 * U)
                        dve.wait_ge(at_dst[r], 16 * i + 16)
                        p4 = prod[r][:, :].rearrange("p (u h f) -> p u h f", h=c, f=D)
                        dve.tensor_tensor(p4, rows(r, K1, K1 + c * D).rearrange("p u (h f) -> p u h f", f=D),
                                          bcast(xd[r][:, :].rearrange("p (u f) -> p u f", f=D), 2, c),
                                          ALU.mult).then_inc(multiplied, 1)
                        dve.wait_ge(multiplied, i * SLOTS + r + 1)
                        if not first:
                            dve.wait_ge(wrote[r], 16 * outs * i)
                        dve.tensor_reduce(sc[r][:, :], prod[r][:, :].rearrange("p (n f) -> p n f", f=D),
                                          AX, ALU.add).then_inc(scored, 1)

                trip(0, True)
                with dve.Fori(1, TRIPS_G) as i:
                    trip(i, False)


def stage_segmax(nc, k, name, scores, c, scanned, amax):
    with Stage(nc, name) as st:
        v = st.sb("v", [P, J, c])
        mask = st.sb("mask", [P, J])
        diag, room = st.sb("diag", [P, 2, P]), st.sb("room", [P, 2, P])
        carry = st.sb("carry", [P, c])
        p_b = [st.ps(f"p_b{n}", [128, 512]) for n in range(2)]
        got, steps, diags, spread, dumped, fetched = (
            st.sem(n) for n in ("got", "steps", "diags", "spread", "dumped", "fetched"))
        done = st.sem("done")
        block = st.block()

        @block.sync
        def _(sp):
            sp.dma_start(v[:, :, :], scores[0:E, :].rearrange("(p j) c -> p j c", j=J)).then_inc(got, 16)
            sp.wait_ge(done, 1)
            sp.dma_start(scanned[0:E, :].rearrange("(p j) c -> p j c", j=J), v[:, :, :]).then_inc(dumped, 16)
            sp.dma_start(scanned[E:E + 1, :], k.negs[0:1, 0:c]).then_inc(dumped, 16)
            sp.wait_ge(dumped, 32)

        @block.vector
        def _(dve):
            s = Steps(dve, steps)
            s.link(dve.tensor_scalar(mask[:, :], k.nstart[:, :], BIG, -BIG, ALU.mult, ALU.add))
            dve.wait_ge(got, 16)
            for h in range(c):
                s.did(dve.tensor_tensor_scan(v[:, :, h], mask[:, :], v[:, :, h], -BIG, ALU.add, ALU.max))
            dve.wait_ge(steps, s.n)
            s.did(dve.tensor_scalar(mask[:, :], k.infirst[:, :], BIG, -BIG, ALU.mult, ALU.add))
            for h in range(c):
                if h >= 2:
                    dve.wait_ge(spread, h - 1)
                dve.tensor_scalar(diag[:, h % 2, :], k.ident[0:P, 0:P], v[:, J - 1, h:h + 1], None,
                                  ALU.mult).then_inc(diags, 1)
                dve.wait_ge(spread, h + 1)
                s.link(dve.tensor_tensor(room[:, h % 2, :], p_b[h % 2][0:P, 0:P], k.earlier[:, :], ALU.add))
                s.did(dve.tensor_reduce(carry[:, h:h + 1], room[:, h % 2, :], AX, ALU.max))
            dve.wait_ge(steps, s.n)
            for h in range(c):
                ins = dve.scalar_tensor_tensor(v[:, :, h], mask[:, :], carry[:, h:h + 1], v[:, :, h],
                                               ALU.add, ALU.max)
            ins.then_inc(done, 1)

        @block.tensor
        def _(pe):
            for h in range(c):
                pe.wait_ge(diags, h + 1)
                nc.tensor.matmul(p_b[h % 2][0:P, 0:P], k.ones[:, :], diag[:, h % 2, :], start=True,
                                 stop=True).then_inc(spread, 1)

        @block.gpsimd
        def _(pool):
            pool.wait_ge(dumped, 32)
            for w in range(W):
                pool.indirect_dma_start(out=amax[:, w, :], out_offset=None, in_=scanned,
                                        in_offset=bass.IndirectOffsetOnAxis(ap=k.end[:, w:w + 1], axis=0)
                                        ).then_inc(fetched, 16)
            pool.wait_ge(fetched, 16 * W)


def stage_spread(nc, k, name, tab, table, start, xdst=None, scores=None, heads=0, weights=None):
    c = tab.shape[2]
    with Stage(nc, name) as st:
        v = st.sb("v", [P, J, c])
        head = st.sb("head", [P, c])
        if scores is not None:
            z = st.sb("z", [P, J, heads])
        wrote, placed, first, got, steps, ready, expd, ends = (
            st.sem(n) for n in ("wrote", "placed", "first", "got", "steps", "ready", "expd", "ends"))
        block = st.block()

        @block.sync
        def _(sp):
            sp.dma_start(nodes_view(table), tab[:, :, :]).then_inc(wrote, 16)
            if scores is not None:
                sp.dma_start(z[:, :, :], scores[0:E, :].rearrange("(p j) c -> p j c", j=J)).then_inc(got, 16)
            sp.wait_ge(placed, 16 * W)
            sp.dma_start(v[:, :, :], start.rearrange("(p j) c -> p j c", j=J)).then_inc(got, 16)
            if xdst is not None:
                sp.wait_ge(ready, 1)
                sp.dma_start(xdst[0:E, :].rearrange("(p j) c -> p j c", j=J), v[:, :, :]).then_inc(ends, 16)
                sp.wait_ge(ends, 16)
            else:
                sp.wait_ge(expd, 1)
                sp.dma_start(weights[0:E, :].rearrange("(p j) c -> p j c", j=J), z[:, :, :]).then_inc(ends, 16)
                sp.wait_ge(ends, 16)

        @block.gpsimd
        def _(pool):
            for w in range(W):
                pool.indirect_dma_start(out=start, in_=tab[:, w, :], in_offset=None,
                                        out_offset=bass.IndirectOffsetOnAxis(ap=k.start[:, w:w + 1], axis=0),
                                        bounds_check=E - 1, oob_is_err=False).then_inc(placed, 16)
            pool.wait_ge(wrote, 16)
            pool.indirect_dma_start(out=head[:, :], out_offset=None, in_=table,
                                    in_offset=bass.IndirectOffsetOnAxis(ap=k.first_i[:, :], axis=0)).then_inc(first, 16)

        @block.vector
        def _(dve):
            s = Steps(dve, steps)
            dve.wait_ge(first, 16)
            dve.wait_ge(got, 16 if scores is None else 32)
            for h in range(c):
                ins = dve.tensor_tensor_scan(v[:, :, h], k.nstart[:, :], v[:, :, h], head[:, h:h + 1],
                                             ALU.mult, ALU.add)
                if h < c - 1 or scores is not None:
                    s.did(ins)
            if scores is None:
                ins.then_inc(ready, 1)
                return
            dve.wait_ge(steps, s.n)
            if c == 2 * heads:
                s.link(dve.tensor_tensor(z[:, :, :], z[:, :, :], v[:, :, 0:heads], ALU.add))
                s.link(dve.scalar_tensor_tensor(z[:, :, :], z[:, :, :], 0.2, z[:, :, :], ALU.mult, ALU.max))
            dve.tensor_tensor(z[:, :, :], z[:, :, :], v[:, :, c - heads:c], ALU.subtract).then_inc(ready, 1)

        if scores is not None:
            @block.scalar
            def _(act):
                act.wait_ge(ready, 1)
                nc.scalar.activation(z[:, :, :], z[:, :, :], ACT.Exp).then_inc(expd, 1)


class Turn:
    EVEN = P + 1
    ROOM = [(0, 7), (7, 13), (13, 19), (19, 25)]

    def __init__(self, nc, k, counts):
        self.nc, self.k, self.counts = nc, k, counts

    def room(self, st):
        self.ident = st.sb("ident", [P, P], BF16)
        self.p_t = [st.ps(f"p_t{n}", [128, 1024], BF16) for n in range(len(self.ROOM))]
        self.cst, self.turned, self.kept_a, self.kept_d = (st.sem(n) for n in ("cst", "turned", "kept_a", "kept_d"))

    def keep(self, copy, w, n, sem):
        a, b = self.ROOM[n]
        copy(self.counts[:, bass.ds(w, 1), a * P:b * P].rearrange("p o (n e) -> p (o n) e", e=P),
             self.p_t[n][0:P, 0:(b - a) * self.EVEN].rearrange("p (n e) -> p n e", e=self.EVEN)[:, :, 0:P]
             ).then_inc(sem, 1)

    def tensor_start(self, pe):
        pe.wait_ge(self.cst, 1)

    def tensor(self, pe, w, first):
        for n, (a, b) in enumerate(self.ROOM):
            if not first and n == 0:
                pe.wait_ge(self.kept_a, 2 * w)
                pe.wait_ge(self.kept_d, 2 * w)
            for c in range(a, b):
                ins = self.nc.tensor.transpose(self.p_t[n][0:P, (c - a) * self.EVEN:(c - a) * self.EVEN + P],
                                               self.counts[:, bass.ds(w, 1), c * P:(c + 1) * P]
                                               .rearrange("p o n -> p (o n)"), self.ident[:, :])
            ins.then_inc(self.turned, 1)

    def vector_start(self, dve):
        dve.tensor_copy(self.ident[:, :], self.k.ident[0:P, 0:P]).then_inc(self.cst, 1)

    def vector(self, dve, w):
        for n in (0, 2):
            dve.wait_ge(self.turned, w * 4 + n + 1)
            self.keep(dve.tensor_copy, w, n, self.kept_d)

    def scalar(self, act, w):
        for n in (1, 3):
            act.wait_ge(self.turned, w * 4 + n + 1)
            self.keep(self.nc.scalar.copy, w, n, self.kept_a)


def mark_window(nc, act, k, j, r, n, far, hot, apart, marked, summed=None):
    if summed is not None:
        act.wait_ge(summed, j - SLOTS + 1)
    if not isinstance(n, int) or n > 0:
        act.wait_ge(marked, n)
    for u in range(U):
        ins = nc.scalar.activation(far[:, u, :], k.lane[:, :], ACT.Abs, scale=-1.0,
                                   bias=k.dloc[:, bass.ds(j * U + u, 1)])
    ins.then_inc(apart, 1)
    act.wait_ge(apart, n + 1)
    nc.scalar.activation(hot[r][:, :, :], far[:, :, :], ACT.Relu, scale=-1.0, bias=k.ones[:, 0:1]).then_inc(marked, 1)


def stage_sum(nc, k, name, gx, weights, heads, acc, ours=(1,), beside=None):
    m = heads * K1
    with Stage(nc, name) as st:
        fx = [st.sb(f"fx{r}", [P, U * K1]) for r in range(SLOTS)]
        wt = [st.sb(f"wt{r}", [P, U * heads]) for r in range(SLOTS)]
        even = max(m, 64)
        msg = [st.sb(f"msg{r}", [P, U, even]) for r in range(SLOTS)]
        hot, far = [st.sb(f"hot{r}", [P, U, P]) for r in range(SLOTS)], st.sb("far", [P, U, P])
        p_s = [st.ps(f"p_s{r}", [128, 512]) for r in range(SLOTS)]
        got = [st.sem(f"got{r}") for r in range(SLOTS)]
        made, summed, added, apart, marked_a, marked_d = (
            st.sem(n) for n in ("made", "summed", "added", "apart", "marked_a", "marked_d"))
        if beside:
            beside.room(st)
        block = st.block()
        turns = W if beside else 0

        @block.sync
        def _(sp):
            def trip(i, first, extra=False):
                for r in range(SLOTS):
                    group = i * SLOTS + r
                    if extra:
                        group = sp.value_load(k.grow[0:1, bass.ds(group, 1)], min_val=0, max_val=G - 1)
                    if not first:
                        sp.wait_ge(made, i * SLOTS + r + 1 - SLOTS)
                    for dram, o, c in ((gx, fx, K1), (weights, wt, heads)):
                        sp.dma_start(o[r][:, :], edge_rows(dram, c)[bass.ds(group, 1)]
                                     .rearrange("o p c -> (o p) c")).then_inc(got[r], 16)

            trip(0, True)
            with sp.Fori(1, TRIPS_G) as i:
                trip(i, False)
            with sp.Fori(TRIPS_G, TRIPS) as i:
                trip(i, False, True)

        @block.scalar
        def _(act):
            def trip(i, first):
                for n, r in enumerate(ours):
                    mark_window(nc, act, k, i * SLOTS + r, r, i * len(ours) + n, far, hot, apart, marked_a,
                                None if first else summed)

            trip(0, True)
            if beside:
                with act.Fori(1, turns + 1) as i:
                    trip(i, False)
                    beside.scalar(act, i - 1)
            with act.Fori(turns + 1, TRIPS) as i:
                trip(i, False)

        @block.vector
        def _(dve):
            def message(i, r, first):
                dve.wait_ge(got[r], 32 * i + 32)
                if not first:
                    dve.wait_ge(summed, i * SLOTS + r + 1 - SLOTS)
                dve.tensor_tensor(msg[r][:, :, 0:m].rearrange("p u (h f) -> p u h f", f=K1),
                                  bcast(fx[r][:, :].rearrange("p (u f) -> p u f", f=K1), 2, heads),
                                  bcast(wt[r][:, :].rearrange("p (u h) -> p u h", h=heads), 3, K1),
                                  ALU.mult).then_inc(made, 1)
                if r not in ours:
                    dve.tensor_tensor(hot[r][:, :, :], bcast(k.lane[:, :], 1, U),
                                      bcast(k.dloc[:, bass.ds((i * SLOTS + r) * U, U)], 2, P), ALU.is_equal
                                      ).then_inc(marked_d, 1)

            def add(g, r):
                w = dve.value_load(k.wrow[0:1, bass.ds(g, 1)], min_val=0, max_val=W - 1)
                dve.wait_ge(summed, g + 1)
                a = acc[:, bass.ds(w, 1), :].rearrange("p o m -> p (o m)")
                dve.wait_ge(added, g + 1)
                dve.tensor_tensor(a, a, p_s[r][0:P, 0:m], ALU.add).then_inc(added, 1)

            if beside:
                beside.vector_start(dve)
            if even > m:
                for r in range(SLOTS):
                    dve.memset(msg[r][:, :, m:even], 0.0)
            dve.memset(acc[:, :, :], 0.0).then_inc(added, 1)
            message(0, 0, True)
            message(0, 1, True)
            message(0, 2, True)
            add(0, 0)
            def trip(i):
                for r in range(SLOTS):
                    message(i, r, False)
                    add(i * SLOTS + r - 2, (r - 2) % SLOTS)

            if beside:
                with dve.Fori(1, turns + 1) as i:
                    trip(i)
                    beside.vector(dve, i - 1)
            with dve.Fori(turns + 1, TRIPS) as i:
                trip(i)
            for g in (NG - 2, NG - 1):
                add(g, g % SLOTS)

        @block.tensor
        def _(pe):
            def trip(i, first):
                for r in range(SLOTS):
                    pe.wait_ge(made, i * SLOTS + r + 1)
                    if r in ours:
                        pe.wait_ge(marked_a, i * len(ours) + ours.index(r) + 1)
                    else:
                        theirs = [x for x in range(SLOTS) if x not in ours]
                        pe.wait_ge(marked_d, i * len(theirs) + theirs.index(r) + 1)
                    if not first:
                        pe.wait_ge(added, i * SLOTS + r + 2 - SLOTS)
                    for u in range(U):
                        ins = nc.tensor.matmul(p_s[r][0:P, 0:even], hot[r][:, u, :], msg[r][:, u, :],
                                               start=u == 0, stop=u == U - 1)
                    ins.then_inc(summed, 1)

            pe.wait_ge(added, 1)
            trip(0, True)
            if beside:
                beside.tensor_start(pe)
                beside.tensor(pe, 0, True)
                with pe.Fori(1, turns) as i:
                    trip(i, False)
                    beside.tensor(pe, i, False)
            with pe.Fori(max(turns, 1), TRIPS) as i:
                trip(i, False)


def stage_gat_max(nc, k, name, heads, amax, a_src, a_dst, tab, self_w):
    with Stage(nc, name) as st:
        z = st.sb("z", [P, W, heads])
        steps, ready, done = st.sem("steps"), st.sem("ready"), st.sem("done")
        block = st.block()

        @block.vector
        def _(dve):
            s = Steps(dve, steps)
            m = tab[:, :, heads:2 * heads]
            s.did(dve.tensor_copy(tab[:, :, 0:heads], a_dst))
            s.link(dve.tensor_tensor(m, amax[:, :, :], a_src, ALU.max))
            s.did(dve.tensor_tensor(z[:, :, :], a_src, a_dst, ALU.add))
            s.link(dve.tensor_tensor(m, m, a_dst, ALU.add))
            s.did(dve.scalar_tensor_tensor(z[:, :, :], z[:, :, :], 0.2, z[:, :, :], ALU.mult, ALU.max))
            s.link(dve.scalar_tensor_tensor(m, m, 0.2, m, ALU.mult, ALU.max))
            dve.tensor_tensor(z[:, :, :], z[:, :, :], m, ALU.subtract).then_inc(ready, 1)

        @block.scalar
        def _(act):
            act.wait_ge(ready, 1)
            nc.scalar.activation(self_w[:, :, :], z[:, :, :], ACT.Exp).then_inc(done, 1)
            act.wait_ge(done, 1)


def stage_gat_mean(nc, k, name, heads, acc, self_w, feats, out):
    with Stage(nc, name) as st:
        own = st.sb("own", [P, W, heads, D])
        den = st.sb("den", [P, W, heads])
        steps = st.sem("steps")
        block = st.block()

        @block.vector
        def _(dve):
            s = Steps(dve, steps)
            a = acc[:, :, :].rearrange("p w (h f) -> p w h f", f=K1)
            for h in range(heads):
                s.did(dve.tensor_tensor(own[:, :, h, :], feats, self_w[:, :, h:h + 1].broadcast_to([P, W, D]), ALU.mult))
            s.link(dve.tensor_tensor(den[:, :, :], a[:, :, :, D], self_w[:, :, :], ALU.add))
            s.link(dve.tensor_scalar(den[:, :, :], den[:, :, :], 1e-16, None, ALU.add))
            s.link(dve.reciprocal(den[:, :, :], den[:, :, :]))
            for h in range(heads):
                s.link(dve.tensor_tensor(own[:, :, h, :], own[:, :, h, :], a[:, :, h, 0:D], ALU.add))
                s.did(dve.tensor_tensor(out[:, :, h * D:(h + 1) * D], own[:, :, h, :],
                                        den[:, :, h:h + 1].broadcast_to([P, W, D]), ALU.mult))


def stage_norm(nc, k, name, y, scale=1.0, bias=None, twice=False, out=None):
    with Stage(nc, name) as st:
        sq = st.sb("sq", [P, W, D])
        mean, var = st.sb("mean", [P, W]), st.sb("var", [P, W])
        steps, ready, rooted, fin, wrote = (st.sem(n) for n in ("steps", "ready", "rooted", "fin", "wrote"))
        block = st.block()

        @block.vector
        def _(dve):
            s = Steps(dve, steps)
            if twice:
                s.link(dve.tensor_tensor(y, y, k.x[:, :, :], ALU.add))
            s.link(dve.scalar_tensor_tensor(k.x[:, :, :], y, scale, k.x[:, :, :], ALU.mult, ALU.add))
            if bias is not None:
                s.link(dve.tensor_tensor(k.x[:, :, :], k.x[:, :, :], bcast(bias, 1, W), ALU.add))
            s.link(dve.tensor_reduce(mean[:, :], k.x[:, :, :], AX, ALU.add))
            s.link(dve.tensor_scalar(mean[:, :], mean[:, :], 1.0 / D, None, ALU.mult))
            s.link(dve.tensor_tensor(k.x[:, :, :], k.x[:, :, :], bcast(mean[:, :], 2, D), ALU.subtract))
            s.link(dve.tensor_tensor(sq[:, :, :], k.x[:, :, :], k.x[:, :, :], ALU.mult))
            s.link(dve.tensor_reduce(var[:, :], sq[:, :, :], AX, ALU.add))
            dve.tensor_scalar(var[:, :], var[:, :], 1.0 / D, EPS_LN, ALU.mult, ALU.add).then_inc(ready, 1)
            dve.wait_ge(rooted, 1)
            s.link(dve.reciprocal(var[:, :], var[:, :]))
            dve.tensor_tensor(k.x[:, :, :], k.x[:, :, :], bcast(var[:, :], 2, D), ALU.mult).then_inc(fin, 1)

        @block.scalar
        def _(act):
            act.wait_ge(ready, 1)
            nc.scalar.activation(var[:, :], var[:, :], ACT.Sqrt).then_inc(rooted, 1)

        if out is not None:
            @block.sync
            def _(sp):
                sp.wait_ge(fin, 1)
                sp.dma_start(nodes_view(out), k.x[:, :, :]).then_inc(wrote, 16)
                sp.wait_ge(wrote, 16)


def stage_load(nc, k, x):
    with Stage(nc, "ld") as st:
        got = st.sem("got")
        block = st.block()

        @block.sync
        def _(sp):
            sp.dma_start(k.x[:, :, :], nodes_view(x)).then_inc(got, 16)
            sp.wait_ge(got, 16)


def gat(nc, k, t):
    with Stage(nc, "gat") as st:
        hid = st.sb("hid", [P, W, D + 2])
        b2 = st.sb("b2", [P, D])
        with Stage(nc, "gat1") as s1:
            k.mix1 = s1.sb("mix1", [128, 2, 128])
            k.w2, k.b1, k.b2 = s1.sb("w2", [128, 2, D + 2]), s1.sb("b1", [128, 2]), b2
            k.att1 = s1.sb("att1", [D, 1, 2 * H1])
            stage_gat_weights(nc, k, t)
            a1 = s1.sb("a1", [P, W, 2 * H1])
            stage_windows(nc, k, "wa", k.x, 1, D, k.att1, a1)
            stage_table(nc, k, "ta", k.table1, (k.x[:, :, :], None, a1[:, :, 0:H1]))
            stage_gather(nc, k, "ga", k.table1, k.gx, k.sc8, H1,
                         beside=Degrees(nc, k, t["src"], t["dst"], Attributes(k, t["edge_attr_4"], t["edge_attr_8"])))
            amax, tab, self_w = s1.sb("amax", [P, W, H1]), s1.sb("tab", [P, W, 2 * H1]), s1.sb("self_w", [P, W, H1])
            stage_segmax(nc, k, "sa", k.sc8, H1, k.scan8, amax)
            stage_gat_max(nc, k, "ma", H1, amax, a1[:, :, 0:H1], a1[:, :, H1:2 * H1], tab, self_w)
            stage_spread(nc, k, "ea", tab, k.node16, k.start16, scores=k.sc8, heads=H1, weights=k.wt8)
            acc, mean = s1.sb("acc", [P, W, H1 * K1]), s1.sb("mean", [P, W, H1 * D])
            stage_sum(nc, k, "ua", k.gx, k.wt8, H1, acc, ours=(0, 2))
            stage_gat_mean(nc, k, "na", H1, acc, self_w, k.x[:, :, :], mean)
            stage_windows(nc, k, "wb", mean, 2, 128, k.w2, hid, mid=k.mix1, bias=k.b1)
        with Stage(nc, "gat2") as s2:
            counts = s2.sb("counts", [P, W, N], BF16)
            stage_table(nc, k, "tb", k.table2, (hid[:, :, 0:D], None, hid[:, :, D:D + 1]))
            stage_gather(nc, k, "gb", k.table2, k.gx, k.sc1, H2, beside=Adjacency(nc, k, counts))
            with Stage(nc, "gat3") as s3:
                amax, tab, self_w = s3.sb("amax", [P, W, H2]), s3.sb("tab", [P, W, 2 * H2]), s3.sb("self_w", [P, W, H2])
                stage_segmax(nc, k, "sb", k.sc1, H2, k.scan1, amax)
                stage_gat_max(nc, k, "mb", H2, amax, hid[:, :, D:D + 1], hid[:, :, D + 1:D + 2], tab, self_w)
                stage_spread(nc, k, "eb", tab, k.node2, k.start2, scores=k.sc1, heads=H2, weights=k.wt1)
                acc, mean2 = s3.sb("acc", [P, W, H2 * K1]), s3.sb("mean2", [P, W, D])
                stage_sum(nc, k, "ub", k.gx, k.wt1, H2, acc,
                          beside=Turn(nc, k, counts))
                stage_gat_mean(nc, k, "nb", H2, acc, self_w, hid[:, :, 0:D], mean2)
                stage_norm(nc, k, "l0", mean2[:, :, :], bias=k.b2[:, :])
            appnp(nc, k, counts)


CHUNK = 4 * P
CHUNKS = -(-N // CHUNK)
RING = 3


class Adjacency:
    GROUPS = NG

    def __init__(self, nc, k, counts):
        self.nc, self.k, self.counts = nc, k, counts

    def room(self, st):
        self.column = st.sb("column", [P, N], mybir.dt.float16)
        self.hot_s = st.sb("hot_s", [P, RING, N], BF16)
        self.hot_d = st.sb("hot_d", [P, RING, P], BF16)
        self.ident, self.lane = st.sb("ident", [P, P], BF16), st.sb("lane", [P, P], BF16)
        self.p_c = [st.ps(f"p_c{c}", [128, 512]) for c in range(CHUNKS)]
        self.cst, self.hot, self.used, self.full, self.kept_a, self.kept_d, self.zeros = (
            st.sem(n) for n in ("cst", "hot", "used", "full", "kept_a", "kept_d", "zeros"))

    def bank(self, w, c):
        n = min(CHUNK, N - c * CHUNK)
        return (self.counts[:, bass.ds(w, 1), c * CHUNK:c * CHUNK + n].rearrange("p o n -> p (o n)"),
                self.p_c[c][0:P, 0:n])

    def sync(self, sp):
        pass

    def spans(self):
        return [(0, 1, None), (1, TRIPS_G, None)]

    def sync_end(self, sp):
        pass

    def gpsimd(self, pool):
        pool.iota(self.column[:, :], [[1, N]], base=-MIDDLE, channel_multiplier=0,
                  allow_small_or_imprecise_dtypes=True).then_inc(self.cst, 1)
        pool.memset(self.counts[:, W // 2:W, :], 0.0).then_inc(self.zeros, 1)

    def scalar(self, act, g):
        w = act.value_load(self.k.wrow[0:1, bass.ds(g, 1)], min_val=0, max_val=W - 1)
        for c in range(0, CHUNKS, 2):
            act.wait_ge(self.full, g * CHUNKS + c + 1)
            a, p = self.bank(w, c)
            self.nc.scalar.copy(a, p).then_inc(self.kept_a, 1)

    def vector(self, dve):
        k, hot_s, hot_d = self.k, self.hot_s, self.hot_d

        def one_hot(q, slot, first=False):
            if not first:
                dve.wait_ge(self.used, q - RING + 1)
            dve.tensor_scalar(hot_s[:, slot, :], self.column[:, :], k.srcf[:, bass.ds(q, 1)], None, ALU.is_equal)
            dve.tensor_scalar(hot_d[:, slot, :], self.lane[:, :], k.dloc[:, bass.ds(q, 1)], None,
                              ALU.is_equal).then_inc(self.hot, 1)

        def keep(g):
            w = dve.value_load(k.wrow[0:1, bass.ds(g, 1)], min_val=0, max_val=W - 1)
            for c in range(1, CHUNKS, 2):
                dve.wait_ge(self.full, g * CHUNKS + c + 1)
                a, p = self.bank(w, c)
                dve.tensor_copy(a, p).then_inc(self.kept_d, 1)

        def group(g, r, start):
            for q in range(2, U + 2):
                one_hot(g * U + q, (r * U + q) % RING, start and q < RING)
            keep(g)

        dve.tensor_copy(self.ident[:, :], k.ident[0:P, 0:P]).then_inc(self.cst, 1)
        dve.tensor_copy(self.lane[:, :], k.lane[:, :]).then_inc(self.cst, 1)
        dve.wait_ge(self.cst, 3)
        one_hot(0, 0, True)
        one_hot(1, 1, True)
        dve.memset(self.counts[:, 0:W // 2, :], 0.0).then_inc(self.zeros, 1)
        for r in range(SLOTS):
            group(r, r, r == 0)
        with dve.Fori(1, TRIPS) as i:
            for r in range(SLOTS):
                group(i * SLOTS + r, r, False)

    def tensor(self, pe):
        evens, odds = (CHUNKS + 1) // 2, CHUNKS // 2

        def group(g, r, first):
            w = pe.value_load(self.k.wrow[0:1, bass.ds(g, 1)], min_val=0, max_val=W - 1)
            for u in range(U):
                slot = (r * U + u) % RING
                pe.wait_ge(self.hot, g * U + u + 1)
                for c in range(CHUNKS):
                    n = min(CHUNK, N - c * CHUNK)
                    if u == 0 and not first:
                        if c % 2 == 0:
                            pe.wait_ge(self.kept_a, (g - 1) * evens + c // 2 + 1)
                        else:
                            pe.wait_ge(self.kept_d, (g - 1) * odds + c // 2 + 1)
                    ins = self.nc.tensor.matmul(self.p_c[c][0:P, 0:n], self.hot_d[:, slot, :],
                                                self.hot_s[:, slot, c * CHUNK:c * CHUNK + n], start=u == 0, stop=False)
                ins.then_inc(self.used, 1)
            for c in range(CHUNKS):
                a, p = self.bank(w, c)
                self.nc.tensor.matmul(p, self.ident[:, :], a, start=False, stop=True).then_inc(self.full, 1)

        pe.wait_ge(self.cst, 3)
        pe.wait_ge(self.zeros, 2)
        for r in range(SLOTS):
            group(r, r, r == 0)
        with pe.Fori(1, TRIPS) as i:
            for r in range(SLOTS):
                group(i * SLOTS + r, r, False)


def stage_appnp(nc, k, counts, out):
    WB = 5
    BANKS = W // WB
    with Stage(nc, "ap") as st:
        sn, dn = st.sb("sn", [P, W]), st.sb("dn", [P, W])
        x0 = st.sb("x0", [P, W, D])
        parts = st.sb("parts", [P, 2, W, 3, D], BF16)
        rest = st.sb("rest", [P, W, D])
        p_f = [st.ps(f"p_f{b}", [128, 512]) for b in range(BANKS)]
        steps, ready, rooted, split, summed, own = (
            st.sem(n) for n in ("steps", "ready", "rooted", "split", "summed", "own"))
        block = st.block()

        @block.scalar
        def _(act):
            act.wait_ge(ready, 2)
            nc.scalar.activation(sn[:, :], sn[:, :], ACT.Sqrt)
            nc.scalar.activation(dn[:, :], dn[:, :], ACT.Sqrt).then_inc(rooted, 1)

        @block.vector
        def _(dve):
            LINKS = 8

            def scale_and_split(at, w0, n, chain):
                f, rs = out[:, w0:w0 + n, :], rest[:, w0:w0 + n, :]
                hi, mid, lo = (parts[:, at, w0:w0 + n, j, :] for j in range(3))
                chain.link(dve.tensor_tensor(rs, f, bcast(sn[:, w0:w0 + n], 2, D), ALU.mult))
                chain.link(dve.tensor_copy(hi, rs))
                chain.link(dve.tensor_tensor(rs, rs, hi, ALU.subtract))
                chain.link(dve.tensor_copy(mid, rs))
                chain.link(dve.tensor_tensor(rs, rs, mid, ALU.subtract))
                dve.tensor_copy(lo, rs).then_inc(split, 1)

            dve.tensor_scalar(sn[:, :], k.outdeg[:, :], 1.0, None, ALU.max).then_inc(ready, 1)
            dve.tensor_scalar(dn[:, :], k.indeg[:, :], 1.0, None, ALU.max).then_inc(ready, 1)
            dve.wait_ge(rooted, 1)
            s = Steps(dve, steps)
            s.did(dve.reciprocal(sn[:, :], sn[:, :]))
            s.link(dve.reciprocal(dn[:, :], dn[:, :]))
            s.did(dve.tensor_scalar(dn[:, :], dn[:, :], 1.0 - ALPHA, None, ALU.mult))
            s.did(dve.tensor_scalar(x0[:, :, :], k.x[:, :, :], ALPHA, None, ALU.mult))
            s.link(dve.tensor_copy(out[:, :, :], k.x[:, :, :]))
            for b in range(BANKS):
                scale_and_split(0, b * WB, WB, s)
            with dve.Fori(0, STEPS_APPNP // 2) as i:
                for half in range(2):
                    for b in range(BANKS):
                        w0 = b * WB
                        step = (i * 2 + half) * BANKS + b
                        chain = Steps(dve, own, step * LINKS)
                        dve.wait_ge(summed, step + 1)
                        f = out[:, w0:w0 + WB, :]
                        chain.link(dve.tensor_reduce(
                            f, p_f[b][0:P, 0:WB * 3 * D].rearrange("p (w j f) -> p w f j", w=WB, j=3), AX, ALU.add))
                        chain.link(dve.tensor_tensor(f, f, bcast(dn[:, w0:w0 + WB], 2, D), ALU.mult))
                        chain.link(dve.tensor_tensor(f, f, x0[:, w0:w0 + WB, :], ALU.add))
                        scale_and_split(1 - half, w0, WB, chain)

        @block.tensor
        def _(pe):
            def bank(i, half, b):
                for w in range(b * WB, (b + 1) * WB):
                    for c in range(W):
                        at = (w - b * WB) * 3 * D
                        ins = nc.tensor.matmul(p_f[b][0:P, at:at + 3 * D], counts[:, w, c * P:(c + 1) * P],
                                               parts[:, half, c, :, :].rearrange("p j f -> p (j f)"),
                                               start=c == 0, stop=c == W - 1)
                ins.then_inc(summed, 1)

            with pe.Fori(0, STEPS_APPNP // 2) as i:
                for half in range(2):
                    pe.wait_ge(split, (i * 2 + half) * BANKS + BANKS)
                    for b in range(BANKS):
                        bank(i, half, b)


def appnp(nc, k, counts):
    with Stage(nc, "pp") as st:
        f = st.sb("f", [P, W, D])
        stage_appnp(nc, k, counts, f)
        stage_norm(nc, k, "l1", f[:, :, :])


def stage_attention_weights(nc, k, t, keys, values):
    with Stage(nc, "aw") as st:
        raw = st.sb("raw", [D, 3, HQ, D])
        turned = st.sb("turned", [D, 3, HQ * D])
        wout = st.sb("wout", [D, D])
        p_t, p_k, p_v = (st.ps(n, [128, 512]) for n in ("p_t", "p_k", "p_v"))
        got, flipped, copied, done = (st.sem(n) for n in ("got", "flipped", "copied", "done"))
        block = st.block()

        @block.sync
        def _(sp):
            for n, a in enumerate(("L2_gnn_Wq", "L2_gnn_Wk", "L2_gnn_Wv")):
                sp.dma_start(raw[:, n, :, :], t[a].rearrange("h f o -> f h o")).then_inc(got, 16)
            sp.dma_start(wout[:, :], t["L2_gnn_Wout"]).then_inc(got, 16)

        @block.tensor
        def _(pe):
            pe.wait_ge(got, 64)
            for n in range(3):
                for h in range(HQ):
                    at = (n * HQ + h) * D
                    ins = nc.tensor.transpose(p_t[0:D, at:at + D], raw[:, n, h, :], k.ident[0:D, 0:D])
            ins.then_inc(flipped, 1)
            pe.wait_ge(copied, 1)
            for h in range(HQ):
                ins = nc.tensor.matmul(p_k[0:D, h * D:(h + 1) * D], turned[:, 1, h * D:(h + 1) * D],
                                       turned[:, 0, h * D:(h + 1) * D], start=True, stop=True)
            ins.then_inc(flipped, 1)
            nc.tensor.matmul(p_v[0:HQ * D, 0:D], turned[:, 2, :], wout[:, :], start=True, stop=True).then_inc(flipped, 1)

        @block.vector
        def _(dve):
            dve.wait_ge(flipped, 1)
            dve.tensor_copy(turned[:, :, :], p_t[0:D, 0:3 * HQ * D].rearrange("p (n c) -> p n c", n=3)).then_inc(copied, 1)
            dve.wait_ge(flipped, 3)
            dve.tensor_scalar(keys[:, 0, :], p_k[0:D, 0:HQ * D], float(D) ** -0.5, None, ALU.mult)
            dve.tensor_scalar(values[:, 0, :], p_v[0:HQ * D, 0:D], 1.0 / HQ, None, ALU.mult).then_inc(done, 1)


def stage_divide(nc, k, acc, mean):
    with Stage(nc, "dv") as st:
        den, none = st.sb("den", [P, W, HQ]), st.sb("none", [P, W, HQ])
        steps = st.sem("steps")
        block = st.block()

        @block.vector
        def _(dve):
            s = Steps(dve, steps)
            a = acc[:, :, :].rearrange("p w (h f) -> p w h f", f=K1)
            s.link(dve.tensor_scalar(none[:, :, :], a[:, :, :, D], 0.0, None, ALU.is_le))
            s.link(dve.tensor_tensor(den[:, :, :], a[:, :, :, D], none[:, :, :], ALU.add))
            s.link(dve.reciprocal(den[:, :, :], den[:, :, :]))
            for h in range(HQ):
                s.did(dve.tensor_tensor(mean[:, :, h * D:(h + 1) * D], a[:, :, h, 0:D],
                                        den[:, :, h:h + 1].broadcast_to([P, W, D]), ALU.mult))


def attention(nc, k, t):
    with Stage(nc, "at") as st:
        keys, values = st.sb("keys", [D, 1, HQ * D]), st.sb("values", [HQ * D, 1, D])
        stage_attention_weights(nc, k, t, keys, values)
        with Stage(nc, "at1") as s1:
            y = s1.sb("y", [P, W, HQ * D])
            stage_windows(nc, k, "wk", k.x, 1, D, keys, y)
            stage_table(nc, k, "tk", k.table4, (k.x[:, :, :], None, y[:, :, :]))
        stage_spread(nc, k, "xd", k.x, k.node32, k.start32, xdst=k.xdst)
        stage_gather(nc, k, "gk", k.table4, k.gx, k.sc4, HQ, products=True)
        amax = st.sb("amax", [P, W, HQ])
        stage_segmax(nc, k, "sk", k.sc4, HQ, k.scan4, amax)
        stage_spread(nc, k, "ek", amax, k.node4, k.start4, scores=k.sc4, heads=HQ, weights=k.wt4)
        acc, mean, y = st.sb("acc", [P, W, HQ * K1]), st.sb("mean", [P, W, HQ * D]), st.sb("y", [P, W, D])
        stage_sum(nc, k, "uk", k.gx, k.wt4, HQ, acc)
        stage_divide(nc, k, acc, mean)
        stage_windows(nc, k, "wv", mean, 1, HQ * D, values, y)
        stage_norm(nc, k, "l2", y[:, :, :], twice=True)


def stage_conv_weights(nc, k, t, fc1, fc2):
    with Stage(nc, "cw") as st:
        raw, rest = st.sb("raw", [BASIS, HID]), st.sb("rest", [BASIS, HID])
        parts = st.sb("parts", [BASIS, 3, HID], BF16)
        got, z, steps, made, placed = (st.sem(n) for n in ("got", "z", "steps", "made", "placed"))
        block = st.block()

        @block.gpsimd
        def _(pool):
            pool.memset(fc1[:, :, :, :], 0.0).then_inc(z, 1)

        @block.sync
        def _(sp):
            sp.dma_start(raw[:, :], t["L3_gnn_fc_w1"]).then_inc(got, 16)
            sp.dma_start(fc2[:, :, :], t["L3_gnn_fc_w2"].rearrange("(c h) n -> h c n", c=2)).then_inc(got, 16)
            sp.wait_ge(z, 1)
            sp.wait_ge(made, 1)
            for u in range(2):
                for j, part in enumerate(PARTS_FC):
                    at = u * ROWS + j * BASIS
                    sp.dma_start(fc1[at:at + BASIS, u, :, :], parts[:, part, :].rearrange("b (c h) -> b c h", c=2)
                                 ).then_inc(placed, 16)
            sp.wait_ge(placed, 16 * 12)

        @block.vector
        def _(dve):
            s = Steps(dve, steps)
            dve.wait_ge(got, 32)
            s.did(dve.tensor_scalar(fc2[:, :, :], fc2[:, :, :], float(np.sqrt(2.0)) * float(HID) ** -0.5, None, ALU.mult))
            s.link(dve.tensor_scalar(raw[:, :], raw[:, :], float(BASIS) ** -0.5, None, ALU.mult))
            split(s.link, dve, raw[:, :], rest[:, :], [parts[:, j, :] for j in range(3)])
            dve.memset(rest[:, :], 0.0).then_inc(made, 1)


def stage_conv(nc, k, fc1, fc2, acc):
    PAIR = [(0, 2), (2, 4), (4, 5)]
    BANKS_H = [(0, 4), (4, 8), (8, 10)]
    KF = 3 * MUL
    EVEN = P + 1
    HEAD, TAIL = 4, 3
    with Stage(nc, "cv") as st:
        idx = [st.sb(f"idx{r}", [P, U], I32) for r in range(SLOTS)]
        row = [st.sb(f"row{r}", [P, U * D]) for r in range(SLOTS)]
        vecs = [st.sb(f"vecs{r}", [P, U * 8]) for r in range(SLOTS)]
        scal = [st.sb(f"scal{r}", [P, U * ROWS], BF16) for r in range(SLOTS)]
        scal_t = [st.sb(f"scal_t{r}", [2 * ROWS, 3, EVEN], BF16) for r in range(SLOTS)]
        ident = st.sb("ident", [P, P], BF16)
        hid = [st.sb(f"hid{r}", [128, 2 * U, P]) for r in range(SLOTS)]
        dot = [st.sb(f"dot{r}", [P, U, MUL, 3]) for r in range(SLOTS)]
        fac = [st.sb(f"fac{r}", [P, U, KF]) for r in range(SLOTS)]
        vec = [st.sb(f"vec{r}", [P, U, 3, MUL]) for r in range(SLOTS)]
        prod = st.sb("prod", [P, U, MUL, 2 * KF])
        red = st.sb("red", [P, U, MUL, 4])
        outer = st.sb("outer", [P, U, MUL, 3])
        msg = st.sb("msg", [P, G * U, D])
        hot, far = [st.sb(f"hot{r}", [P, U, P]) for r in range(SLOTS)], st.sb("far", [P, U, P])
        p_t, p_s = st.ps("p_t", [128, 1024], BF16), st.ps("p_s", [128, 512])
        p_h = [st.ps(f"p_h{n}", [128, 512]) for n in range(3)]
        p_w = [st.ps(f"p_w{n}", [128, 512]) for n in range(3)]
        (named, turned, flat, hidden, bent, weighed, read, made, summed, added, own, cst, copied, apart,
         marked, gt) = (st.sem(n) for n in ("named", "turned", "flat", "hidden", "bent", "weighed", "read", "made",
                                    "summed", "added", "own", "cst", "copied", "apart", "marked",
                                    "gt"))
        fetched = [st.sem(f"fetched{r}") for r in range(SLOTS)]
        got, got_s = ([st.sem(f"{n}{r}") for r in range(SLOTS)] for n in ("got", "got_s"))
        block = st.block()

        @block.sync
        def _(sp):
            def fetch(dram, o, r, g, sem):
                sp.dma_start(o[r][:, :], dram[bass.ds(g, 1)].rearrange("o p c -> (o p) c")).then_inc(sem[r], 16)

            def trip(i, first, last=False):
                for r in range(SLOTS):
                    g = i * SLOTS + r
                    if not first:
                        sp.wait_ge(made, g + 1 - SLOTS)
                    fetch(k.eav, vecs, r, g, got)
                    if not last:
                        sp.wait_ge(turned, g + 1)
                        fetch(k.eas, scal, r, g + SLOTS, got_s)

            for r in range(SLOTS):
                fetch(k.eas, scal, r, r, got_s)
            trip(0, True)
            with sp.Fori(1, TRIPS_G - 1) as i:
                trip(i, False)
            trip(TRIPS_G - 1, False, True)

        @block.gpsimd
        def _(pool):
            with pool.Fori(0, TRIPS_G) as i:
                for r in range(SLOTS):
                    pool.wait_ge(named, i * SLOTS + r + 1)
                    gate(pool, gt)
                    for u in range(U):
                        pool.indirect_dma_start(
                            out=row[r][:, u * D:(u + 1) * D], out_offset=None, in_=k.table3,
                            in_offset=bass.IndirectOffsetOnAxis(ap=idx[r][:, u:u + 1], axis=0)).then_inc(fetched[r], 16)

        @block.scalar
        def _(act):
            def name_edges(g, r):
                nc.scalar.activation(idx[r][:, :], k.srcf[:, bass.ds(g * U, U)], ACT.Copy,
                                     bias=float(MIDDLE)).then_inc(named, 1)

            def mark(j, r, first=False):
                mark_window(nc, act, k, j, r, j, far, hot, apart, marked, None if first else summed)

            def units(i, r, first):
                g = i * SLOTS + r
                act.wait_ge(turned, g + 1)
                nc.scalar.copy(scal_t[r][:, 0:2, 0:P], p_t[0:2 * ROWS, 0:2 * EVEN]
                               .rearrange("k (n e) -> k n e", e=EVEN)[:, :, 0:P])
                nc.scalar.copy(scal_t[r][0:ROWS, 2, 0:P], p_t[0:ROWS, 2 * EVEN:2 * EVEN + P]).then_inc(flat, 1)
                if not first:
                    act.wait_ge(weighed, (g - SLOTS) * 3 + 3)
                for n, (a, b) in enumerate(BANKS_H):
                    act.wait_ge(hidden, g * 3 + n + 1)
                    nc.scalar.activation(hid[r][:, a:b, :], p_h[n][:, 0:(b - a) * P]
                                         .rearrange("p (n e) -> p n e", e=P), ACT.Relu).then_inc(bent, 1)
                act.wait_ge(fetched[r], 16 * U * i + 16 * U)
                if not first:
                    act.wait_ge(read, (g - SLOTS) * 3 + 3)
                nc.scalar.copy(fac[r][:, :, 2 * MUL:KF], row[r][:, :].rearrange("p (u c) -> p u c", c=D)[:, :, 0:MUL]
                               ).then_inc(copied, 1)

            def trip(i, first, last=False):
                for r in range(SLOTS):
                    g = i * SLOTS + r
                    if r < SLOTS - 1:
                        units(i, r + 1, first)
                    elif not last:
                        units(i + 1, 0, False)
                    mark(g, r, first)
                    act.wait_ge(own, g * (HEAD + TAIL) + HEAD - 1)
                    act.wait_ge(copied, g + 1)
                    name_edges(g + SLOTS, r)

            for r in range(SLOTS):
                name_edges(r, r)
            units(0, 0, True)
            trip(0, True)
            with act.Fori(1, TRIPS_G - 1) as i:
                trip(i, False)
            trip(TRIPS_G - 1, False, True)
            with act.Fori(TRIPS_G, TRIPS) as i:
                for r in range(SLOTS):
                    mark(i * SLOTS + r, r)

        @block.tensor
        def _(pe):
            pe.wait_ge(cst, 1)
            gate(pe, gt)

            def hide(i, r, g, first):
                pe.wait_ge(got_s[r], 16 * i + 16)
                gate(pe, gt)
                if not first:
                    pe.wait_ge(flat, g)
                    gate(pe, gt)
                for n in range(3):
                    rows = 2 * ROWS if n < 2 else ROWS
                    ins = nc.tensor.transpose(p_t[0:rows, n * EVEN:n * EVEN + P],
                                              scal[r][:, n * 2 * ROWS:n * 2 * ROWS + rows], ident[:, :])
                ins.then_inc(turned, 1)

            def hide2(g, r, first):
                pe.wait_ge(flat, g + 1)
                for n, (a, b) in enumerate(BANKS_H):
                    rows = 2 * ROWS if n < 2 else ROWS
                    if not first:
                        pe.wait_ge(bent, (g - 1) * 3 + n + 1)
                    for m in range(a, b):
                        ins = nc.tensor.matmul(p_h[n][:, (m - a) * P:(m - a + 1) * P],
                                               fc1[0:rows, (m // 2) % 2, m % 2, :], scal_t[r][0:rows, n, 0:P],
                                               start=True, stop=True)
                    ins.then_inc(hidden, 1)

            def look(j):
                return pe.value_load(k.grow[0:1, bass.ds(j, 1)], min_val=0, max_val=G - 1)

            def weigh(g, r, first):
                for n, (a, b) in enumerate(PAIR):
                    if not first:
                        pe.wait_ge(read, (g - 1) * 3 + n + 1)
                    pe.wait_ge(bent, g * 3 + n + 1)
                    for u in range(a, b):
                        for c in range(2):
                            ins = nc.tensor.matmul(p_w[n][0:P, (u - a) * HID:(u - a + 1) * HID],
                                                   hid[r][:, 2 * u + c, :], fc2[:, c, :], start=c == 0, stop=c == 1)
                    ins.then_inc(weighed, 1)

            def gather_up(j, r, first, group):
                pe.wait_ge(marked, j + 1)
                if not first:
                    pe.wait_ge(added, j + 1)
                for u in range(U):
                    ins = nc.tensor.matmul(p_s[0:P, 0:D], hot[r][:, u, :],
                                           msg[:, bass.ds(group * U + u, 1), :].rearrange("p o d -> p (o d)"),
                                           start=u == 0, stop=u == U - 1)
                ins.then_inc(summed, 1)

            def trip(i, first, last=False):
                for r in range(SLOTS):
                    g = i * SLOTS + r
                    more, most = divmod(r + 1, SLOTS), divmod(r + 2, SLOTS)
                    if not last or more[0] == 0:
                        hide2(g + 1, more[1], False)
                    if not last or most[0] == 0:
                        hide(i + most[0], most[1], g + 2, False)
                    if first and r == 0:
                        weigh(g, r, True)
                        continue
                    weigh(g, r, False)
                    pe.wait_ge(made, g)
                    gather_up(g - 1, (r - 1) % SLOTS, first and r == 1, g - 1)

            hide(0, 0, 0, True)
            hide2(0, 0, True)
            hide(0, 1, 1, False)
            trip(0, True)
            with pe.Fori(1, TRIPS_G - 1) as i:
                trip(i, False)
            trip(TRIPS_G - 1, False, True)
            pe.wait_ge(made, G)
            gather_up(G - 1, SLOTS - 1, False, G - 1)
            with pe.Fori(TRIPS_G, TRIPS) as i:
                for r in range(SLOTS):
                    gather_up(i * SLOTS + r, r, False, look(i * SLOTS + r))

        @block.vector
        def _(dve):
            def window(j):
                return dve.value_load(k.wrow[0:1, bass.ds(j, 1)], min_val=0, max_val=W - 1)

            def parts(r):
                return vecs[r][:, :].rearrange("p (u c) -> p u c", c=8)

            def factors(s, i, r):
                rw, e = row[r][:, :].rearrange("p (u c) -> p u c", c=D), parts(r)
                scalars, vectors = rw[:, :, 0:MUL], rw[:, :, MUL:D].rearrange("p u (m i) -> p u m i", i=3)
                dve.wait_ge(fetched[r], 16 * U * i + 16 * U)
                dve.wait_ge(got[r], 16 * i + 16)
                s.did(dve.tensor_tensor(dot[r][:, :, :, :], vectors, bcast(e[:, :, 2:5], 2, MUL), ALU.mult))
                s.did(dve.tensor_tensor(fac[r][:, :, 0:MUL], scalars, e[:, :, 0:1].broadcast_to([P, U, MUL]), ALU.mult))
                s.did(dve.tensor_tensor(vec[r][:, :, :, :], vectors.rearrange("p u m i -> p u i m"),
                                        bcast(e[:, :, 1:2].broadcast_to([P, U, 3]), 3, MUL), ALU.mult))

            def dots(s, r):
                s.did(dve.tensor_reduce(fac[r][:, :, MUL:2 * MUL], dot[r][:, :, :, :], AX, ALU.add))

            def messages(i, r, g, more=True, j=None):
                s = Steps(dve, own, g * (HEAD + TAIL) + HEAD)
                dve.wait_ge(own, s.base)
                dve.wait_ge(copied, g + 1)
                m, e = msg[:, bass.ds(g * U, U), :], parts(r)
                for n, (a, b) in enumerate(PAIR):
                    dve.wait_ge(weighed, g * 3 + n + 1)
                    wv = p_w[n][0:P, 0:(b - a) * HID].rearrange("p (u k w) -> p u w k", k=4 * MUL, w=MUL)
                    dve.tensor_tensor(prod[:, a:b, :, 0:KF], wv[:, :, :, 0:KF], bcast(fac[r][:, a:b, :], 2, MUL), ALU.mult)
                    for u in range(a, b):
                        ins = dve.tensor_tensor(prod[:, u, :, KF:].rearrange("p w (x k) -> p w x k", k=MUL),
                                                bcast(wv[:, u - a, :, KF:4 * MUL], 2, 3),
                                                bcast(vec[r][:, u, :, :], 1, MUL), ALU.mult)
                    ins.then_inc(read, 1)
                dve.wait_ge(read, g * 3 + 3)
                s.did(dve.tensor_reduce(red[:, :, :, :], prod[:, :, :, 2 * MUL:2 * KF]
                                        .rearrange("p u w (x k) -> p u w x k", k=MUL), AX, ALU.add))
                s.did(dve.tensor_reduce(m[:, :, 0:MUL], prod[:, :, :, 0:2 * MUL], AX, ALU.add))
                w = window(j) if j is not None else None
                if more:
                    factors(s, i + (r + 1) // SLOTS, (r + 1) % SLOTS)
                dve.wait_ge(own, s.base + s.n)
                s.did(dve.tensor_tensor(outer[:, :, :, :], red[:, :, :, 0:1].broadcast_to([P, U, MUL, 3]),
                                        bcast(e[:, :, 5:8], 2, MUL), ALU.mult))
                if more:
                    dots(s, (r + 1) % SLOTS)
                    assert s.n == HEAD + TAIL
                dve.wait_ge(own, s.base + s.n)
                dve.tensor_tensor(m[:, :, MUL:D].rearrange("p u (w x) -> p u w x", x=3), outer[:, :, :, :],
                                  red[:, :, :, 1:4], ALU.add).then_inc(made, 1)
                return w

            def add(g, w):
                dve.wait_ge(summed, g + 1)
                dve.wait_ge(added, g + 1)
                a = acc[:, bass.ds(w, 1), :].rearrange("p o m -> p (o m)")
                dve.tensor_tensor(a, a, p_s[0:P, 0:D], ALU.add).then_inc(added, 1)

            dve.tensor_copy(ident[:, :], k.ident[0:P, 0:P]).then_inc(cst, 1)
            dve.memset(acc[:, :, :], 0.0).then_inc(added, 1)
            s = Steps(dve, own)
            factors(s, 0, 0)
            dve.wait_ge(own, s.n)
            dots(s, 0)
            messages(0, 0, 0)
            for r in range(1, SLOTS):
                add(r - 1, messages(0, r, r, j=r - 1))
            with dve.Fori(1, TRIPS_G - 1) as i:
                for r in range(SLOTS):
                    g = i * SLOTS + r
                    add(g - 1, messages(i, r, g, j=g - 1))
            for r in range(SLOTS):
                g = (TRIPS_G - 1) * SLOTS + r
                add(g - 1, messages(TRIPS_G - 1, r, g, more=r < SLOTS - 1, j=g - 1))
            with dve.Fori(G - 1, NG) as j:
                add(j, window(j))


def conv(nc, k, t):
    with Stage(nc, "cn") as st:
        acc = st.sb("acc", [P, W, D])
        fc1 = st.sb("fc1", [2 * ROWS, 2, 2, 128], BF16)
        fc2 = st.sb("fc2", [128, 2, HID])
        stage_conv_weights(nc, k, t, fc1, fc2)
        stage_table(nc, k, "tc", k.table3, (k.x[:, :, :],))
        stage_conv(nc, k, fc1, fc2, acc)
        stage_norm(nc, k, "l3", acc[:, :, :], scale=float(1.0 / np.sqrt(E / N)), out=k.out)


def build(nc, t, out):
    k = Kept()
    with ExitStack() as ctx:
        def sb(name, shape, dt=F32):
            return ctx.enter_context(nc.sbuf_tensor(name, shape, dt))

        def dram(name, shape, dt=F32):
            return nc.dram_tensor(name, shape, dt, kind="Internal").ap()

        k.ident = sb("ident", [128, 128])
        k.ones = sb("ones", [P, P])
        k.lane = sb("lane", [P, P])
        k.earlier = sb("earlier", [P, P])
        k.negs = sb("negs", [1, 8])
        k.srcf = sb("srcf", [P, NGP * U])
        k.dloc = sb("dloc", [P, NGP * U])
        k.wrow, k.grow = sb("wrow", [1, NG], I32), sb("grow", [1, NG], I32)
        k.first_i = sb("first_i", [P, 1], I32)
        k.nstart, k.infirst = sb("nstart", [P, J], BF16), sb("infirst", [P, J], BF16)
        k.indeg, k.outdeg = sb("indeg", [P, W]), sb("outdeg", [P, W])
        k.end, k.start = sb("end", [P, W], I32), sb("start", [P, W], I32)
        k.x = sb("x", [P, W, D])
        k.start16, k.start2, k.start32, k.start4 = (dram(f"start{c}", (E, c)) for c in (16, 2, 32, 4))
        k.xdst = dram("xdst", (E, D))
        k.wind, k.kxd = dram("wind", (NG, 1), I32), dram("kxd", (X, 1), I32)
        stage_index(nc, k, t["src"], t["dst"])
        k.out = out
        k.table1, k.table2 = dram("table1", (N, K1 + H1)), dram("table2", (N, K1 + H2))
        k.eas, k.eav = dram("eas", (G, P, U * ROWS), BF16), dram("eav", (G, P, U * 8))
        k.table3, k.table4 = dram("table3", (N, D)), dram("table4", (N, K1 + HQ * D))
        k.gx = dram("gx", (E, K1))
        k.sc8, k.sc1, k.sc4 = (dram(f"sc{c}", (E, c)) for c in (8, 1, 4))
        k.wt8, k.wt1, k.wt4 = (dram(f"wt{c}", (E, c)) for c in (8, 1, 4))
        k.scan8, k.scan1, k.scan4 = (dram(f"scan{c}", (E + 1, c)) for c in (8, 1, 4))
        k.node16, k.node2, k.node32, k.node4 = (dram(f"node{c}", (N, c)) for c in (16, 2, 32, 4))
        stage_load(nc, k, t["x"])
        gat(nc, k, t)
        attention(nc, k, t)
        conv(nc, k, t)


_INS = ["x", "src", "dst", "edge_attr_4", "edge_attr_8", "L0_gnn_W1", "L0_gnn_att_src1", "L0_gnn_att_dst1",
        "L0_gnn_b1", "L0_gnn_W2", "L0_gnn_att_src2", "L0_gnn_att_dst2", "L0_gnn_b2", "L2_gnn_Wq", "L2_gnn_Wk",
        "L2_gnn_Wv", "L2_gnn_Wout", "L3_gnn_fc_w1", "L3_gnn_fc_w2"]


def kernel(**inputs):
    import concourse.bacc as bacc
    from concourse.bass_utils import run_bass_kernel_spmd

    nc = bacc.Bacc("TRN2", target_bir_lowering=False, num_devices=1)
    arrays, t = {}, {}
    for name in _INS:
        a = np.ascontiguousarray(inputs[name])
        arrays[f"in_{name}"] = a
        t[name] = nc.dram_tensor(f"in_{name}", a.shape, mybir.dt.from_np(a.dtype), kind="ExternalInput").ap()
    out = nc.dram_tensor("out_nodes", (N, D), F32, kind="ExternalOutput").ap()
    build(nc, t, out)
    r = run_bass_kernel_spmd(nc, [arrays], core_ids=[0])
    return r.results[0]["out_nodes"]
```
